# Optimizing a Trainium2 kernel written in Bass

```python
import numpy as np
import jax
import jax.numpy as jnp

def _softmax(x, axis=-1):
    return jax.nn.softmax(x, axis=axis)

def _gelu(x):
    return jax.nn.gelu(x, approximate=True)

def _silu(x):
    return jax.nn.silu(x)

def _sigmoid(x):
    return jax.nn.sigmoid(x)

def _layernorm(x, axis=-1, eps=1e-05):
    m = jnp.mean(x, axis=axis, keepdims=True)
    v = jnp.var(x, axis=axis, keepdims=True)
    return (x - m) / jnp.sqrt(v + eps)

def _scatter_add(tgt, idx, src, axis=0):
    return tgt.at[idx].add(src)

def _segment_sum(src, seg, n):
    return jax.ops.segment_sum(src, seg, n)
kernel_name = 'mk_decoder_preln_d2_seqx_r4_b738e9'

def setup_inputs(seed: int=0):
    np.random.seed(seed)
    _w = jnp.asarray

    def _rec_inputs():
        import jax
        import jax.numpy as jnp
        _rk = jax.random.key(seed)
        x = 0.0003765 + 1 * jax.random.normal(jax.random.fold_in(_rk, 1), (8, 256, 512), jnp.float32)
        _lenS = 256 - jax.random.randint(jax.random.fold_in(_rk, 7), (8,), 0, max(1, 256 // 4) + 1, jnp.int32)
        _lenS2 = 256 - jax.random.randint(jax.random.fold_in(_rk, 8), (8,), 0, max(1, 256 // 4) + 1, jnp.int32)
        _ctx_2048P = jax.random.normal(jax.random.fold_in(_rk, 11), (8, 16, 512), jnp.float32)
        _ctx_2048c = jax.random.dirichlet(jax.random.fold_in(_rk, 511), 0.3 * jnp.ones((16,), jnp.float32), (8, 256))
        _ctx_2048t = jnp.einsum('bsk,bkd->bsd', _ctx_2048c, _ctx_2048P)
        _ctx_2048t = _ctx_2048t * jax.lax.rsqrt(jnp.mean(jnp.square(_ctx_2048t)) + 1e-12) * 0.953939
        ctx_2048 = -0.000292821 + 1.00034 * (_ctx_2048t + 0.3 * jax.random.normal(jax.random.fold_in(_rk, 611), (8, 256, 512), jnp.float32))
        return (x, ctx_2048)
    x, ctx_2048 = _rec_inputs()

    def _L0_attn_setup():
        import jax, jax.numpy as jnp
        import numpy as np
        import math
        HID = 512
        HEADS = 16
        HEAD_DIM = HID // HEADS
        SEQ = 1024
        BATCH = 1
        ROPE_THETA = 10000.0
        START_RATIO = 0.1
        RECENT_RATIO = 0.25

        def _rope_sin_cos(seq_len, dtype):
            theta = 1.0 / ROPE_THETA ** (jnp.arange(0, HEAD_DIM, 2, dtype=jnp.float32) / HEAD_DIM)
            sinusoid = jnp.arange(seq_len, dtype=jnp.float32)[:, None] * theta[None, :]
            return (jnp.sin(sinusoid).astype(dtype), jnp.cos(sinusoid).astype(dtype))

        def _apply_rope(x, sin, cos):
            x1, x2 = (x[..., 0::2], x[..., 1::2])
            return jnp.concatenate([x1 * cos - x2 * sin, x1 * sin + x2 * cos], axis=-1)
        key = jax.random.key(seed)
        ks = jax.random.split(key, 9)
        s = 0.02
        return {'hidden_states': jax.random.normal(ks[0], (BATCH, SEQ, HID), jnp.float32), 'Wq': jax.random.normal(ks[1], (HID, HID), jnp.float32) * s, 'bq': jnp.zeros((HID,), jnp.float32), 'Wk': jax.random.normal(ks[2], (HID, HID), jnp.float32) * s, 'bk': jnp.zeros((HID,), jnp.float32), 'Wv': jax.random.normal(ks[3], (HID, HID), jnp.float32) * s, 'bv': jnp.zeros((HID,), jnp.float32), 'Wo': jax.random.normal(ks[4], (HID, HID), jnp.float32) * s, 'bo': jnp.zeros((HID,), jnp.float32)}
    _L0_attn_all = _L0_attn_setup()
    _L0_attn_in = {k: v for k, v in _L0_attn_all.items() if k in ('Wq', 'bq', 'Wk', 'bk', 'Wv', 'bv', 'Wo', 'bo')}
    del _L0_attn_all

    def _L0_xattn_setup():
        import jax, jax.numpy as jnp
        import numpy as np
        key = jax.random.key(seed)
        k1, k2, k3, k4, k5 = jax.random.split(key, 5)
        B, D_MODEL, L = (2, 256, 512)
        HEAD_DIM = 8
        H = D_MODEL // HEAD_DIM
        return {'k': jax.random.normal(k1, (B, D_MODEL, L), dtype=jnp.float32), 'v': jax.random.normal(k2, (B, D_MODEL, L), dtype=jnp.float32), 'q': jax.random.normal(k3, (B, D_MODEL, L), dtype=jnp.float32), 'ssm_kernel': jax.random.normal(k4, (H, L), dtype=jnp.float32), 'D': jax.random.normal(k5, (H,), dtype=jnp.float32), 'head_dim': HEAD_DIM}
    _L0_xattn_all = _L0_xattn_setup()
    _L0_xattn_in = {k: v for k, v in _L0_xattn_all.items() if k in ('ssm_kernel', 'D')}
    del _L0_xattn_all

    def _L0_ffn_setup():
        import jax, jax.numpy as jnp
        import numpy as np
        LAYER_IDX = 16
        key = jax.random.key(seed)
        k0, k1, k2 = jax.random.split(key, 3)
        B, S, H = (4, 1024, 512)
        NV, L = (1250, 33)
        x = jax.random.normal(k0, (B, S, H), dtype=jnp.float32)
        gate_w = jax.random.normal(k1, (NV + 1, H), dtype=jnp.float32) * 0.02
        gate_b = jnp.zeros((NV + 1,), dtype=jnp.float32)
        vector_pool = jax.random.normal(k2, (NV, L, H), dtype=jnp.float32)
        return {'x': x, 'gate_w': gate_w, 'gate_b': gate_b, 'vector_pool': vector_pool}
    _L0_ffn_all = _L0_ffn_setup()
    _L0_ffn_in = {k: v for k, v in _L0_ffn_all.items() if k in ('gate_w', 'gate_b', 'vector_pool')}
    del _L0_ffn_all

    def _L1_attn_setup():
        import jax, jax.numpy as jnp
        import numpy as np
        D_MODEL = 512
        N_HEADS = 16
        HEAD_DIM = D_MODEL // N_HEADS
        B, T = (2, 512)

        def _alibi_bias(n_heads: int, seq_len: int) -> jnp.ndarray:
            exponents = jnp.arange(1, n_heads + 1, dtype=jnp.float32)
            slopes = 0.5 ** (exponents * 8.0 / n_heads)
            pos = jnp.arange(seq_len, dtype=jnp.float32)
            rel = pos[None, :] - pos[:, None]
            bias = slopes[:, None, None] * rel[None]
            causal = pos[None, :] <= pos[:, None]
            return jnp.where(causal[None], bias, -jnp.inf)
        key = jax.random.key(seed)
        ks = jax.random.split(key, 5)
        s = 1.0 / np.sqrt(D_MODEL)
        x = jax.random.normal(ks[0], (B, T, D_MODEL), dtype=jnp.float32)
        Wq = jax.random.uniform(ks[1], (D_MODEL, D_MODEL), jnp.float32, -s, s)
        Wk = jax.random.uniform(ks[2], (D_MODEL, D_MODEL), jnp.float32, -s, s)
        Wv = jax.random.uniform(ks[3], (D_MODEL, D_MODEL), jnp.float32, -s, s)
        Wo = jax.random.uniform(ks[4], (D_MODEL, D_MODEL), jnp.float32, -s, s)
        return {'x': x, 'Wq': Wq, 'Wk': Wk, 'Wv': Wv, 'Wo': Wo}
    _L1_attn_all = _L1_attn_setup()
    _L1_attn_in = {k: v for k, v in _L1_attn_all.items() if k in ('Wq', 'Wk', 'Wv', 'Wo')}
    del _L1_attn_all

    def _L1_xattn_setup():
        import jax, jax.numpy as jnp
        import numpy as np
        B, S, DIM, HD = (4, 256, 512, 128)
        H = DIM // HD
        GN_EPS = 0.001

        def _decay_masks(n_heads, seq_len):
            gam = 1.0 - 2.0 ** (-5.0 - jnp.arange(n_heads, dtype=jnp.float32))
            idx = jnp.arange(seq_len, dtype=jnp.float32)
            expo = idx[None, :] - idx[:, None]
            D = jnp.where(expo[None, :, :] <= 0, gam[:, None, None] ** expo[None, :, :], 0.0)
            return D / jnp.sqrt(D.sum(axis=-1))[:, None, :]
        key = jax.random.key(seed)
        ks = jax.random.split(key, 8)
        x = jax.random.normal(ks[0], (B, S, DIM), dtype=jnp.float32)
        k = jax.random.normal(ks[1], (B, S, DIM), dtype=jnp.float32)
        v = jax.random.normal(ks[2], (B, S, DIM), dtype=jnp.float32)
        Wh = jax.random.normal(ks[3], (H, HD, HD), dtype=jnp.float32) / np.sqrt(HD)
        wg_w = jax.random.normal(ks[4], (DIM, DIM), dtype=jnp.float32) / np.sqrt(DIM)
        wo_w = jax.random.normal(ks[5], (DIM, DIM), dtype=jnp.float32) / np.sqrt(DIM)
        gn_gamma = jnp.ones((DIM,), dtype=jnp.float32)
        gn_beta = jnp.zeros((DIM,), dtype=jnp.float32)
        return {'x': x, 'k': k, 'v': v, 'Wh': Wh, 'wg_w': wg_w, 'wo_w': wo_w, 'gn_gamma': gn_gamma, 'gn_beta': gn_beta}
    _L1_xattn_all = _L1_xattn_setup()
    _L1_xattn_in = {k: v for k, v in _L1_xattn_all.items() if k in ('Wh', 'wg_w', 'wo_w', 'gn_gamma', 'gn_beta')}
    del _L1_xattn_all

    def _L1_ffn_setup():
        import jax, jax.numpy as jnp
        import numpy as np
        B, S, H, E = (4, 1024, 512, 8)
        key = jax.random.key(seed)
        k1, k2, k3 = jax.random.split(key, 3)
        x = jax.random.normal(k1, (B, S, H), dtype=jnp.float32)
        Wg = jax.random.normal(k2, (H, E), dtype=jnp.float32) * (1.0 / np.sqrt(H))
        bg = jnp.zeros((E,), dtype=jnp.float32)
        We = jax.random.normal(k3, (H, H), dtype=jnp.float32) * (1.0 / np.sqrt(H))
        be = jnp.zeros((H,), dtype=jnp.float32)
        return {'x': x, 'Wg': Wg, 'bg': bg, 'We': We, 'be': be}
    _L1_ffn_all = _L1_ffn_setup()
    _L1_ffn_in = {k: v for k, v in _L1_ffn_all.items() if k in ('Wg', 'bg', 'We', 'be')}
    del _L1_ffn_all
    return {'x': x, 'ctx_2048': ctx_2048, 'L0_attn_Wq': _L0_attn_in['Wq'], 'L0_attn_bq': _L0_attn_in['bq'], 'L0_attn_Wk': _L0_attn_in['Wk'], 'L0_attn_bk': _L0_attn_in['bk'], 'L0_attn_Wv': _L0_attn_in['Wv'], 'L0_attn_bv': _L0_attn_in['bv'], 'L0_attn_Wo': _L0_attn_in['Wo'], 'L0_attn_bo': _L0_attn_in['bo'], 'L0_xattn_ssm_kernel': _L0_xattn_in['ssm_kernel'], 'L0_xattn_D': _L0_xattn_in['D'], 'L0_ffn_gate_w': _L0_ffn_in['gate_w'], 'L0_ffn_gate_b': _L0_ffn_in['gate_b'], 'L0_ffn_vector_pool': _L0_ffn_in['vector_pool'], 'L1_attn_Wq': _L1_attn_in['Wq'], 'L1_attn_Wk': _L1_attn_in['Wk'], 'L1_attn_Wv': _L1_attn_in['Wv'], 'L1_attn_Wo': _L1_attn_in['Wo'], 'L1_xattn_Wh': _L1_xattn_in['Wh'], 'L1_xattn_wg_w': _L1_xattn_in['wg_w'], 'L1_xattn_wo_w': _L1_xattn_in['wo_w'], 'L1_xattn_gn_gamma': _L1_xattn_in['gn_gamma'], 'L1_xattn_gn_beta': _L1_xattn_in['gn_beta'], 'L1_ffn_Wg': _L1_ffn_in['Wg'], 'L1_ffn_bg': _L1_ffn_in['bg'], 'L1_ffn_We': _L1_ffn_in['We'], 'L1_ffn_be': _L1_ffn_in['be']}

def reference(x, ctx_2048, L0_attn_Wq, L0_attn_bq, L0_attn_Wk, L0_attn_bk, L0_attn_Wv, L0_attn_bv, L0_attn_Wo, L0_attn_bo, L0_xattn_ssm_kernel, L0_xattn_D, L0_ffn_gate_w, L0_ffn_gate_b, L0_ffn_vector_pool, L1_attn_Wq, L1_attn_Wk, L1_attn_Wv, L1_attn_Wo, L1_xattn_Wh, L1_xattn_wg_w, L1_xattn_wo_w, L1_xattn_gn_gamma, L1_xattn_gn_beta, L1_ffn_Wg, L1_ffn_bg, L1_ffn_We, L1_ffn_be):
    import jax
    import jax.numpy as jnp

    def _L0_attn_ref(hidden_states, Wq, bq, Wk, bk, Wv, bv, Wo, bo):
        import jax, jax.numpy as jnp
        import numpy as np
        import math
        HID = 512
        HEADS = 16
        HEAD_DIM = HID // HEADS
        SEQ = 1024
        BATCH = 1
        ROPE_THETA = 10000.0
        START_RATIO = 0.1
        RECENT_RATIO = 0.25

        def _rope_sin_cos(seq_len, dtype):
            theta = 1.0 / ROPE_THETA ** (jnp.arange(0, HEAD_DIM, 2, dtype=jnp.float32) / HEAD_DIM)
            sinusoid = jnp.arange(seq_len, dtype=jnp.float32)[:, None] * theta[None, :]
            return (jnp.sin(sinusoid).astype(dtype), jnp.cos(sinusoid).astype(dtype))

        def _apply_rope(x, sin, cos):
            x1, x2 = (x[..., 0::2], x[..., 1::2])
            return jnp.concatenate([x1 * cos - x2 * sin, x1 * sin + x2 * cos], axis=-1)
        b, s, _ = hidden_states.shape

        def proj(W, bias):
            y = jnp.einsum('bsd,ed->bse', hidden_states, W) + bias
            return y.reshape(b, s, HEADS, HEAD_DIM).transpose(0, 2, 1, 3)
        q = proj(Wq, bq)
        k = proj(Wk, bk)
        v = proj(Wv, bv)
        sin, cos = _rope_sin_cos(s, hidden_states.dtype)
        q = _apply_rope(q, sin, cos)
        k = _apply_rope(k, sin, cos)
        scale = 1.0 / math.sqrt(HEAD_DIM)
        scores = jnp.einsum('bhqd,bhkd->bhqk', q, k) * scale
        start_budget = math.ceil(START_RATIO * s)
        recent_budget = math.ceil(RECENT_RATIO * s)
        pos = np.arange(s)
        cam = jnp.asarray((pos < start_budget) | (pos >= s - recent_budget))
        neg = jnp.finfo(scores.dtype).min
        scores = jnp.where(cam[None, None, None, :], scores, neg)
        attn = jax.nn.softmax(scores, axis=-1)
        out = jnp.einsum('bhqk,bhkd->bhqd', attn, v)
        out = out.transpose(0, 2, 1, 3).reshape(b, s, HID)
        return jnp.einsum('bsd,ed->bse', out, Wo) + bo

    def _L0_xattn_ref(k, v, q, ssm_kernel, D, head_dim):
        import jax, jax.numpy as jnp
        import numpy as np
        B, HD, L = k.shape
        H = HD // head_dim
        fft_size = 2 * L
        k_ = k.reshape(B, H, head_dim, L)
        v_ = v.reshape(B, H, head_dim, L)
        q_ = q.reshape(B, H, head_dim, L)
        kv = jnp.einsum('bhil,bhjl->bijhl', k_, v_)
        kv_f = jnp.fft.rfft(kv, n=fft_size)
        kernel_f = jnp.fft.rfft(ssm_kernel, n=fft_size)
        y = jnp.fft.irfft(kv_f * kernel_f, n=fft_size)[..., :L]
        out = y + kv * D[None, None, None, :, None]
        out = jnp.einsum('bijhl,bhil->bjhl', out, q_)
        out = jnp.transpose(out, (0, 2, 1, 3)).reshape(B, H * head_dim, L)
        return out.astype(k.dtype)

    def _L0_ffn_ref(x, gate_w, gate_b, vector_pool):
        import jax, jax.numpy as jnp
        import numpy as np
        LAYER_IDX = 16
        num_vector = vector_pool.shape[0]
        scores = jnp.einsum('bsh,vh->bsv', x, gate_w) + gate_b
        max_idx = jnp.argmax(scores, axis=-1)
        safe_idx = jnp.minimum(max_idx, num_vector - 1)
        replacement = vector_pool[safe_idx, LAYER_IDX]
        keep = (max_idx == num_vector)[..., None]
        return jnp.where(keep, x, replacement)

    def _L1_attn_ref(x, Wq, Wk, Wv, Wo):
        import jax, jax.numpy as jnp
        import numpy as np
        D_MODEL = 512
        N_HEADS = 16
        HEAD_DIM = D_MODEL // N_HEADS
        B, T = (2, 512)

        def _alibi_bias(n_heads: int, seq_len: int) -> jnp.ndarray:
            exponents = jnp.arange(1, n_heads + 1, dtype=jnp.float32)
            slopes = 0.5 ** (exponents * 8.0 / n_heads)
            pos = jnp.arange(seq_len, dtype=jnp.float32)
            rel = pos[None, :] - pos[:, None]
            bias = slopes[:, None, None] * rel[None]
            causal = pos[None, :] <= pos[:, None]
            return jnp.where(causal[None], bias, -jnp.inf)
        Bsz, Tlen, _ = x.shape
        H, D = (N_HEADS, HEAD_DIM)

        def split_heads(t):
            return t.reshape(Bsz, Tlen, H, D).transpose(0, 2, 1, 3)
        q = split_heads(x @ Wq.T)
        k = split_heads(x @ Wk.T)
        v = split_heads(x @ Wv.T)
        scale = jnp.sqrt(jnp.float32(D))
        scores = jnp.einsum('bhqd,bhkd->bhqk', q, k) / scale
        scores = scores + _alibi_bias(H, Tlen)[None]
        attn = jax.nn.softmax(scores, axis=-1)
        out = jnp.einsum('bhqk,bhkd->bhqd', attn, v)
        out = out.transpose(0, 2, 1, 3).reshape(Bsz, Tlen, H * D)
        return out @ Wo.T

    def _L1_xattn_ref(x, k, v, Wh, wg_w, wo_w, gn_gamma, gn_beta):
        import jax, jax.numpy as jnp
        import numpy as np
        B, S, DIM, HD = (4, 256, 512, 128)
        H = DIM // HD
        GN_EPS = 0.001

        def _decay_masks(n_heads, seq_len):
            gam = 1.0 - 2.0 ** (-5.0 - jnp.arange(n_heads, dtype=jnp.float32))
            idx = jnp.arange(seq_len, dtype=jnp.float32)
            expo = idx[None, :] - idx[:, None]
            D = jnp.where(expo[None, :, :] <= 0, gam[:, None, None] ** expo[None, :, :], 0.0)
            return D / jnp.sqrt(D.sum(axis=-1))[:, None, :]
        b, s, dim = x.shape
        h, hd, _ = Wh.shape
        xh = x.reshape(b, s, h, hd)
        kh = k.reshape(b, s, h, hd)
        vh = v.reshape(b, s, h, hd)
        Q = jnp.einsum('bshd,hde->bshe', xh, Wh)
        K = jnp.einsum('bshd,hde->bshe', kh, Wh)
        V = jnp.einsum('bshd,hde->bshe', vh, Wh)
        scores = jnp.einsum('bshe,bthe->bhst', Q, K) / jnp.sqrt(jnp.float32(hd))
        Dn = _decay_masks(h, s)
        masked = scores * Dn[None, :, :, :]
        A = jnp.maximum(jnp.abs(masked.sum(axis=0)), 1.0)
        O = jnp.einsum('hst,bthe->bshe', A, V).reshape(b, s, dim)
        mu = O.mean(axis=-1, keepdims=True)
        var = O.var(axis=-1, keepdims=True)
        Y = (O - mu) / jnp.sqrt(var + GN_EPS) * gn_gamma + gn_beta
        W = jax.nn.relu(x @ wg_w)
        return W * Y @ wo_w

    def _L1_ffn_ref(x, Wg, bg, We, be):
        import jax, jax.numpy as jnp
        import numpy as np
        B, S, H, E = (4, 1024, 512, 8)
        b, s, h = x.shape
        hidden = x.reshape(-1, h)
        logits = hidden @ Wg + bg
        probs = jax.nn.softmax(logits, axis=1)
        best = jnp.argmax(probs, axis=1)
        order = jnp.argsort(best)
        sorted_hidden = hidden[order]
        expert_out = sorted_hidden @ We + be
        combined = expert_out.reshape(b, s, h)
        best_p = jnp.take_along_axis(probs, best[:, None], axis=1)[:, 0]
        return combined * best_p.reshape(b, s, 1)
    x = x + _L0_attn_ref(_layernorm(x, axis=-1), L0_attn_Wq, L0_attn_bq, L0_attn_Wk, L0_attn_bk, L0_attn_Wv, L0_attn_bv, L0_attn_Wo, L0_attn_bo)
    x = x + _L0_xattn_ref(ctx_2048, ctx_2048, _layernorm(x, axis=-1), L0_xattn_ssm_kernel, L0_xattn_D, 8)
    x = x + _L0_ffn_ref(_layernorm(x, axis=-1), L0_ffn_gate_w, L0_ffn_gate_b, L0_ffn_vector_pool)
    x = x + _L1_attn_ref(_layernorm(x, axis=-1), L1_attn_Wq, L1_attn_Wk, L1_attn_Wv, L1_attn_Wo)
    x = x + _L1_xattn_ref(_layernorm(x, axis=-1), ctx_2048, ctx_2048, L1_xattn_Wh, L1_xattn_wg_w, L1_xattn_wo_w, L1_xattn_gn_gamma, L1_xattn_gn_beta)
    x = x + _L1_ffn_ref(_layernorm(x, axis=-1), L1_ffn_Wg, L1_ffn_bg, L1_ffn_We, L1_ffn_be)
    return x

_drawn_inputs = setup_inputs


def setup_inputs(seed=0):
    import zlib

    import numpy as np

    out = dict(_drawn_inputs(seed))
    spreads = {'L0_attn_bq': (0.0, 0.8),
     'L0_attn_bk': (0.0, 0.8),
     'L0_attn_bv': (0.0, 0.1),
     'L0_attn_bo': (0.0, 0.1),
     'L0_ffn_gate_b': (0.0, 0.48),
     'L1_xattn_gn_gamma': (1.0, 0.6),
     'L1_xattn_gn_beta': (0.0, 0.8),
     'L1_ffn_bg': (0.0, 0.8),
     'L1_ffn_be': (0.0, 0.8)}
    factors = {'L0_attn_Wq': 7.101,
     'L0_attn_Wk': 7.211,
     'L0_ffn_gate_w': 2.977,
     'L0_ffn_vector_pool': 2.992,
     'L1_attn_Wq': 8.0,
     'L1_attn_Wk': 8.0,
     'L1_attn_Wv': 8.0,
     'L1_attn_Wo': 8.0,
     'L1_xattn_Wh': 3.9,
     'L1_xattn_wg_w': 4.535,
     'L1_xattn_wo_w': 3.832,
     'L1_ffn_Wg': 8.0,
     'L1_ffn_We': 8.0}
    for name, (base, spread) in spreads.items():
        noise = np.random.default_rng([zlib.crc32(name.encode()), seed]).standard_normal(out[name].shape)
        drawn = base * np.exp(spread * noise) if base else spread * noise
        out[name] = jnp.asarray(drawn.astype(out[name].dtype))
    for name, factor in factors.items():
        out[name] = (out[name] * factor).astype(out[name].dtype)
    return out
```

```python
from contextlib import ExitStack

import concourse.bass as bass
from concourse import mybir
import numpy as np

P = 128
B, S, D = 8, 256, 512
TOK = B * S
TILES = TOK // P
TB = S // P
KC = D // P
H, HD = 16, 32
G = H // 4
LN_EPS = 1e-5
START = -(-S // 10)
RECENT = -(-S // 4)
NKEY = START + RECENT

CH = 32
CD = S // CH
NDEL = 5
CEXT = 12
CW = CD * B
NV = 1250
VCH = 417
RH, RD = 4, 128
GN_EPS = 1e-3
NE = 8

F32 = mybir.dt.float32
BF16 = mybir.dt.bfloat16
U32 = mybir.dt.uint32
I32 = mybir.dt.int32
ALU = mybir.AluOpType
ACT = mybir.ActivationFunctionType
AX = mybir.AxisListType
SWAP16 = [(i + 16) % 32 for i in range(32)]


def wait(eng, sem, value):
    if isinstance(value, int) and value <= 0:
        return
    eng.wait_ge(sem, value)


def wait_apart(eng, sem, value, passed):
    eng.wait_ge(sem, value)
    eng.sem_inc(passed, 1)


def attention(nc, first_layer, x_sb, big, ident, w_dram, consts, x_dram):
    A = first_layer
    pre = "a_" if A else "d_"
    NQ = NKEY if A else S
    with ExitStack() as ctx:
        def sb(name, shape, dt=F32):
            return ctx.enter_context(nc.sbuf_tensor(pre + name, shape, dt))

        def sem(name):
            return ctx.enter_context(nc.semaphore(pre + name))

        wq, wk, wv, wo = (sb(n, [P, KC, D]) for n in ("wq", "wk", "wv", "wo"))
        xn = sb("xn", [P, TB, D])
        xnT = sb("xnT", [P, KC, S])
        qT = sb("qT", [P, G, S])
        kD = sb("kD", [P, G, 4, NQ])
        v = sb("v", [P, 1 if A else TB, D])
        PW = TB * P if A else 3 * P
        prob = sb("prob", [P, 2, 4, PW])
        probT = sb("probT", [P, 4, S])
        probT1 = None if A else sb("probT1", [P, 4, P])
        oT = sb("oT", [P, G, S])
        xo = sb("xo", [P, TB, D])
        nmax = sb("nmax", [P, 2, 8])
        mx = sb("mx", [P, 2, 8])
        rsum = sb("rsum", [P, 2, 8])
        rinv = sb("rinv", [P, 2, 8])
        st = sb("st", [P, 2, TB, 6])
        mv = sb("mv", [P, 2, TB, 2])
        ve = sb("ve", [P, 2, TB])
        rstd = sb("rstd", [P, 2, TB])
        mhalf = sb("mhalf", [P, TB])
        if A:
            xkT = sb("xkT", [P, KC, NKEY])
            bq = sb("bq", [P, G])
            bk, bv, bo = (sb(n, [P, D]) for n in ("bk", "bv", "bo"))
            qcos, qsin = sb("qcos", [P, S]), sb("qsin", [P, S])
            kcos, ksin = sb("kcos", [P, HD]), sb("ksin", [P, HD])
            qraw, qsw, qm1, qm2 = (sb(n, [P, S]) for n in ("qraw", "qsw", "qm1", "qm2"))
            kraw, km1, km2, krope = (sb(n, [P, D]) for n in ("kraw", "km1", "km2", "krope"))
        else:
            rel = sb("rel", [P, 3 * P])
            slope = sb("slope", [P, H])
            alibi = sb("alibi", [P, H, 3 * P])

        bank = [ctx.enter_context(nc.psum_tensor(f"{pre}bank{i}", [P, 512], F32)) for i in range(3)]
        ps_s = ctx.enter_context(nc.psum_tensor(pre + "ps_s", [P, 3, 512], F32))
        ps_t = ctx.enter_context(nc.psum_tensor(pre + "ps_t", [P, 2, 512], F32))

        ld_w, ld_x0, ld_x, ld_c = sem("ld_w"), sem("ld_x0"), sem("ld_x"), sem("ld_c")
        stats, lnvar, lnrstd, normed = sem("stats"), sem("lnvar"), sem("lnrstd"), sem("normed")
        ostats, olnvar, olnrstd, onormed = sem("ostats"), sem("olnvar"), sem("olnrstd"), sem("onormed")
        aggr, oaggr = sem("aggr"), sem("oaggr")
        pe_xT, pe_q, pe_k, pe_v, pe_s = sem("pe_xT"), sem("pe_q"), sem("pe_k"), sem("pe_v"), sem("pe_s")
        pe_t, pe_pv, pe_o, pe_oT = sem("pe_t"), sem("pe_pv"), sem("pe_o"), sem("pe_oT")
        xT_copied, q_copied, q_ready = sem("xT_copied"), sem("q_copied"), sem("q_ready")
        k_act, k_dve, v_copied = sem("k_act"), sem("k_dve"), sem("v_copied")
        maxed, negated, exped, summed, scaled = (sem("maxed"), sem("negated"), sem("exped"),
                                                 sem("summed"), sem("scaled"))
        pT_act, pT_dve, pv_copied = sem("pT_act"), sem("pT_dve"), sem("pv_copied")
        x_added, x_biased, oT_copied = sem("x_added"), sem("x_biased"), sem("oT_copied")
        zeroed, setup = sem("zeroed"), sem("setup")
        passed_dve, passed_pool = sem("passed_dve"), sem("passed_pool")
        if A:
            pe_kn, kn_copied, k_mul, k_rope = sem("pe_kn"), sem("kn_copied"), sem("k_mul"), sem("k_rope")
            q_swap, q_cos, q_sin, xk_ready = sem("q_swap"), sem("q_cos"), sem("q_sin"), sem("xk_ready")

        block = ctx.enter_context(nc.Block())

        def xt(b, t):
            return x_sb[:, bass.ds((b * TB + t) * D, D)]

        def proj_of(b, g):
            return (b, 3, 4 * b + 3) if g == 0 else (b + 1, g - 1, 4 * b + 3 + g)

        @block.sync
        def _(sp):
            if A:
                xr = x_dram.rearrange("(t p) d -> p t d", p=P)
                xs = x_sb[:].rearrange("p (t d) -> p t d", d=D)
                sp.dma_start(xs[:, 0:TB], xr[:, 0:TB]).then_inc(ld_x0, 16)
            sp.dma_start(wq[:], w_dram["wq"]).then_inc(ld_w, 16)
            sp.dma_start(wk[:], w_dram["wk"]).then_inc(ld_w, 16)
            sp.dma_start(wv[:], w_dram["wv"]).then_inc(ld_w, 16)
            if A:
                for b in range(1, B):
                    sp.dma_start(xs[:, b * TB:(b + 1) * TB], xr[:, b * TB:(b + 1) * TB]).then_inc(ld_x, 16)
            sp.dma_start(wo[:], w_dram["wo"]).then_inc(ld_w, 16)

        @block.gpsimd
        def _(pool):
            def rstd_of(b, mv_, ve_, rstd_, got, done1, done2):
                wait_apart(pool, got, b + 1, passed_pool)
                nc.gpsimd.tensor_scalar(ve_, mv_[:, :, 1], LN_EPS, None, ALU.add).then_inc(done1, 1)
                pool.wait_ge(done1, b + 1)
                nc.gpsimd.tensor_tensor(rstd_, ve_, mhalf[:], ALU.pow).then_inc(done2, 1)

            def ln_in(b):
                rstd_of(b, mv[:, 0], ve[:, 0], rstd[:, 0], aggr, lnvar, lnrstd)

            def ln_out(b):
                rstd_of(b, mv[:, 1], ve[:, 1], rstd[:, 1], oaggr, olnvar, olnrstd)

            def scale_probs(n, g):
                pool.wait_ge(summed, n + 1)
                pr = prob[:, g % 2]
                iv = rinv[:, g % 2]
                if A:
                    pr = pr.rearrange("p j (t k) -> p j t k", t=TB)[:, :, :, 0:NKEY]
                    iv = iv.rearrange("p (t j one) -> p j t one", t=TB, one=1).broadcast_to([P, 4, TB, NKEY])
                    nc.gpsimd.tensor_tensor(pr, pr, iv, ALU.mult).then_inc(scaled, 1)
                else:
                    i0 = iv[:, 0:4].rearrange("p (j one) -> p j one", one=1).broadcast_to([P, 4, P])
                    i1 = iv[:, 4:8].rearrange("p (j one) -> p j one", one=1).broadcast_to([P, 4, 2 * P])
                    nc.gpsimd.tensor_tensor(pr[:, :, 0:P], pr[:, :, 0:P], i0, ALU.mult)
                    nc.gpsimd.tensor_tensor(pr[:, :, P:], pr[:, :, P:], i1, ALU.mult).then_inc(scaled, 1)

            def q_times_cos(n):
                pool.wait_ge(q_copied, n + 1)
                wait(pool, q_ready, n)
                nc.gpsimd.tensor_tensor(qm1[:], qraw[:], qcos[:], ALU.mult).then_inc(q_cos, 1)

            def kept_keys(b):
                wait_apart(pool, xT_copied, TB * (b + 1), passed_pool)
                nc.gpsimd.tensor_copy(xkT[:, :, 0:START], xnT[:, :, 0:START])
                nc.gpsimd.tensor_copy(xkT[:, :, START:], xnT[:, :, S - RECENT:]).then_inc(xk_ready, 1)

            def k_rotate(b):
                pool.wait_ge(kn_copied, b + 1)
                kv3 = lambda t: t[0:NKEY].rearrange("p (h f) -> p h f", f=HD)
                tb = lambda t, a, z: t[0:NKEY, a:z].rearrange("p (one f) -> p one f", one=1).broadcast_to(
                    [NKEY, H, z - a])
                nc.gpsimd.tensor_tensor(kv3(km1), kv3(kraw), tb(kcos, 0, HD), ALU.mult)
                nc.gpsimd.tensor_tensor(kv3(km2)[:, :, 0:16], kv3(kraw)[:, :, 16:32], tb(ksin, 0, 16), ALU.mult)
                nc.gpsimd.tensor_tensor(kv3(km2)[:, :, 16:32], kv3(kraw)[:, :, 0:16], tb(ksin, 16, 32),
                                        ALU.mult).then_inc(k_mul, 1)
                pool.wait_ge(k_mul, b + 1)
                nc.gpsimd.tensor_tensor(krope[0:NKEY], km1[0:NKEY], km2[0:NKEY], ALU.add).then_inc(k_rope, 1)

            def add_bo(b):
                pool.wait_ge(normed, b + 1)
                nc.gpsimd.tensor_tensor(xt(b, 0), xt(b, 0), bo[:], ALU.add)
                nc.gpsimd.tensor_tensor(xt(b, 1), xt(b, 1), bo[:], ALU.add).then_inc(x_biased, 1)

            nc.gpsimd.memset(mhalf[:], -0.5).then_inc(setup, 1)
            pool.wait_ge(setup, 1)
            if A:
                pool.wait_ge(ld_c, 16 * 8)
            else:
                pool.wait_ge(ld_c, 16 * 2)
                for h in range(0, H, 4):
                    nc.gpsimd.tensor_tensor(
                        alibi[:, h:h + 4], rel[:].rearrange("p (one k) -> p one k", one=1).broadcast_to([P, 4, 3 * P]),
                        slope[:, h:h + 4].rearrange("p (h one) -> p h one", one=1).broadcast_to([P, 4, 3 * P]),
                        ALU.mult).then_inc(setup, 1)
            ln_in(0)
            if A:
                kept_keys(0)
                k_rotate(0)
                add_bo(0)
                for n in range(3):
                    q_times_cos(n)

            def slot(b, g, first, last):
                n = 4 * b + g
                if g == 0 and not last:
                    ln_in(b + 1)
                if g == 1 and not first:
                    ln_out(b - 1)
                if A and g == 1 and not last:
                    kept_keys(b + 1)
                scale_probs(n, g)
                if A and (g == 0 or not last):
                    q_times_cos(proj_of(b, g)[2])
                if A and not last:
                    if g == 1:
                        k_rotate(b + 1)
                    if g == 2:
                        add_bo(b + 1)

            def batch(b, first=False, last=False):
                for g in range(G):
                    slot(b, g, first, last)

            batch(0, first=True)
            with pool.Fori(1, B - 1) as b:
                batch(b)
            batch(B - 1, last=True)
            ln_out(B - 1)

        @block.vector
        def _(dve):
            def ln_stats(b, i, got, agg):
                if not isinstance(b, int):
                    dve.sem_inc(passed_dve, 1)
                for t in range(TB):
                    last = nc.vector.bn_stats(st[:, i, t], xt(b, t))
                last.then_inc(got, 1)
                wait_apart(dve, got, b + 1, passed_dve)
                for t in range(TB):
                    last = nc.vector.bn_aggr(mv[:, i, t], st[:, i, t])
                last.then_inc(agg, 1)

            def ln_apply(b, i, got, out, done):
                dve.wait_ge(got, b + 1)
                for t in range(TB):
                    last = nc.vector.tensor_scalar(out[:, t], xt(b, t), mv[:, i, t, 0:1], rstd[:, i, t:t + 1],
                                                   ALU.subtract, ALU.mult)
                last.then_inc(done, 1)

            def ln_in(b):
                ln_stats(b, 0, stats, aggr)

            def ln_in_apply(b):
                wait(dve, pe_xT, TB * b)
                ln_apply(b, 0, lnrstd, xn, normed)

            def ln_out(b):
                ln_stats(b, 1, ostats, oaggr)

            def ln_out_apply(b):
                wait(dve, pe_oT, TB * b)
                ln_apply(b, 1, olnrstd, xo, onormed)

            def max_scores(n, g):
                dve.wait_ge(pe_s, n + 1)
                wait(dve, exped, n - 1)
                wait(dve, pe_t, n - 1)
                if not A:
                    dve.sem_inc(passed_dve, 1)
                if A:
                    nc.vector.tensor_reduce(mx[:, g % 2].rearrange("p (t j) -> p t j", t=TB),
                                            ps_s[:, 0:TB, 0:4 * NKEY].rearrange("p t (j k) -> p t j k", j=4),
                                            AX.X, ALU.max).then_inc(maxed, 1)
                else:
                    for j in range(4):
                        nc.vector.tensor_tensor_reduce(
                            out=prob[:, g % 2, j, 0:P], in0=ps_s[:, 0, j * P:(j + 1) * P],
                            in1=alibi[:, 4 * g + j, 0:P], scale=1.0, scalar=-3e38, op0=ALU.add, op1=ALU.max,
                            accum_out=mx[:, g % 2, j:j + 1])
                        last = nc.vector.tensor_tensor_reduce(
                            out=prob[:, g % 2, j, P:3 * P],
                            in0=ps_s[:, 1 + j // 2, (j % 2) * S:(j % 2) * S + S],
                            in1=alibi[:, 4 * g + j, P:3 * P], scale=1.0, scalar=-3e38, op0=ALU.add, op1=ALU.max,
                            accum_out=mx[:, g % 2, 4 + j:5 + j])
                    last.then_inc(maxed, 1)
                dve.wait_ge(maxed, n + 1)
                nc.vector.tensor_scalar(nmax[:, g % 2], mx[:, g % 2], -1.0, None, ALU.mult).then_inc(negated, 1)

            def turn_copy(n):
                dve.wait_ge(pe_t, n + 1)
                nc.vector.tensor_copy(probT[:, 0:2], ps_t[:, 0].rearrange("p (j q) -> p j q", j=2)).then_inc(pT_dve, 1)

            def reciprocals(n, g):
                dve.wait_ge(exped, n + 1)
                wait(dve, scaled, n - 1)
                nc.vector.reciprocal(rinv[:, g % 2], rsum[:, g % 2]).then_inc(summed, 1)

            def q_rotate(n, g):
                wait_apart(dve, q_copied, n + 1, passed_dve)
                nc.vector.stream_shuffle(qsw[:], qraw[:], SWAP16).then_inc(q_swap, 1)
                dve.wait_ge(q_swap, n + 1)
                nc.vector.tensor_tensor(qm2[:], qsw[:], qsin[:], ALU.mult).then_inc(q_sin, 1)
                dve.wait_ge(q_sin, n + 1)
                dve.wait_ge(q_cos, n + 1)
                nc.vector.tensor_tensor(qT[:, g], qm1[:], qm2[:], ALU.add).then_inc(q_ready, 1)

            def k_copy(n, g):
                dve.wait_ge(pe_k, n + 1)
                for j in (0, 1):
                    last = nc.vector.tensor_copy(kD[32 * j:32 * j + 32, g, j], bank[1][32 * j:32 * j + 32, 0:S])
                last.then_inc(k_dve, 1)

            def k_copy_a(b):
                dve.wait_ge(pe_k, b + 1)
                for j in (0, 1):
                    last = nc.vector.tensor_copy(kD[32 * j:32 * j + 32, :, j],
                                                 bank[2][32 * j:32 * j + 32, 0:4 * NKEY]
                                                 .rearrange("p (g k) -> p g k", g=G))
                last.then_inc(k_dve, 1)

            def kn_copy(b):
                dve.wait_ge(pe_kn, b + 1)
                wait(dve, k_mul, b)
                nc.vector.tensor_tensor(kraw[0:NKEY], bank[1][0:NKEY, :], bk[0:NKEY], ALU.add)\
                    .then_inc(kn_copied, 1)

            def v_copy(n, g):
                dve.wait_ge(pe_v, n + 1)
                c = slice(g * P, g * P + P)
                if A:
                    nc.vector.tensor_tensor(v[0:NKEY, 0, c], bank[1][0:NKEY, 0:P], bv[0:NKEY, c], ALU.add)\
                        .then_inc(v_copied, 1)
                else:
                    nc.vector.tensor_copy(v[:, :, c], bank[1][:, 0:TB * P].rearrange("p (t f) -> p t f", t=TB))\
                        .then_inc(v_copied, 1)

            def add_out(b):
                if A:
                    dve.wait_ge(x_biased, b + 1)
                for t in range(TB):
                    dve.wait_ge(pe_o, TB * b + t + 1)
                    nc.vector.tensor_tensor(xt(b, t), xt(b, t), bank[t][:], ALU.add).then_inc(x_added, 1)

            nc.vector.memset(kD[:], 0.0).then_inc(zeroed, 1)
            if A:
                nc.vector.memset(prob[:], 0.0).then_inc(zeroed, 1)
                nc.vector.memset(v[:], 0.0).then_inc(zeroed, 1)
                dve.wait_ge(zeroed, 3)
                dve.wait_ge(ld_x0, 16)
                dve.wait_ge(ld_c, 16 * 8)
            else:
                dve.wait_ge(zeroed, 1)
            ln_in(0)
            ln_in_apply(0)
            if A:
                kn_copy(0)
                k_copy_a(0)
            for g in range(3):
                if A:
                    q_rotate(g, g)
                else:
                    k_copy(g, g)
                v_copy(g, g)
            if A:
                dve.wait_ge(ld_x, 16 * (B - 1))
            else:
                dve.wait_ge(setup, 5)

            def slot(b, g, first, last):
                n = 4 * b + g
                _, pg, pn = proj_of(b, g)
                project = g == 0 or not last
                if g == 0 and not last:
                    ln_in(b + 1)
                max_scores(n, g)
                if not (first and g == 0):
                    turn_copy(n - 1)
                if g == 0 and not last:
                    ln_in_apply(b + 1)
                if project and not A:
                    k_copy(pn, pg)
                reciprocals(n, g)
                if project and A:
                    q_rotate(pn, pg)
                if not (first and g == 0):
                    dve.wait_ge(pe_pv, n)
                    nc.vector.tensor_copy(oT[:, (g - 1) % 4], bank[0][:, 0:S]).then_inc(pv_copied, 1)
                if project:
                    v_copy(pn, pg)
                if A and not last and g == 1:
                    kn_copy(b + 1)
                if A and not last and g == 3:
                    k_copy_a(b + 1)
                if not first:
                    if g == 0:
                        add_out(b - 1)
                        dve.wait_ge(x_added, TB * b)
                        ln_out(b - 1)
                    if g == 1:
                        ln_out_apply(b - 1)

            def batch(b, first=False, last=False):
                for g in range(G):
                    slot(b, g, first, last)

            batch(0, first=True)
            with dve.Fori(1, B - 1) as b:
                batch(b)
            batch(B - 1, last=True)
            turn_copy(4 * B - 1)
            dve.wait_ge(pe_pv, 4 * B)
            nc.vector.tensor_copy(oT[:, 3], bank[0][:, 0:S]).then_inc(pv_copied, 1)
            add_out(B - 1)
            dve.wait_ge(x_added, TB * B)
            ln_out(B - 1)
            ln_out_apply(B - 1)

        @block.scalar
        def _(act):
            nc.scalar.preload_act_table(ACT.Exp)
            if A:
                for name, t in (("bq", bq), ("bk", bk), ("bv", bv), ("bo", bo), ("qcos", qcos), ("qsin", qsin)):
                    act.dma_start(t[:], consts[name]).then_inc(ld_c, 16)
                act.dma_start(kcos[0:NKEY], consts["kcos"]).then_inc(ld_c, 16)
                act.dma_start(ksin[0:NKEY], consts["ksin"]).then_inc(ld_c, 16)
            else:
                act.dma_start(rel[:], consts["rel"]).then_inc(ld_c, 16)
                act.dma_start(slope[:], consts["slope"]).then_inc(ld_c, 16)
            act.wait_ge(zeroed, 3 if A else 1)

            def xT_copy(b):
                for t in range(TB):
                    act.wait_ge(pe_xT, TB * b + t + 1)
                    nc.scalar.activation(xnT[:, :, t * P:(t + 1) * P],
                                         bank[t][:].rearrange("p (k q) -> p k q", k=KC),
                                         ACT.Copy).then_inc(xT_copied, 1)

            def q_copy(n, g):
                act.wait_ge(pe_q, n + 1)
                if A:
                    wait(act, q_swap, n)
                    wait(act, q_cos, n)
                    nc.scalar.activation(qraw[:], bank[0][:, 0:S], ACT.Identity, bias=bq[:, g:g + 1])\
                        .then_inc(q_copied, 1)
                else:
                    nc.scalar.activation(qT[:, g], bank[0][:, 0:S], ACT.Copy, scale=float(HD) ** -0.5)\
                        .then_inc(q_copied, 1)

            def k_copy(n, g):
                act.wait_ge(pe_k, n + 1)
                for j in (2, 3):
                    last = nc.scalar.activation(kD[32 * j:32 * j + 32, g, j], bank[1][32 * j:32 * j + 32, 0:S],
                                                ACT.Copy)
                last.then_inc(k_act, 1)

            def k_copy_a(b):
                act.wait_ge(pe_k, b + 1)
                for j in (2, 3):
                    last = nc.scalar.activation(kD[32 * j:32 * j + 32, :, j],
                                                bank[2][32 * j:32 * j + 32, 0:4 * NKEY]
                                                .rearrange("p (g k) -> p g k", g=G), ACT.Copy)
                last.then_inc(k_act, 1)

            def exponentials(n, g):
                act.wait_ge(negated, n + 1)
                wait(act, summed, n - 1)
                for j in range(4):
                    for t in range(TB):
                        c = t * 4 + j
                        if A:
                            out = prob[:, g % 2, j, t * P:t * P + NKEY]
                            src = ps_s[:, t, j * NKEY:(j + 1) * NKEY]
                        else:
                            src = out = prob[:, g % 2, j, 0:P] if t == 0 else prob[:, g % 2, j, P:3 * P]
                        last = nc.scalar.activation(out, src, ACT.Exp, bias=nmax[:, g % 2, c:c + 1],
                                                    accum_out=rsum[:, g % 2, c:c + 1])
                last.then_inc(exped, 1)

            def turn_copy(n):
                act.wait_ge(pe_t, n + 1)
                last = nc.scalar.activation(probT[:, 2:4], ps_t[:, 1].rearrange("p (j q) -> p j q", j=2), ACT.Copy)
                if not A:
                    last = nc.scalar.activation(probT1[:], bank[2][:].rearrange("p (j q) -> p j q", j=4), ACT.Copy)
                last.then_inc(pT_act, 1)

            def oT_copy(b):
                for t in range(TB):
                    act.wait_ge(pe_oT, TB * b + t + 1)
                    src = bank[t][:].rearrange("p (k q) -> p k q", k=KC)
                    if A:
                        dst = big[:, :, bass.ds(b + t * P * B, P, step=B)] if isinstance(b, int) else \
                            big[:].rearrange("p k (q b) -> p k q b", b=B)[:, :, t * P:(t + 1) * P, bass.ds(b, 1)]
                        if not isinstance(b, int):
                            src = src.rearrange("p k (q one) -> p k q one", one=1)
                    else:
                        dst = big[:, :, bass.ds(b * S + t * P, P)]
                    nc.scalar.activation(dst, src, ACT.Copy).then_inc(oT_copied, 1)

            xT_copy(0)
            if A:
                k_copy_a(0)
            for g in range(3):
                q_copy(g, g)
                if not A:
                    k_copy(g, g)

            def slot(b, g, first, last):
                n = 4 * b + g
                _, pg, pn = proj_of(b, g)
                if not (first and g == 0):
                    turn_copy(n - 1)
                exponentials(n, g)
                if g == 0 or not last:
                    q_copy(pn, pg)
                    if not A:
                        k_copy(pn, pg)
                if g == 0 and not last:
                    xT_copy(b + 1)
                if A and g == 3 and not last:
                    k_copy_a(b + 1)
                if g == 2 and not first:
                    oT_copy(b - 1)

            def batch(b, first=False, last=False):
                for g in range(G):
                    slot(b, g, first, last)

            batch(0, first=True)
            with act.Fori(1, B - 1) as b:
                batch(b)
            batch(B - 1, last=True)
            turn_copy(4 * B - 1)
            oT_copy(B - 1)

        @block.tensor
        def _(pe):
            mm, tr = nc.tensor.matmul, nc.tensor.transpose

            def turn_x(b, src, ready, done, copied):
                pe.wait_ge(ready, b + 1)
                for t in range(TB):
                    for k in range(KC):
                        last = tr(bank[t][:, k * P:(k + 1) * P], src[:, t, k * P:(k + 1) * P], ident[:])
                    last.then_inc(done, 1)

            def project_q(n, g):
                for k in range(KC):
                    last = mm(bank[0][:, 0:S], wq[:, k, g * P:(g + 1) * P], xnT[:, k], start=(k == 0),
                              stop=(k == KC - 1))
                last.then_inc(pe_q, 1)

            def project_k(n, g):
                for k in range(KC):
                    last = mm(bank[1][:, 0:S], wk[:, k, g * P:(g + 1) * P], xnT[:, k], start=(k == 0),
                              stop=(k == KC - 1))
                last.then_inc(pe_k, 1)

            def project_kn(b):
                for k in range(KC):
                    last = mm(bank[1][0:NKEY, :], xkT[:, k], wk[:, k], start=(k == 0), stop=(k == KC - 1))
                last.then_inc(pe_kn, 1)

            def turn_k(b):
                pe.wait_ge(k_rope, b + 1)
                for g in range(G):
                    last = tr(bank[2][:, g * NKEY:(g + 1) * NKEY], krope[0:NKEY, g * P:(g + 1) * P],
                              ident[0:NKEY, 0:NKEY])
                last.then_inc(pe_k, 1)

            def project_v(n, g):
                c = slice(g * P, (g + 1) * P)
                for t in range(1 if A else TB):
                    out = bank[1][0:NKEY, 0:P] if A else bank[1][:, t * P:(t + 1) * P]
                    for k in range(KC):
                        lhs = xkT[:, k] if A else xnT[:, k, t * P:(t + 1) * P]
                        last = mm(out, lhs, wv[:, k, c], start=(k == 0), stop=(k == KC - 1))
                last.then_inc(pe_v, 1)

            def scores(n, g):
                if A:
                    for t in range(TB):
                        last = mm(ps_s[:, t, 0:4 * NKEY], qT[:, g, t * P:(t + 1) * P],
                                  kD[:, g].rearrange("p j k -> p (j k)"), start=True, stop=True)
                else:
                    mm(ps_s[:, 0, :], qT[:, g, 0:P], kD[:, g, :, 0:P], start=True, stop=True)
                    for jj in range(2):
                        last = mm(ps_s[:, 1 + jj, :], qT[:, g, P:2 * P],
                                  kD[:, g, 2 * jj:2 * jj + 2].rearrange("p j k -> p (j k)"), start=True, stop=True)
                last.then_inc(pe_s, 1)

            def turn_probs(n, g):
                pe.wait_ge(scaled, n + 1)
                pr = prob[:, g % 2]
                for j in range(4):
                    pt = ps_t[:, j // 2, (j % 2) * S:(j % 2) * S + S]
                    last = tr(pt[:, 0:P], pr[:, j, 0:P], ident[:])
                    last = tr(pt[:, P:2 * P], pr[:, j, P:2 * P], ident[:])
                    if not A:
                        last = tr(bank[2][:, j * P:(j + 1) * P], pr[:, j, 2 * P:3 * P], ident[:])
                last.then_inc(pe_t, 1)

            def apply_probs(n, g):
                pe.wait_ge(pT_dve, n + 1)
                pe.wait_ge(pT_act, n + 1)
                for j in range(4):
                    c = slice(g * P + j * HD, g * P + (j + 1) * HD)
                    out = bank[0][32 * j:32 * j + 32]
                    last = mm(out[:, 0:S], v[:, 0, c], probT[:, j], start=True, stop=A, skip_group_check=True)
                    if not A:
                        last = mm(out[:, P:S], v[:, 1, c], probT1[:, j], start=False, stop=True,
                                  skip_group_check=True)
                last.then_inc(pe_pv, 1)

            def project_out(b):
                for t in range(TB):
                    for k in range(KC):
                        last = mm(bank[t][:], oT[:, k, t * P:(t + 1) * P], wo[:, k], start=(k == 0),
                                  stop=(k == KC - 1))
                    last.then_inc(pe_o, 1)

            turn_x(0, xn, normed, pe_xT, xT_copied)
            pe.wait_ge(ld_w, 16 * 4)
            pe.wait_ge(xT_copied, TB)
            if A:
                pe.wait_ge(xk_ready, 1)
                project_kn(0)
                turn_k(0)
            for g in range(3):
                if g:
                    pe.wait_ge(q_copied, g)
                project_q(g, g)
                if A:
                    wait(pe, v_copied, g)
                    if g == 0:
                        pe.wait_ge(kn_copied, 1)
                else:
                    wait(pe, v_copied, g)
                    project_k(g, g)
                    pe.wait_ge(k_dve, g + 1)
                    pe.wait_ge(k_act, g + 1)
                project_v(g, g)

            def slot(b, g, first, last):
                n = 4 * b + g
                begun = not (first and g == 0)
                _, pg, pn = proj_of(b, g)
                project = g == 0 or not last
                if A:
                    pe.wait_ge(q_ready, n + 1)
                    pe.wait_ge(k_dve, b + 1)
                    pe.wait_ge(k_act, b + 1)
                    wait(pe, exped, n)
                else:
                    pe.wait_ge(q_copied, n + 1)
                    wait(pe, maxed, n)
                scores(n, g)
                if begun:
                    turn_probs(n - 1, (g - 1) % 4)
                if project:
                    if g == 1:
                        pe.wait_ge(xT_copied, TB * (b + 2))
                        if not first:
                            pe.wait_ge(x_added, TB * b)
                    wait(pe, pv_copied, n - 1)
                    if not begun:
                        pe.wait_ge(q_copied, pn)
                    if g == 3 and not first:
                        pe.wait_ge(oT_copied, TB * b)
                    project_q(pn, pg)
                    wait(pe, v_copied, pn)
                    if A:
                        if g == 2:
                            pe.wait_ge(kn_copied, b + 2)
                    else:
                        project_k(pn, pg)
                if begun:
                    wait(pe, q_copied, pn + 1 if project else 4 * B)
                    if g == 3 and last:
                        pe.wait_ge(oT_copied, TB * b)
                    if not project:
                        pe.wait_ge(pv_copied, n - 1)
                        if g == 1:
                            pe.wait_ge(x_added, TB * b)
                    apply_probs(n - 1, (g - 1) % 4)
                if project:
                    if A:
                        if g == 1:
                            pe.wait_ge(xk_ready, b + 2)
                    else:
                        pe.wait_ge(k_dve, pn + 1)
                        pe.wait_ge(k_act, pn + 1)
                    project_v(pn, pg)
                if A and g == 1 and not last:
                    pe.wait_ge(v_copied, pn + 1)
                    project_kn(b + 1)
                if A and g == 3 and not last:
                    turn_k(b + 1)
                if g == 0:
                    if not first:
                        pe.wait_ge(pv_copied, n)
                    else:
                        pe.wait_ge(q_copied, pn + 1)
                    pe.wait_ge(v_copied, pn + 1)
                    if not last:
                        turn_x(b + 1, xn, normed, pe_xT, xT_copied)
                    if not first:
                        if not last:
                            pe.wait_ge(xT_copied, TB * (b + 2))
                        project_out(b - 1)
                if g == 2 and not first:
                    pe.wait_ge(pv_copied, n)
                    pe.wait_ge(v_copied, (pn + 1) if project else 4 * B)
                    turn_x(b - 1, xo, onormed, pe_oT, oT_copied)

            def batch(b, first=False, last=False):
                for g in range(G):
                    slot(b, g, first, last)

            batch(0, first=True)
            with pe.Fori(1, B - 1) as b:
                batch(b)
            batch(B - 1, last=True)
            turn_probs(4 * B - 1, 3)
            pe.wait_ge(pv_copied, 4 * B - 1)
            apply_probs(4 * B - 1, 3)
            pe.wait_ge(pv_copied, 4 * B)
            project_out(B - 1)
            turn_x(B - 1, xo, onormed, pe_oT, oT_copied)


def convolution(nc, big, t, kpad):
    with ExitStack() as ctx:
        def sb(name, shape, dt=F32):
            return ctx.enter_context(nc.sbuf_tensor("b_" + name, shape, dt))

        def sem(name):
            return ctx.enter_context(nc.semaphore("b_" + name))

        kz = sb("kz", [CH, P + D])
        dk = sb("dk", [CH, 1])
        toep = sb("toep", [P, 2, D])
        cext = sb("cext", [P, 2, KC, CEXT * B])
        pair = sb("pair", [P, 2, KC, NDEL, CW])
        qx = sb("qx", [P, 2, KC, 11 * B])
        prod = sb("prod", [P, 2, KC, 8, CEXT * B])
        ps = ctx.enter_context(nc.psum_tensor("b_ps", [P, 2, KC, 512], F32))
        loaded, tapped, padded = sem("loaded"), sem("tapped"), sem("padded")
        toep_in = [sem("toep_in0"), sem("toep_in1")]
        cext_in = [sem("cext_in0"), sem("cext_in1")]
        paired, conv, extended = sem("paired"), sem("conv"), sem("extended")
        multiplied, wrapped, reduced, passed = sem("multiplied"), sem("wrapped"), sem("reduced"), sem("passed")
        block = ctx.enter_context(nc.Block())

        def loop(eng, body):
            for u in range(2):
                body(u, u, 0)
            with eng.Fori(1, CH // 2) as m:
                for u in range(2):
                    body(2 * m + u, u, m)

        @block.sync
        def _(sp):
            sp.dma_start(dk[:], t["conv_d"]).then_inc(loaded, 16)
            sp.wait_ge(tapped, 1)
            sp.dma_start(kz[:, P:], t["conv_k"]).then_inc(loaded, 16)
            sp.wait_ge(tapped, 2)
            sp.dma_start(kpad, kz[:]).then_inc(padded, 16)
            sp.wait_ge(padded, 16)

            def head(h, u, m):
                wait(sp, conv, h - 1)
                row = kpad[bass.ds(h, 1), 1:1 + D]
                src = bass.AP(row.tensor, row.offset, [[1, P], [1, D]])
                sp.dma_start(toep[:, u], src).then_inc(toep_in[u], 16)
                wait(sp, paired, h - 1)
                sp.dma_start(cext[:, u], t["ctx_rev"][bass.ds(h, 1)].rearrange("one p k c -> (one p) k c"))\
                    .then_inc(cext_in[u], 16)
            loop(sp, head)

        @block.gpsimd
        def _(pool):
            def pairs(h, u, m):
                pool.wait_ge(cext_in[u], 16 * (m + 1))
                wait(pool, conv, h - 1)
                c = cext[:, u]
                whole = bass.AP(c.tensor, c.offset, [list(c.ap[0]), list(c.ap[1]), [B, NDEL], [1, CW]])
                one = bass.AP(c.tensor, c.offset, [list(c.ap[0]), list(c.ap[1]), [0, NDEL], [1, CW]])
                nc.gpsimd.tensor_tensor(pair[:, u], whole, one, ALU.mult).then_inc(paired, 1)

            def wrap(h, u):
                pool.wait_ge(multiplied, h + 1)
                low = prod[:, u, :, 0:4, 0:4 * B]
                nc.gpsimd.tensor_tensor(low, low, prod[:, u, :, 4:8, CW:CEXT * B], ALU.add).then_inc(wrapped, 1)

            def head(h, u, m):
                pairs(h, u, m)
                if not (isinstance(h, int) and h == 0):
                    wrap(h - 1, 1 - u)
            loop(pool, head)
            wrap(CH - 1, 1)

        @block.scalar
        def _(act):
            def head(h, u, m):
                wait(act, multiplied, h - 1)
                nc.scalar.activation(qx[:, u, :, 0:CW], big[:, :, bass.ds(h * CW, CW)], ACT.Copy)
                nc.scalar.activation(qx[:, u, :, CW:], big[:, :, bass.ds(h * CW, 3 * B)], ACT.Copy)\
                    .then_inc(extended, 1)
            loop(act, head)

        @block.tensor
        def _(pe):
            def head(h, u, m):
                pe.wait_ge(toep_in[u], 16 * (m + 1))
                pe.wait_ge(paired, h + 1)
                wait(pe, multiplied, h - 1)
                for lb in range(KC):
                    for mb in range(lb + 1):
                        last = nc.tensor.matmul(ps[:, u, lb, 0:NDEL * CW], toep[:, u, (lb - mb) * P:(lb - mb + 1) * P],
                                                pair[:, u, mb].rearrange("p d c -> p (d c)"),
                                                start=(mb == 0), stop=(mb == lb))
                last.then_inc(conv, 1)
            loop(pe, head)

        @block.vector
        def _(dve):
            nc.vector.memset(kz[:], 0.0).then_inc(tapped, 1)
            dve.wait_ge(loaded, 32)
            dve.wait_ge(tapped, 1)
            nc.vector.tensor_tensor(kz[:, P:P + 1], kz[:, P:P + 1], dk[:], ALU.add).then_inc(tapped, 1)
            nc.vector.memset(prod[:], 0.0).then_inc(tapped, 1)
            dve.wait_ge(tapped, 3)

            def multiply(h, u):
                dve.wait_ge(conv, h + 1)
                dve.wait_ge(extended, h + 1)
                wait(dve, reduced, h - 1)
                y = ps[:, u, :, 0:NDEL * CW].rearrange("p k (d c) -> p k d c", d=NDEL)
                q, f = qx[:, u], prod[:, u]
                qs, fs = list(q.ap[1]), list(f.ap[1])
                one = bass.AP(q.tensor, q.offset, [list(q.ap[0]), qs, [0, NDEL], [1, CW]])
                to = bass.AP(f.tensor, f.offset + 3 * CEXT * B, [list(f.ap[0]), fs, [CEXT * B + B, NDEL], [1, CW]])
                nc.vector.tensor_tensor(to, y, one, ALU.mult)
                other = bass.AP(q.tensor, q.offset + B, [list(q.ap[0]), qs, [B, 3], [1, CW]])
                nc.vector.tensor_tensor(f[:, :, 0:3, 0:CW], y[:, :, 1:4], other, ALU.mult)\
                    .then_inc(multiplied, 1)

            def reduce(h, u):
                wait_apart(dve, wrapped, h + 1, passed)
                nc.vector.tensor_reduce(big[:, :, bass.ds(h * CW, CW)],
                                        prod[:, u, :, :, 0:CW].rearrange("p k r c -> p k c r"),
                                        AX.X, ALU.add).then_inc(reduced, 1)

            def head(h, u, m):
                multiply(h, u)
                if not (isinstance(h, int) and h == 0):
                    reduce(h - 1, 1 - u)
            loop(dve, head)
            reduce(CH - 1, 1)


def router(nc, x_sb, big, ident, t):
    R = 4
    NG = 3 * VCH
    with ExitStack() as ctx:
        def sb(name, shape, dt=F32):
            return ctx.enter_context(nc.sbuf_tensor("c_" + name, shape, dt))

        def sem(name):
            return ctx.enter_context(nc.semaphore("c_" + name))

        wg = sb("wg", [P, KC, NG])
        gb = sb("gb", [P, NG])
        yT = sb("yT", [P, 2, KC, P])
        xn = sb("xn", [P, R, D])
        xnT = sb("xnT", [P, 2, KC, P])
        sc = sb("sc", [P, 2, NG])
        top = sb("top", [P, 2, 8])
        ix = sb("ix", [P, R, 8], U32)
        st, mv = sb("st", [P, 2, 6]), sb("mv", [P, 2, 2])
        ve, rstd, mhalf = sb("ve", [P, 2]), sb("rstd", [P, 2]), sb("mhalf", [P, 1])
        ps = ctx.enter_context(nc.psum_tensor("c_ps", [P, 2, 3, 512], F32))
        ps_y = ctx.enter_context(nc.psum_tensor("c_ps_y", [P, 512], F32))
        ps_x = ctx.enter_context(nc.psum_tensor("c_ps_x", [P, 512], F32))
        ld, y_cut, pe_y, added = sem("ld"), sem("y_cut"), sem("pe_y"), sem("added")
        stats, aggr, lnvar, lnrstd, normed = sem("stats"), sem("aggr"), sem("lnvar"), sem("lnrstd"), sem("normed")
        pe_x, xT_copied, scored = sem("pe_x"), sem("xT_copied"), sem("scored")
        biased, maxed, found, chosen = sem("biased"), sem("maxed"), sem("found"), sem("chosen")
        gathered = [sem(f"gathered{i}") for i in range(R)]
        setup, passed, passed_pool = sem("setup"), sem("passed"), sem("passed_pool")
        block = ctx.enter_context(nc.Block())

        def loop(eng, body):
            M = TILES // R
            for u in range(R):
                body(u, u, 0, True, False)
            with eng.Fori(1, M - 1) as m:
                for u in range(R):
                    body(R * m + u, u, m, False, False)
            for u in range(R):
                body(R * (M - 1) + u, u, M - 1, False, True)

        def x_tile(n):
            return x_sb[:, bass.ds(n * D, D)]

        @block.sync
        def _(sp):
            sp.dma_start(wg[:], t["gate_w"]).then_inc(ld, 16)
            sp.dma_start(gb[:], t["gate_b"].rearrange("(one g) -> one g", one=1).broadcast_to([P, NG]))\
                .then_inc(ld, 16)

        @block.scalar
        def _(act):
            def cut(n, u, m):
                wait(act, pe_y, n - 1)
                b = m * (R // TB) + u // TB
                src = big[:].rearrange("p k (q b) -> p k q b", b=B)[:, :, (u % TB) * P:(u % TB + 1) * P, bass.ds(b, 1)]
                nc.scalar.activation(yT[:, u % 2].rearrange("p k (q one) -> p k q one", one=1), src, ACT.Copy)\
                    .then_inc(y_cut, 1)

            def turned(n, u):
                act.wait_ge(pe_x, n + 1)
                wait(act, scored, n - 1)
                nc.scalar.activation(xnT[:, u % 2], ps_x[:].rearrange("p (k q) -> p k q", k=KC), ACT.Copy)\
                    .then_inc(xT_copied, 1)

            cut(0, 0, 0)
            cut(1, 1, 0)
            turned(0, 0)

            def tile(n, u, m, first, last):
                if not (last and u >= R - 2):
                    cut(n + 2, (u + 2) % R, m + (u + 2) // R)
                if not (last and u >= R - 1):
                    turned(n + 1, (u + 1) % R)
            loop(act, tile)

        @block.tensor
        def _(pe):
            def turn_y(n, u):
                pe.wait_ge(y_cut, n + 1)
                wait(pe, added, n)
                for k in range(KC):
                    last = nc.tensor.transpose(ps_y[:, k * P:(k + 1) * P], yT[:, u % 2, k], ident[:])
                last.then_inc(pe_y, 1)

            def turn_x(n, u):
                pe.wait_ge(normed, n + 1)
                wait(pe, xT_copied, n)
                for k in range(KC):
                    last = nc.tensor.transpose(ps_x[:, k * P:(k + 1) * P], xn[:, u, k * P:(k + 1) * P], ident[:])
                last.then_inc(pe_x, 1)

            def scores(n, u):
                pe.wait_ge(xT_copied, n + 1)
                wait(pe, biased, n - 1)
                for c in range(3):
                    for k in range(KC):
                        last = nc.tensor.matmul(ps[:, u % 2, c, 0:VCH], xnT[:, u % 2, k],
                                                wg[:, k, c * VCH:(c + 1) * VCH], start=(k == 0), stop=(k == KC - 1))
                last.then_inc(scored, 1)

            turn_y(0, 0)
            turn_y(1, 1)
            turn_x(0, 0)
            pe.wait_ge(ld, 32)

            def tile(n, u, m, first, last):
                if not (last and u >= R - 2):
                    turn_y(n + 2, (u + 2) % R)
                scores(n, u)
                if not (last and u >= R - 1):
                    turn_x(n + 1, (u + 1) % R)
            loop(pe, tile)

        @block.gpsimd
        def _(pool):
            def rstd_of(n, u):
                wait_apart(pool, aggr, n + 1, passed_pool)
                nc.gpsimd.tensor_scalar(ve[:, u % 2:u % 2 + 1], mv[:, u % 2, 1:2], LN_EPS, None, ALU.add)\
                    .then_inc(lnvar, 1)
                pool.wait_ge(lnvar, n + 1)
                nc.gpsimd.tensor_tensor(rstd[:, u % 2:u % 2 + 1], ve[:, u % 2:u % 2 + 1], mhalf[:], ALU.pow)\
                    .then_inc(lnrstd, 1)

            def gather(n, u):
                wait_apart(pool, found, n + 1, passed_pool)
                wait_apart(pool, pe_x, n + 1, passed_pool)
                nc.gpsimd.indirect_dma_start(
                    xn[:, u], None, t["pool"], bass.IndirectOffsetOnAxis(ap=ix[:, u, 0:1], axis=0),
                    bounds_check=NV - 1, oob_is_err=False).then_inc(gathered[u], 16)

            def add(n, u, m):
                pool.wait_ge(gathered[u], 16 * (m + 1))
                nc.gpsimd.tensor_tensor(x_tile(n), x_tile(n), xn[:, u], ALU.add).then_inc(chosen, 1)

            nc.gpsimd.memset(mhalf[:], -0.5).then_inc(setup, 1)
            pool.wait_ge(setup, 1)
            rstd_of(0, 0)
            rstd_of(1, 1)

            def tile(n, u, m, first, last):
                if not (first and u == 0):
                    add(n - 1, (u - 1) % R, m if u else m - 1)
                gather(n, u)
                if not (last and u >= R - 2):
                    rstd_of(n + 2, (u + 2) % R)
            loop(pool, tile)
            add(TILES - 1, R - 1, TILES // R - 1)

        @block.vector
        def _(dve):
            def norm(n, u, m):
                dve.wait_ge(pe_y, n + 1)
                nc.vector.tensor_tensor(x_tile(n), x_tile(n), ps_y[:], ALU.add).then_inc(added, 1)
                wait_apart(dve, added, n + 1, passed)
                nc.vector.bn_stats(st[:, u % 2], x_tile(n)).then_inc(stats, 1)
                wait_apart(dve, stats, n + 1, passed)
                nc.vector.bn_aggr(mv[:, u % 2], st[:, u % 2]).then_inc(aggr, 1)
                dve.wait_ge(lnrstd, n + 1)
                wait(dve, chosen, n - R + 1)
                nc.vector.tensor_scalar(xn[:, u], x_tile(n), mv[:, u % 2, 0:1], rstd[:, u % 2:u % 2 + 1],
                                        ALU.subtract, ALU.mult).then_inc(normed, 1)

            def best(n, u):
                dve.wait_ge(scored, n + 1)
                s = sc[:, u % 2]
                nc.vector.tensor_tensor(s.rearrange("p (c g) -> p c g", c=3), ps[:, u % 2, :, 0:VCH],
                                        gb[:].rearrange("p (c g) -> p c g", c=3), ALU.add).then_inc(biased, 1)
                wait_apart(dve, biased, n + 1, passed)
                nc.vector.max(top[:, u % 2], s).then_inc(maxed, 1)
                wait_apart(dve, maxed, n + 1, passed)
                nc.vector.max_index(ix[:, u], top[:, u % 2], s).then_inc(found, 1)

            norm(0, 0, 0)
            norm(1, 1, 0)
            dve.wait_ge(ld, 32)

            def tile(n, u, m, first, last):
                best(n, u)
                if not (last and u >= R - 2):
                    norm(n + 2, (u + 2) % R, m)
            loop(dve, tile)


def retention(nc, x_sb, big, ident, t, o_sb, wgate, wout):
    CHUNK = 512
    NCH = TOK // CHUNK
    with ExitStack() as ctx:
        def sb(name, shape, dt=F32):
            return ctx.enter_context(nc.sbuf_tensor("e_" + name, shape, dt))

        def sem(name):
            return ctx.enter_context(nc.semaphore("e_" + name))

        wh = sb("wh", [P, 2, RD])
        cT = sb("cT", [P, 2, TOK])
        decay = sb("decay", [P, 2, TB, S])
        qT, kT = sb("qT", [P, TOK]), sb("kT", [P, TOK])
        v = sb("v", [P, TILES, RD])
        raw, a = sb("raw", [P, TB, S]), sb("a", [P, TB, S])
        ps_p = [ctx.enter_context(nc.psum_tensor(f"e_ps_p{i}", [P, CHUNK], F32)) for i in range(2)]
        ps_v = [ctx.enter_context(nc.psum_tensor(f"e_ps_v{i}", [P, CHUNK], F32)) for i in range(2)]
        ps_s = ctx.enter_context(nc.psum_tensor("e_ps_s", [P, TB, S], F32))
        ps_o = [ctx.enter_context(nc.psum_tensor(f"e_ps_o{i}", [P, CHUNK], F32)) for i in range(2)]
        w_in = sem("w_in")
        in_ = [sem("in0"), sem("in1")]
        pe_q, pe_k, pe_v, pe_s, pe_o = sem("pe_q"), sem("pe_k"), sem("pe_v"), sem("pe_s"), sem("pe_o")
        q_copied, k_copied, v_copied = sem("q_copied"), sem("k_copied"), sem("v_copied")
        decayed, negated, clamped, o_copied = sem("decayed"), sem("negated"), sem("clamped"), sem("o_copied")
        block = ctx.enter_context(nc.Block())

        def loop(eng, body):
            for h in range(RH):
                body(h, h % 2, h // 2, h == 0, h == RH - 1)

        @block.sync
        def _(sp):
            def head(h, u, m, first, last):
                wait(sp, pe_v, NCH * (h - 1))
                wait(sp, decayed, h - 1)
                sp.dma_start(wh[:, u], t["wh"][h]).then_inc(in_[u], 16)
                sp.dma_start(cT[:, u], t["ctxT"][h]).then_inc(in_[u], 16)
                sp.dma_start(decay[:, u], t["decay"][h]).then_inc(in_[u], 16)
                if first:
                    sp.dma_start(wgate[:], t["wgate"]).then_inc(w_in, 16)
                    sp.dma_start(wout[:], t["wout"]).then_inc(w_in, 16)
            loop(sp, head)
            sp.wait_ge(w_in, 32)

        @block.tensor
        def _(pe):
            mm = nc.tensor.matmul

            def queries(h, u, m, first, last):
                pe.wait_ge(in_[u], 48 * (m + 1))
                for c in range(NCH):
                    i = NCH * h + c
                    wait(pe, k_copied, NCH * h - 1 + c) if c < 2 else pe.wait_ge(q_copied, i - 1)
                    mm(ps_p[c % 2][:], wh[:, u], big[:, h, c * CHUNK:(c + 1) * CHUNK], start=True, stop=True)\
                        .then_inc(pe_q, 1)

            def keys(h, u):
                for c in range(NCH):
                    i = NCH * h + c
                    pe.wait_ge(q_copied, NCH * h + NCH - 1 + c) if c < 2 else pe.wait_ge(k_copied, i - 1)
                    mm(ps_p[c % 2][:], wh[:, u], cT[:, u, c * CHUNK:(c + 1) * CHUNK], start=True, stop=True)\
                        .then_inc(pe_k, 1)

            def values(h, u):
                for c in range(NCH):
                    wait(pe, v_copied, NCH * h + c - 1)
                    for i in range(4):
                        last = mm(ps_v[c % 2][:, i * P:(i + 1) * P], cT[:, u, (4 * c + i) * P:(4 * c + i + 1) * P],
                                  wh[:, u], start=True, stop=True)
                    last.then_inc(pe_v, 1)

            def scores(h):
                pe.wait_ge(q_copied, NCH * (h + 1))
                pe.wait_ge(k_copied, NCH * (h + 1))
                wait(pe, decayed, h)
                for tt in range(TB):
                    for b in range(B):
                        last = mm(ps_s[:, tt], kT[:, b * S + tt * P:b * S + (tt + 1) * P], qT[:, b * S:(b + 1) * S],
                                  start=(b == 0), stop=(b == B - 1))
                last.then_inc(pe_s, 1)

            def outputs(h):
                pe.wait_ge(clamped, h + 1)
                pe.wait_ge(v_copied, NCH * (h + 1))
                for ss in range(TB):
                    for half in range(2):
                        wait(pe, o_copied, NCH * h + 2 * ss + half - 1)
                        vs = v[:].rearrange("p (b t) e -> p b t e", t=TB)
                        for tt in range(TB):
                            last = mm(ps_o[half][:], a[:, tt, ss * P:(ss + 1) * P],
                                      vs[:, 4 * half:4 * half + 4, tt, :], start=(tt == 0), stop=(tt == TB - 1))
                        last.then_inc(pe_o, 1)

            def head(h, u, m, first, last):
                if first:
                    queries(h, u, m, first, last)
                keys(h, u)
                if not first:
                    outputs(h - 1)
                values(h, u)
                scores(h)
                if not last:
                    queries(h + 1, 1 - u, m + u, first, last)
                else:
                    outputs(h)
            loop(pe, head)

        @block.scalar
        def _(act):
            def head(h, u, m, first, last):
                for c in range(NCH):
                    i = NCH * h + c
                    act.wait_ge(pe_q, i + 1)
                    wait(act, pe_s, h)
                    nc.scalar.activation(qT[:, c * CHUNK:(c + 1) * CHUNK], ps_p[c % 2][:], ACT.Copy)\
                        .then_inc(q_copied, 1)
                for c in range(NCH):
                    i = NCH * h + c
                    act.wait_ge(pe_v, i + 1)
                    wait(act, pe_o, NCH * h)
                    nc.scalar.activation(v[:, 4 * c:4 * c + 4], ps_v[c % 2][:].rearrange("p (t e) -> p t e", t=4),
                                         ACT.Copy).then_inc(v_copied, 1)
            loop(act, head)

        @block.vector
        def _(dve):
            def outputs(h):
                for ss in range(TB):
                    for half in range(2):
                        dve.wait_ge(pe_o, NCH * h + 2 * ss + half + 1)
                        o4 = o_sb[:].rearrange("p (b t) f -> p b t f", t=TB)
                        nc.vector.tensor_copy(o4[:, 4 * half:4 * half + 4, ss, h * RD:(h + 1) * RD],
                                              ps_o[half][:].rearrange("p (b e) -> p b e", b=4)).then_inc(o_copied, 1)

            def head(h, u, m, first, last):
                for c in range(NCH):
                    dve.wait_ge(pe_k, NCH * h + c + 1)
                    wait(dve, pe_s, h)
                    nc.vector.tensor_copy(kT[:, c * CHUNK:(c + 1) * CHUNK], ps_p[c % 2][:]).then_inc(k_copied, 1)
                if not first:
                    outputs(h - 1)
                dve.wait_ge(pe_s, h + 1)
                wait(dve, clamped, h)
                nc.vector.tensor_tensor(raw[:], ps_s[:], decay[:, u], ALU.mult).then_inc(decayed, 1)
                dve.wait_ge(decayed, h + 1)
                wait(dve, pe_o, NCH * h)
                nc.vector.tensor_scalar(a[:], raw[:], -1.0, 1.0, ALU.mult, ALU.max).then_inc(negated, 1)
                dve.wait_ge(negated, h + 1)
                nc.vector.tensor_tensor(a[:], a[:], raw[:], ALU.max).then_inc(clamped, 1)
            loop(dve, head)
            outputs(RH - 1)


def mixing(nc, x_sb, big, ident, t, o_sb, wgate, wout, logitT, xn_rows):
    with ExitStack() as ctx:
        def sb(name, shape, dt=F32):
            return ctx.enter_context(nc.sbuf_tensor("f_" + name, shape, dt))

        def sem(name):
            return ctx.enter_context(nc.semaphore("f_" + name))

        gamma, beta = sb("gamma", [P, KC]), sb("beta", [P, KC])
        wr, br = sb("wr", [P, KC, NE]), sb("br", [P, 1])
        on = sb("on", [P, 2, D])
        w = sb("w", [P, 2, KC, P])
        y = sb("y", [P, 2, KC, P])
        wy = sb("wy", [P, 2, KC, P])
        xf = sb("xf", [P, 2, D])
        xfT = sb("xfT", [P, 2, KC, P])
        st, mv = sb("st", [P, 2, 2, 6]), sb("mv", [P, 2, 2, 2])
        ve, rstd, mhalf = sb("ve", [P, 2, 2]), sb("rstd", [P, 2, 2]), sb("mhalf", [P, 1])
        ps = [ctx.enter_context(nc.psum_tensor(f"f_ps{i}", [P, 512], F32)) for i in range(5)]
        ps_y, ps_w, ps_o, ps_x, ps_l = ps
        ld, setup = sem("ld"), sem("setup")
        ostats, oaggr, ovar, orstd, onormed = (sem(n) for n in ("ostats", "oaggr", "ovar", "orstd", "onormed"))
        xstats, xaggr, xvar, xrstd, xnormed = (sem(n) for n in ("xstats", "xaggr", "xvar", "xrstd", "xnormed"))
        pe_y, pe_w, pe_o, pe_x, pe_l = (sem(n) for n in ("pe_y", "pe_w", "pe_o", "pe_x", "pe_l"))
        relued, scaled, gated, added = sem("relued"), sem("scaled"), sem("gated"), sem("added")
        xT_copied, l_copied, passed, passed_pool = (sem(n) for n in ("xT_copied", "l_copied", "passed",
                                                                    "passed_pool"))
        stored = [sem("stored0"), sem("stored1")]
        block = ctx.enter_context(nc.Block())

        def loop(eng, body):
            M = TILES // 2
            for u in range(2):
                body(u, u, 0, True, False)
            with eng.Fori(1, M - 1) as m:
                for u in range(2):
                    body(2 * m + u, u, m, False, False)
            for u in range(2):
                body(2 * (M - 1) + u, u, M - 1, False, True)

        def tile_of(s, n):
            return s[:, bass.ds(n * D, D)]

        o2 = o_sb[:].rearrange("p n d -> p (n d)")

        @block.sync
        def _(sp):
            sp.dma_start(gamma[:], t["gn_gamma"]).then_inc(ld, 16)
            sp.dma_start(beta[:], t["gn_beta"]).then_inc(ld, 16)
            sp.dma_start(wr[:], t["wr"]).then_inc(ld, 16)
            sp.dma_start(br[0:NE], t["br"]).then_inc(ld, 16)

            def tile(n, u, m, first, last):
                sp.wait_ge(xnormed, n + 1)
                sp.dma_start(xn_rows[bass.ds(n * P, P), :], xf[:, u]).then_inc(stored[u], 16)
            loop(sp, tile)
            for i in range(2):
                sp.wait_ge(stored[i], 16 * (TILES // 2))

        @block.gpsimd
        def _(pool):
            def rstd_of(n, u, i, eps, got, var, done):
                wait_apart(pool, got, n + 1, passed_pool)
                nc.gpsimd.tensor_scalar(ve[:, i, u:u + 1], mv[:, i, u, 1:2], eps, None, ALU.add).then_inc(var, 1)
                pool.wait_ge(var, n + 1)
                nc.gpsimd.tensor_tensor(rstd[:, i, u:u + 1], ve[:, i, u:u + 1], mhalf[:], ALU.pow).then_inc(done, 1)

            nc.gpsimd.memset(mhalf[:], -0.5).then_inc(setup, 1)
            pool.wait_ge(setup, 1)
            rstd_of(0, 0, 0, GN_EPS, oaggr, ovar, orstd)

            def tile(n, u, m, first, last):
                if not (last and u == 1):
                    rstd_of(n + 1, 1 - u, 0, GN_EPS, oaggr, ovar, orstd)
                rstd_of(n, u, 1, LN_EPS, xaggr, xvar, xrstd)
            loop(pool, tile)

        @block.vector
        def _(dve):
            def stats(src, n, u, i, got, agg):
                nc.vector.bn_stats(st[:, i, u], tile_of(src, n)).then_inc(got, 1)
                wait_apart(dve, got, n + 1, passed)
                nc.vector.bn_aggr(mv[:, i, u], st[:, i, u]).then_inc(agg, 1)

            def apply(src, n, u, i, out, ready, done):
                dve.wait_ge(ready, n + 1)
                nc.vector.tensor_scalar(out[:, u], tile_of(src, n), mv[:, i, u, 0:1], rstd[:, i, u:u + 1],
                                        ALU.subtract, ALU.mult).then_inc(done, 1)

            def norm_o(n, u):
                stats(o2, n, u, 0, ostats, oaggr)
                wait(dve, pe_y, n - 1)
                apply(o2, n, u, 0, on, orstd, onormed)

            def gate(n, u):
                dve.wait_ge(scaled, n + 1)
                dve.wait_ge(relued, n + 1)
                wait(dve, pe_o, n - 1)
                nc.vector.tensor_tensor(wy[:, u], y[:, u], w[:, u], ALU.mult).then_inc(gated, 1)

            def norm_x(n, u, m):
                dve.wait_ge(pe_o, n + 1)
                nc.vector.tensor_tensor(tile_of(x_sb, n), tile_of(x_sb, n), ps_o[:], ALU.add).then_inc(added, 1)
                wait_apart(dve, added, n + 1, passed)
                stats(x_sb, n, u, 1, xstats, xaggr)
                wait(dve, pe_x, n - 1)
                wait(dve, stored[u], 16 * m)
                apply(x_sb, n, u, 1, xf, xrstd, xnormed)

            norm_o(0, 0)

            def tile(n, u, m, first, last):
                gate(n, u)
                if not (last and u == 1):
                    norm_o(n + 1, 1 - u)
                norm_x(n, u, m)
            loop(dve, tile)

        @block.scalar
        def _(act):
            act.wait_ge(ld, 64)

            def gates(n, u):
                act.wait_ge(pe_y, n + 1)
                wait(act, gated, n - 1)
                for k in range(KC):
                    last = nc.scalar.activation(y[:, u, k], ps_y[:, k * P:(k + 1) * P], ACT.Identity,
                                                bias=beta[:, k:k + 1], scale=gamma[:, k:k + 1])
                last.then_inc(scaled, 1)
                act.wait_ge(pe_w, n + 1)
                nc.scalar.activation(w[:, u], ps_w[:].rearrange("p (k q) -> p k q", k=KC), ACT.Relu)\
                    .then_inc(relued, 1)

            def turned(n, u):
                act.wait_ge(pe_x, n + 1)
                wait(act, pe_l, n - 1)
                nc.scalar.activation(xfT[:, u], ps_x[:].rearrange("p (k q) -> p k q", k=KC), ACT.Copy)\
                    .then_inc(xT_copied, 1)

            def logits(n, u):
                act.wait_ge(pe_l, n + 1)
                nc.scalar.activation(logitT[0:NE, bass.ds(n * P, P)], ps_l[0:NE, 0:P], ACT.Identity,
                                     bias=br[0:NE, 0:1]).then_inc(l_copied, 1)

            gates(0, 0)

            def tile(n, u, m, first, last):
                if not (last and u == 1):
                    gates(n + 1, 1 - u)
                if not (first and u == 0):
                    logits(n - 1, 1 - u)
                turned(n, u)
            loop(act, tile)
            logits(TILES - 1, 1)

        @block.tensor
        def _(pe):
            mm, tr = nc.tensor.matmul, nc.tensor.transpose

            def gates(n, u):
                pe.wait_ge(onormed, n + 1)
                wait(pe, scaled, n)
                for k in range(KC):
                    last = tr(ps_y[:, k * P:(k + 1) * P], on[:, u, k * P:(k + 1) * P], ident[:])
                last.then_inc(pe_y, 1)
                wait(pe, relued, n)
                for e in range(KC):
                    for k in range(KC):
                        last = mm(ps_w[:, e * P:(e + 1) * P], wgate[:, k, e * P:(e + 1) * P],
                                  big[:, k, bass.ds(n * P, P)], start=(k == 0), stop=(k == KC - 1))
                last.then_inc(pe_w, 1)

            def project(n, u):
                pe.wait_ge(gated, n + 1)
                wait(pe, added, n)
                for k in range(KC):
                    last = mm(ps_o[:], wy[:, u, k], wout[:, k], start=(k == 0), stop=(k == KC - 1))
                last.then_inc(pe_o, 1)

            def turn_x(n, u):
                pe.wait_ge(xnormed, n + 1)
                wait(pe, xT_copied, n)
                for k in range(KC):
                    last = tr(ps_x[:, k * P:(k + 1) * P], xf[:, u, k * P:(k + 1) * P], ident[:])
                last.then_inc(pe_x, 1)

            def logits(n, u):
                pe.wait_ge(xT_copied, n + 1)
                wait(pe, l_copied, n)
                for k in range(KC):
                    last = mm(ps_l[0:NE, 0:P], wr[:, k], xfT[:, u, k], start=(k == 0), stop=(k == KC - 1))
                last.then_inc(pe_l, 1)

            pe.wait_ge(ld, 64)
            gates(0, 0)

            def tile(n, u, m, first, last):
                if not (first and u == 0):
                    turn_x(n - 1, 1 - u)
                project(n, u)
                if not (first and u == 0):
                    logits(n - 1, 1 - u)
                if not (last and u == 1):
                    gates(n + 1, 1 - u)
            loop(pe, tile)
            turn_x(TILES - 1, 1)
            logits(TILES - 1, 1)


def experts(nc, x_sb, ident, t, logitT, xn_rows, order_rows, out):
    R = 4
    with ExitStack() as ctx:
        def sb(name, shape, dt=F32):
            return ctx.enter_context(nc.sbuf_tensor("g_" + name, shape, dt))

        def sem(name):
            return ctx.enter_context(nc.semaphore("g_" + name))

        we, be = sb("we", [P, KC, D]), sb("be", [P, D])
        before, later = sb("before", [P, P]), sb("later", [P, P])
        iota, ids, ones = sb("iota", [P, TILES, NE]), sb("ids", [P, TILES]), sb("ones", [P, P])
        lg, ex, pr = (sb(n, [P, TILES, NE]) for n in ("lg", "ex", "pr"))
        far, place, hot, ranks = (sb(n, [P, TILES, NE]) for n in ("far", "place", "hot", "ranks"))
        m1, sm, ri, best, first_, rank = (sb(n, [P, TILES]) for n in ("m1", "sm", "ri", "best", "first", "rank"))
        rank_i = sb("rank_i", [P, TILES], U32)
        total = sb("total", [P, 1])
        totals = sb("totals", [P, P])
        ord_t = sb("ord_t", [TILES, P])
        order = sb("order", [P, TILES], U32)
        xs = sb("xs", [P, R, D])
        xsT = sb("xsT", [P, 2, KC, P])
        eo = sb("eo", [P, 2, D])
        ps = [ctx.enter_context(nc.psum_tensor(f"g_ps{i}", [P, 512], F32)) for i in range(8)]
        ps_l, ps_r, ps_t, ps_d = ps[0], ps[1], ps[2], ps[3]
        ps_x, ps_e = ps[4:6], ps[6:8]
        ld, dv, pe_s, ac = sem("ld"), sem("dv"), sem("pe_s"), sem("ac")
        sent, order_in, pl = sem("sent"), sem("order_in"), sem("pl")
        fetched = [sem(f"fetched{i}") for i in range(R)]
        pe_x, xT_copied, pe_e = sem("pe_x"), sem("xT_copied"), sem("pe_e")
        biased, mixed, passed_pool, passed = sem("biased"), sem("mixed"), sem("passed_pool"), sem("passed")
        outs = sem("outs")
        block = ctx.enter_context(nc.Block())

        def loop(eng, body):
            for u in range(R):
                body(u, u, 0)
            with eng.Fori(1, TILES // R) as m:
                for u in range(R):
                    body(R * m + u, u, m)

        def x_tile(n):
            return x_sb[:, bass.ds(n * D, D)]

        @block.sync
        def _(sp):
            for dst, name in ((before[:], "before"), (later[:], "later"), (iota[:], "iota"), (ids[:], "ids"),
                              (we[:], "we")):
                sp.dma_start(dst, t[name]).then_inc(ld, 16)
            sp.dma_start(be[:], t["be"].rearrange("(one d) -> one d", one=1).broadcast_to([P, D])).then_inc(ld, 16)
            sp.wait_ge(sent, 16 * TILES)
            sp.dma_start(ord_t[:], order_rows.rearrange("(n p) one -> n (p one)", p=P)).then_inc(order_in, 16)

            def tile(n, u, m):
                sp.wait_ge(mixed, n + 1)
                sp.dma_start(out[bass.ds(n * P, P), :], x_tile(n)).then_inc(outs, 16)
            loop(sp, tile)
            sp.wait_ge(outs, 16 * TILES)

        @block.tensor
        def _(pe):
            mm, tr = nc.tensor.matmul, nc.tensor.transpose
            for n in range(TILES):
                last = tr(ps_l[:, n * NE:(n + 1) * NE], logitT[0:NE, n * P:(n + 1) * P], ident[0:NE, 0:NE])
            last.then_inc(pe_s, 1)
            pe.wait_ge(dv, 12)
            pe.wait_ge(ld, 96)
            h2 = hot[:].rearrange("p n e -> p (n e)")
            mm(ps_t[:, 0:1], h2, ones[:, 0:1], start=True, stop=True).then_inc(pe_s, 1)
            mm(ps_r[:, 0:P], before[:], h2, start=True, stop=False)
            pe.wait_ge(dv, 14)
            mm(ps_r[:, 0:P], totals[:], later[:], start=False, stop=True).then_inc(pe_s, 1)
            pe.wait_ge(order_in, 16)
            tr(ps_d[:, 0:TILES], ord_t[:], ident[0:TILES, 0:TILES]).then_inc(pe_s, 1)

            def turn(n, u, m):
                pe.wait_ge(fetched[u], 16 * (m + 1))
                wait(pe, xT_copied, n - 1)
                for k in range(KC):
                    last = tr(ps_x[u % 2][:, k * P:(k + 1) * P], xs[:, u, k * P:(k + 1) * P], ident[:])
                last.then_inc(pe_x, 1)

            def expert(n, u):
                pe.wait_ge(xT_copied, n + 1)
                wait(pe, biased, n - 1)
                for k in range(KC):
                    last = mm(ps_e[u % 2][:], xsT[:, u % 2, k], we[:, k], start=(k == 0), stop=(k == KC - 1))
                last.then_inc(pe_e, 1)

            def tile(n, u, m):
                turn(n, u, m)
                if not (isinstance(n, int) and n == 0):
                    expert(n - 1, (u - 1) % R)
            loop(pe, tile)
            expert(TILES - 1, R - 1)

        @block.scalar
        def _(act):
            act.wait_ge(dv, 3)
            nc.scalar.activation(ex[:], lg[:], ACT.Exp).then_inc(ac, 1)

            def tile(n, u, m):
                act.wait_ge(pe_x, n + 1)
                wait(act, pe_e, n - 1)
                nc.scalar.activation(xsT[:, u % 2], ps_x[u % 2][:].rearrange("p (k q) -> p k q", k=KC), ACT.Copy)\
                    .then_inc(xT_copied, 1)
            loop(act, tile)

        @block.gpsimd
        def _(pool):
            pool.wait_ge(dv, 16)
            for n in range(TILES):
                nc.gpsimd.indirect_dma_start(order_rows, bass.IndirectOffsetOnAxis(ap=rank_i[:, n:n + 1], axis=0),
                                             ids[:, n:n + 1], None).then_inc(sent, 16)
            pool.wait_ge(dv, 17)

            for n in range(TILES):
                wait(pool, fetched[n % R], 16 * (n // R))
                wait(pool, pe_x, n - R + 1)
                nc.gpsimd.indirect_dma_start(xs[:, n % R], None, xn_rows,
                                             bass.IndirectOffsetOnAxis(ap=order[:, n:n + 1], axis=0))\
                    .then_inc(fetched[n % R], 16)

        @block.vector
        def _(dve):
            V = nc.vector
            done = [0]

            def step(ins):
                done[0] += 1
                ins.then_inc(dv, 1)
                dve.wait_ge(dv, done[0])

            wide = lambda a: a[:].rearrange("p (n one) -> p n one", one=1).broadcast_to([P, TILES, NE])
            step(V.memset(ones[:], 1.0))
            dve.wait_ge(pe_s, 1)
            dve.wait_ge(ld, 96)
            lp = ps_l[:, 0:TILES * NE].rearrange("p (n e) -> p n e", e=NE)
            step(V.tensor_reduce(m1[:], lp, AX.X, ALU.max))
            step(V.tensor_tensor(lg[:], lp, wide(m1), ALU.subtract))
            dve.wait_ge(ac, 1)
            step(V.tensor_reduce(sm[:], ex[:], AX.X, ALU.add))
            step(V.reciprocal(ri[:], sm[:]))
            step(V.tensor_tensor(pr[:], ex[:], wide(ri), ALU.mult))
            step(V.tensor_reduce(best[:], pr[:], AX.X, ALU.max))
            step(V.tensor_tensor(far[:], pr[:], wide(best), ALU.is_lt))
            step(V.tensor_scalar(far[:], far[:], float(NE), None, ALU.mult))
            step(V.tensor_tensor(place[:], far[:], iota[:], ALU.add))
            step(V.tensor_reduce(first_[:], place[:], AX.X, ALU.min))
            step(V.tensor_tensor(hot[:], iota[:], wide(first_), ALU.is_equal))
            dve.wait_ge(pe_s, 2)
            step(V.tensor_copy(total[:], ps_t[:, 0:1]))
            step(V.tensor_scalar(totals[:], ones[:], total[:, 0:1], None, ALU.mult))
            dve.wait_ge(pe_s, 3)
            step(V.tensor_tensor(ranks[:], hot[:], ps_r[:, 0:P].rearrange("p (n e) -> p n e", e=NE), ALU.mult))
            V.tensor_reduce(rank[:], ranks[:], AX.X, ALU.add).then_inc(passed, 1)
            dve.wait_ge(passed, 1)
            step(V.tensor_copy(rank_i[:], rank[:]))
            dve.wait_ge(pe_s, 4)
            step(V.tensor_copy(order[:], ps_d[:, 0:TILES]))

            def tile(n, u, m):
                dve.wait_ge(pe_e, n + 1)
                wait(dve, mixed, n - 1)
                V.tensor_tensor(eo[:, u % 2], ps_e[u % 2][:], be[:], ALU.add).then_inc(biased, 1)
                dve.wait_ge(biased, n + 1)
                V.scalar_tensor_tensor(out=x_tile(n), in0=eo[:, u % 2], scalar=best[:, bass.ds(n, 1)], in1=x_tile(n),
                                       op0=ALU.mult, op1=ALU.add).then_inc(mixed, 1)
            loop(dve, tile)


def layers(nc, t, out):
    with ExitStack() as ctx:
        def sb(name, shape, dt=F32):
            return ctx.enter_context(nc.sbuf_tensor(name, shape, dt))

        x_sb = sb("x_sb", [P, TILES * D])
        big = sb("big", [P, KC, TOK])
        ident = sb("ident", [P, P])
        started = ctx.enter_context(nc.semaphore("started"))
        with nc.Block() as block:
            @block.sync
            def _(sp):
                sp.dma_start(ident[:], t["identity"]).then_inc(started, 16)
                sp.wait_ge(started, 16)

        a_w = {n: t["a_" + n] for n in ("wq", "wk", "wv", "wo")}
        row = lambda a: a.rearrange("(one d) -> one d", one=1).broadcast_to([P, D])
        a_c = {"bq": t["bq"], "bk": row(t["bk"]), "bv": row(t["bv"]), "bo": row(t["bo"]),
               "qcos": t["qcos"], "qsin": t["qsin"], "kcos": t["kcos"], "ksin": t["ksin"]}
        kpad = nc.dram_tensor("kpad", (CH, P + D), F32).ap()
        attention(nc, True, x_sb, big, ident, a_w, a_c, t["x"])
        used = nc.released_uncleared_semaphores
        with nc.Block() as block:
            @block.gpsimd
            def _(pool):
                pool.sem_clear(range(min(used), max(used) + 1))
        convolution(nc, big, t, kpad)
        router(nc, x_sb, big, ident, t)
        d_w = {n: t["d_" + n] for n in ("wq", "wk", "wv", "wo")}
        attention(nc, False, x_sb, big, ident, d_w, {"rel": t["rel"], "slope": t["slope"]}, None)
        xn_rows = nc.dram_tensor("xn_rows", (TOK, D), F32).ap()
        order_rows = nc.dram_tensor("order_rows", (TOK, 1), F32).ap()
        with nc.sbuf_tensor("logitT", [P, TOK], F32) as logitT:
            with nc.sbuf_tensor("o_sb", [P, TILES, D], F32) as o_sb, \
                    nc.sbuf_tensor("wgate", [P, KC, D], F32) as wgate, \
                    nc.sbuf_tensor("wout", [P, KC, D], F32) as wout:
                retention(nc, x_sb, big, ident, t, o_sb, wgate, wout)
                mixing(nc, x_sb, big, ident, t, o_sb, wgate, wout, logitT, xn_rows)
            experts(nc, x_sb, ident, t, logitT, xn_rows, order_rows, out)


def laid_out(inputs):
    f = lambda n: np.asarray(inputs[n])
    chunks = lambda w: np.ascontiguousarray(w.reshape(KC, P, -1).transpose(1, 0, 2))
    halves = np.concatenate([np.arange(0, HD, 2), np.arange(1, HD, 2)])
    paired = (np.arange(H)[:, None] * HD + halves[None]).reshape(-1)
    a = {"x": f("x").reshape(TOK, D),
         "a_wq": chunks(f("L0_attn_Wq")[paired].T), "a_wk": chunks(f("L0_attn_Wk")[paired].T),
         "a_wv": chunks(f("L0_attn_Wv").T), "a_wo": chunks(f("L0_attn_Wo").T),
         "bq": np.ascontiguousarray(f("L0_attn_bq")[paired].reshape(G, P).T),
         "bk": np.ascontiguousarray(f("L0_attn_bk")[paired]), "bv": f("L0_attn_bv"), "bo": f("L0_attn_bo")}
    for n in "qkvo":
        a["d_w" + n] = chunks(f("L1_attn_W" + n).T)
    ctx = f("ctx_2048")
    rev = ctx.reshape(B, CH, CD, KC, P)[:, :, :, :, ::-1][:, :, np.arange(CEXT) % CD]
    a["ctx_rev"] = np.ascontiguousarray(rev.transpose(1, 4, 3, 2, 0).reshape(CH, P, KC, CEXT * B))
    a["conv_k"], a["conv_d"] = f("L0_xattn_ssm_kernel"), f("L0_xattn_D").reshape(CH, 1)
    a["gate_w"], a["gate_b"] = chunks(f("L0_ffn_gate_w").T), f("L0_ffn_gate_b")
    a["pool"] = np.ascontiguousarray(f("L0_ffn_vector_pool")[:, 16])
    a["wh"] = f("L1_xattn_Wh")
    a["ctxT"] = np.ascontiguousarray(ctx.reshape(TOK, RH, RD).transpose(1, 2, 0))
    a["wgate"], a["wout"] = chunks(f("L1_xattn_wg_w")), chunks(f("L1_xattn_wo_w"))
    a["gn_gamma"] = np.ascontiguousarray(f("L1_xattn_gn_gamma").reshape(KC, P).T)
    a["gn_beta"] = np.ascontiguousarray(f("L1_xattn_gn_beta").reshape(KC, P).T)
    a["wr"], a["br"] = chunks(f("L1_ffn_Wg")), f("L1_ffn_bg").reshape(NE, 1)
    a["we"], a["be"] = chunks(f("L1_ffn_We")), f("L1_ffn_be")
    a.update(shape_constants())
    return a


def shape_constants():
    f32 = np.float32
    theta = f32(1.0) / f32(10000.0) ** (np.arange(0, HD, 2, dtype=f32) / f32(HD))
    angle = np.arange(S, dtype=f32)[:, None] * theta[None]
    cos, sin = np.cos(angle).astype(f32), np.sin(angle).astype(f32)
    cos2, sin2 = np.concatenate([cos, cos], 1), np.concatenate([-sin, sin], 1)
    scale = f32(HD ** -0.5)
    kept = np.concatenate([np.arange(START), np.arange(S - RECENT, S)])
    c = {"qcos": np.tile(cos2.T * scale, (4, 1)), "qsin": np.tile(sin2.T * scale, (4, 1)),
         "kcos": cos2[kept], "ksin": sin2[kept], "identity": np.eye(P, dtype=f32)}
    k, q = np.arange(S)[None, :], np.arange(S)[:, None]
    rel = np.where(k <= q, k - q, -1e30)
    c["rel"] = np.concatenate([rel[0:P, 0:P], rel[P:S]], 1)
    slope = f32(0.5) ** (np.arange(1, H + 1, dtype=f32) * f32(8.0) / f32(H))
    c["slope"] = np.tile(slope[None], (P, 1))
    gam = f32(1.0) - f32(2.0) ** (f32(-5.0) - np.arange(RH, dtype=f32))
    expo = (k - q).astype(f32)
    dm = np.where(expo[None] <= 0, gam[:, None, None] ** expo[None], f32(0))
    dm = dm / np.sqrt(dm.sum(-1, dtype=f32))[:, None, :] / np.sqrt(f32(RD))
    c["decay"] = dm.transpose(0, 2, 1).reshape(RH, TB, P, S).transpose(0, 2, 1, 3)
    i = np.arange(P)
    c["before"] = (i[:, None] < i[None]).astype(f32)
    ne = (i % NE) * TILES + i // NE
    c["later"] = (ne[:, None] < ne[None]).astype(f32)
    c["iota"] = np.broadcast_to(np.arange(NE, dtype=f32), (P, TILES, NE))
    c["ids"] = (np.arange(TILES)[None] * P + i[:, None]).astype(f32)
    return {k: np.ascontiguousarray(a.astype(f32)) for k, a in c.items()}


def kernel(**inputs):
    import concourse.bacc as _bacc
    from concourse.bass_utils import run_bass_kernel_spmd as _run

    nc = _bacc.Bacc("TRN2", target_bir_lowering=False, num_devices=1)
    arrays, t = {}, {}
    for name, a in laid_out(inputs).items():
        arrays[name + "_dram"] = a
        t[name] = nc.dram_tensor(name + "_dram", a.shape, mybir.dt.from_np(a.dtype), kind="ExternalInput").ap()
    out = nc.dram_tensor("out_dram", (TOK, D), F32, kind="ExternalOutput").ap()
    layers(nc, t, out)
    r = _run(nc, [arrays], core_ids=[0])
    return r.results[0]["out_dram"].reshape(B, S, D)
```

```python
from contextlib import ExitStack

import concourse.bass as bass
from concourse import mybir
import numpy as np

P = 128
B, S, D = 8, 256, 512
TOK = B * S
TILES = TOK // P
TB = S // P
KC = D // P
H, HD = 16, 32
G = H // 4
LN_EPS = 1e-5
START = -(-S // 10)
RECENT = -(-S // 4)
NKEY = START + RECENT

CH = 32
CD = S // CH
NDEL = 5
CEXT = 12
CW = CD * B
NV = 1250
VCH = 417
RH, RD = 4, 128
GN_EPS = 1e-3
NE = 8

F32 = mybir.dt.float32
BF16 = mybir.dt.bfloat16
U32 = mybir.dt.uint32
I32 = mybir.dt.int32
ALU = mybir.AluOpType
ACT = mybir.ActivationFunctionType
AX = mybir.AxisListType
SWAP16 = [(i + 16) % 32 for i in range(32)]


def wait(eng, sem, value):
    if isinstance(value, int) and value <= 0:
        return
    eng.wait_ge(sem, value)


def wait_apart(eng, sem, value, passed):
    eng.wait_ge(sem, value)
    eng.sem_inc(passed, 1)


def attention(nc, first_layer, x_sb, big, ident, consts, t, weights, alibi, padded, ahead):
    A = first_layer
    pre = "a_" if A else "d_"
    NQ = NKEY if A else S
    with ExitStack() as ctx:
        def sb(name, shape, dt=F32):
            return ctx.enter_context(nc.sbuf_tensor(pre + name, shape, dt))

        def sem(name):
            return ctx.enter_context(nc.semaphore(pre + name))

        wq, wk, wv, wo = (weights[n][0] for n in ("wq", "wk", "wv", "wo"))
        ld_q, ld_k, ld_v, ld_o = (weights[n][1] for n in ("wq", "wk", "wv", "wo"))
        xn = sb("xn", [P, TB, D])
        xnT = sb("xnT", [P, KC, S])
        qT = sb("qT", [P, G, S])
        kD = sb("kD", [P, G, 4, NQ])
        v = sb("v", [P, 1 if A else TB, D])
        PW = TB * P if A else 3 * P
        prob = sb("prob", [P, 2, 4, PW])
        probT = sb("probT", [P, 4, S])
        probT1 = None if A else sb("probT1", [P, 4, P])
        oT = sb("oT", [P, G, S])
        xo = sb("xo", [P, TB, D])
        nmax = sb("nmax", [P, 2, 8])
        mx = sb("mx", [P, 2, 8])
        rsum = sb("rsum", [P, 2, 8])
        rinv = sb("rinv", [P, 2, 8])
        st = sb("st", [P, 2, TB, 6])
        mv = sb("mv", [P, 2, TB, 2])
        ve = sb("ve", [P, 2, TB])
        rstd = sb("rstd", [P, 2, TB])
        mhalf = sb("mhalf", [P, TB])
        if A:
            xkT = sb("xkT", [P, KC, NKEY])
            bq = sb("bq", [P, G])
            bk, bv, bo = (sb(n, [P, D]) for n in ("bk", "bv", "bo"))
            qcos, qsin = sb("qcos", [P, S]), sb("qsin", [P, S])
            kcos, ksin = sb("kcos", [P, HD]), sb("ksin", [P, HD])
            qraw, qsw, qm1, qm2 = (sb(n, [P, S]) for n in ("qraw", "qsw", "qm1", "qm2"))
            kraw, km1, km2, krope = (sb(n, [P, D]) for n in ("kraw", "km1", "km2", "krope"))
            kz = sb("kz", [CH, P + D])
            dk = sb("dk", [CH, 1])

        bank = [ctx.enter_context(nc.psum_tensor(f"{pre}bank{i}", [P, 512], F32)) for i in range(2 if A else 3)]
        ps_s = ctx.enter_context(nc.psum_tensor(pre + "ps_s", [P, 4 if A else 3, 512], F32))
        ps_t = ctx.enter_context(nc.psum_tensor(pre + "ps_t", [P, 2, 512], F32))

        ld_x0, ld_x, ld_c, ld_b = sem("ld_x0"), sem("ld_x"), sem("ld_c"), sem("ld_b")
        stats, lnvar, lnrstd, normed = sem("stats"), sem("lnvar"), sem("lnrstd"), sem("normed")
        ostats, olnvar, olnrstd, onormed = sem("ostats"), sem("olnvar"), sem("olnrstd"), sem("onormed")
        aggr, oaggr = sem("aggr"), sem("oaggr")
        pe_xT, pe_q, pe_k, pe_v, pe_s = sem("pe_xT"), sem("pe_q"), sem("pe_k"), sem("pe_v"), sem("pe_s")
        pe_t, pe_pv, pe_o, pe_oT = sem("pe_t"), sem("pe_pv"), sem("pe_o"), sem("pe_oT")
        xT_copied, q_copied, q_ready = sem("xT_copied"), sem("q_copied"), sem("q_ready")
        k_act, k_dve, v_copied = sem("k_act"), sem("k_dve"), sem("v_copied")
        maxed, negated, exped, summed, scaled = (sem("maxed"), sem("negated"), sem("exped"),
                                                 sem("summed"), sem("scaled"))
        pT_act, pT_dve, pv_copied = sem("pT_act"), sem("pT_dve"), sem("pv_copied")
        x_added, x_biased, oT_copied = sem("x_added"), sem("x_biased"), sem("oT_copied")
        zeroed, setup = sem("zeroed"), sem("setup")
        passed_dve, passed_pool = sem("passed_dve"), sem("passed_pool")
        if A:
            pe_kn, kn_copied, k_mul, k_rope = sem("pe_kn"), sem("kn_copied"), sem("k_mul"), sem("k_rope")
            q_swap, q_cos, q_sin, xk_ready = sem("q_swap"), sem("q_cos"), sem("q_sin"), sem("xk_ready")
            ld_taps, tapped = sem("ld_taps"), sem("tapped")

        block = ctx.enter_context(nc.Block())

        def xt(b, t):
            return x_sb[:, bass.ds((b * TB + t) * D, D)]

        def proj_of(b, g):
            return (b, g + 2, 4 * b + g + 2) if g < 2 else (b + 1, g - 2, 4 * b + g + 2)

        @block.sync
        def _(sp):
            if A:
                xr = t["x"].rearrange("(t p) d -> p t d", p=P)
                xs = x_sb[:].rearrange("p (t d) -> p t d", d=D)
                sp.dma_start(xs[:, 0:TB], xr[:, 0:TB]).then_inc(ld_x0, 16)
                for n in ("wk", "wq", "wv"):
                    buf, loaded, dram = weights[n]
                    sp.dma_start(buf[:], dram).then_inc(loaded, 16)
                for b in range(1, B):
                    sp.dma_start(xs[:, b * TB:(b + 1) * TB], xr[:, b * TB:(b + 1) * TB]).then_inc(ld_x, 16)
                    if b == 1:
                        buf, loaded, dram = weights["wo"]
                        sp.dma_start(buf[:], dram).then_inc(loaded, 16)
                sp.dma_start(dk[:], t["conv_d"]).then_inc(ld_taps, 16)
                sp.wait_ge(tapped, 1)
                sp.dma_start(kz[:, P:], t["conv_k"]).then_inc(ld_taps, 16)
                sp.wait_ge(tapped, 2)
                sp.dma_start(t["kpad"], kz[:]).then_inc(padded, 16)
                sp.wait_ge(padded, 16)
            if ahead:
                ahead(sp)

        @block.gpsimd
        def _(pool):
            def rstd_of(b, mv_, ve_, rstd_, got, done1, done2):
                wait_apart(pool, got, b + 1, passed_pool)
                nc.gpsimd.tensor_scalar(ve_, mv_[:, :, 1], LN_EPS, None, ALU.add).then_inc(done1, 1)
                pool.wait_ge(done1, b + 1)
                nc.gpsimd.tensor_tensor(rstd_, ve_, mhalf[:], ALU.pow).then_inc(done2, 1)

            def ln_in(b):
                rstd_of(b, mv[:, 0], ve[:, 0], rstd[:, 0], aggr, lnvar, lnrstd)

            def ln_out(b):
                rstd_of(b, mv[:, 1], ve[:, 1], rstd[:, 1], oaggr, olnvar, olnrstd)

            def scale_probs(n, g):
                pool.wait_ge(summed, n + 1)
                pr = prob[:, g % 2]
                iv = rinv[:, g % 2]
                if A:
                    pr = pr.rearrange("p j (t k) -> p j t k", t=TB)[:, :, :, 0:NKEY]
                    iv = iv.rearrange("p (t j one) -> p j t one", t=TB, one=1).broadcast_to([P, 4, TB, NKEY])
                    nc.gpsimd.tensor_tensor(pr, pr, iv, ALU.mult).then_inc(scaled, 1)
                else:
                    i0 = iv[:, 0:4].rearrange("p (j one) -> p j one", one=1).broadcast_to([P, 4, P])
                    i1 = iv[:, 4:8].rearrange("p (j one) -> p j one", one=1).broadcast_to([P, 4, 2 * P])
                    nc.gpsimd.tensor_tensor(pr[:, :, 0:P], pr[:, :, 0:P], i0, ALU.mult)
                    nc.gpsimd.tensor_tensor(pr[:, :, P:], pr[:, :, P:], i1, ALU.mult).then_inc(scaled, 1)

            def q_times_cos(n):
                pool.wait_ge(q_copied, n + 1)
                wait(pool, q_ready, n)
                nc.gpsimd.tensor_tensor(qm1[:], qraw[:], qcos[:], ALU.mult).then_inc(q_cos, 1)

            def kept_keys(b):
                wait_apart(pool, xT_copied, TB * (b + 1), passed_pool)
                nc.gpsimd.tensor_copy(xkT[:, :, 0:START], xnT[:, :, 0:START])
                nc.gpsimd.tensor_copy(xkT[:, :, START:], xnT[:, :, S - RECENT:]).then_inc(xk_ready, 1)

            def k_rotate(b):
                pool.wait_ge(kn_copied, b + 1)
                kv3 = lambda t: t[0:NKEY].rearrange("p (h f) -> p h f", f=HD)
                tb = lambda t, a, z: t[0:NKEY, a:z].rearrange("p (one f) -> p one f", one=1).broadcast_to(
                    [NKEY, H, z - a])
                nc.gpsimd.tensor_tensor(kv3(km1), kv3(kraw), tb(kcos, 0, HD), ALU.mult)
                nc.gpsimd.tensor_tensor(kv3(km2)[:, :, 0:16], kv3(kraw)[:, :, 16:32], tb(ksin, 0, 16), ALU.mult)
                nc.gpsimd.tensor_tensor(kv3(km2)[:, :, 16:32], kv3(kraw)[:, :, 0:16], tb(ksin, 16, 32),
                                        ALU.mult).then_inc(k_mul, 1)
                pool.wait_ge(k_mul, b + 1)
                nc.gpsimd.tensor_tensor(krope[0:NKEY], km1[0:NKEY], km2[0:NKEY], ALU.add).then_inc(k_rope, 1)

            def add_bo(b):
                pool.wait_ge(normed, b + 1)
                nc.gpsimd.tensor_tensor(xt(b, 0), xt(b, 0), bo[:], ALU.add)
                nc.gpsimd.tensor_tensor(xt(b, 1), xt(b, 1), bo[:], ALU.add).then_inc(x_biased, 1)

            nc.gpsimd.memset(mhalf[:], -0.5).then_inc(setup, 1)
            pool.wait_ge(setup, 1)
            if A:
                nc.gpsimd.memset(kz[:], 0.0).then_inc(tapped, 1)
            ln_in(0)
            if A:
                kept_keys(0)
                pool.wait_ge(ld_c, 16 * 4)
                k_rotate(0)
                for n in range(2):
                    q_times_cos(n)
                pool.wait_ge(ld_b, 16 * 3)
                add_bo(0)

            def slot(b, g, first, last):
                n = 4 * b + g
                if g == 0 and not last:
                    ln_in(b + 1)
                if A and not last:
                    if g == 2:
                        kept_keys(b + 1)
                    if g == 3:
                        k_rotate(b + 1)
                if A and (g < 2 or not last):
                    q_times_cos(proj_of(b, g)[2])
                if g == 2 and not first:
                    ln_out(b - 1)
                scale_probs(n, g)
                if A and not last and g == 3:
                    add_bo(b + 1)

            def batch(b, first=False, last=False):
                for g in range(G):
                    slot(b, g, first, last)

            batch(0, first=True)
            if A:
                pool.wait_ge(ld_taps, 32)
                pool.wait_ge(tapped, 1)
                nc.gpsimd.tensor_tensor(kz[:, P:P + 1], kz[:, P:P + 1], dk[:], ALU.add).then_inc(tapped, 1)
            with pool.Fori(1, B - 1) as b:
                batch(b)
            batch(B - 1, last=True)
            ln_out(B - 1)

        @block.vector
        def _(dve):
            def ln_stats(b, i, got, agg):
                if not isinstance(b, int):
                    dve.sem_inc(passed_dve, 1)
                for t in range(TB):
                    last = nc.vector.bn_stats(st[:, i, t], xt(b, t))
                last.then_inc(got, 1)
                wait_apart(dve, got, b + 1, passed_dve)
                for t in range(TB):
                    last = nc.vector.bn_aggr(mv[:, i, t], st[:, i, t])
                last.then_inc(agg, 1)

            def ln_apply(b, i, got, out, done):
                dve.wait_ge(got, b + 1)
                for t in range(TB):
                    last = nc.vector.tensor_scalar(out[:, t], xt(b, t), mv[:, i, t, 0:1], rstd[:, i, t:t + 1],
                                                   ALU.subtract, ALU.mult)
                last.then_inc(done, 1)

            def ln_in(b):
                ln_stats(b, 0, stats, aggr)

            def ln_in_apply(b):
                wait(dve, pe_xT, TB * b)
                ln_apply(b, 0, lnrstd, xn, normed)

            def ln_out(b):
                ln_stats(b, 1, ostats, oaggr)

            def ln_out_apply(b):
                wait(dve, pe_oT, TB * b)
                ln_apply(b, 1, olnrstd, xo, onormed)

            def max_scores(n, g):
                dve.wait_ge(pe_s, n + 1 if A else 3 * n + 1)
                wait(dve, exped, n - 1)
                wait(dve, pe_t, n - 1)
                if not A:
                    dve.sem_inc(passed_dve, 1)
                if A:
                    nc.vector.tensor_reduce(mx[:, g % 2].rearrange("p (t j) -> p t j", t=TB),
                                            ps_s[:, 2 * (g % 2):2 * (g % 2) + TB, 0:4 * NKEY]
                                            .rearrange("p t (j k) -> p t j k", j=4),
                                            AX.X, ALU.max).then_inc(maxed, 1)
                else:
                    for j in range(4):
                        nc.vector.tensor_tensor_reduce(
                            out=prob[:, g % 2, j, 0:P], in0=ps_s[:, 0, j * P:(j + 1) * P],
                            in1=alibi[:, 4 * g + j, 0:P], scale=1.0, scalar=-3e38, op0=ALU.add, op1=ALU.max,
                            accum_out=mx[:, g % 2, j:j + 1])
                    for j in range(4):
                        if j % 2 == 0:
                            dve.wait_ge(pe_s, 3 * n + 2 + j // 2)
                            dve.sem_inc(passed_dve, 1)
                        last = nc.vector.tensor_tensor_reduce(
                            out=prob[:, g % 2, j, P:3 * P],
                            in0=ps_s[:, 1 + j // 2, (j % 2) * S:(j % 2) * S + S],
                            in1=alibi[:, 4 * g + j, P:3 * P], scale=1.0, scalar=-3e38, op0=ALU.add, op1=ALU.max,
                            accum_out=mx[:, g % 2, 4 + j:5 + j])
                    last.then_inc(maxed, 1)
                dve.wait_ge(maxed, n + 1)
                nc.vector.tensor_scalar(nmax[:, g % 2], mx[:, g % 2], -1.0, None, ALU.mult).then_inc(negated, 1)

            def turn_copy(n):
                dve.wait_ge(pe_t, n + 1)
                nc.vector.tensor_copy(probT[:, 0:2], ps_t[:, 0].rearrange("p (j q) -> p j q", j=2)).then_inc(pT_dve, 1)

            def reciprocals(n, g):
                dve.wait_ge(exped, n + 1)
                wait(dve, scaled, n - 1)
                nc.vector.reciprocal(rinv[:, g % 2], rsum[:, g % 2]).then_inc(summed, 1)

            def q_rotate(n, g):
                wait_apart(dve, q_copied, n + 1, passed_dve)
                nc.vector.stream_shuffle(qsw[:], qraw[:], SWAP16).then_inc(q_swap, 1)
                dve.wait_ge(q_swap, n + 1)
                nc.vector.tensor_tensor(qm2[:], qsw[:], qsin[:], ALU.mult).then_inc(q_sin, 1)
                dve.wait_ge(q_sin, n + 1)
                dve.wait_ge(q_cos, n + 1)
                nc.vector.tensor_tensor(qT[:, g], qm1[:], qm2[:], ALU.add).then_inc(q_ready, 1)

            def k_copy(n, g):
                dve.wait_ge(pe_k, n + 1)
                for j in (0, 1):
                    last = nc.vector.tensor_copy(kD[32 * j:32 * j + 32, g, j], bank[1][32 * j:32 * j + 32, 0:S])
                last.then_inc(k_dve, 1)

            def k_copy_a(b):
                dve.wait_ge(pe_k, b + 1)
                for j in (0, 1):
                    last = nc.vector.tensor_copy(kD[32 * j:32 * j + 32, :, j],
                                                 bank[1][32 * j:32 * j + 32, 0:4 * NKEY]
                                                 .rearrange("p (g k) -> p g k", g=G))
                last.then_inc(k_dve, 1)

            def kn_copy(b):
                dve.wait_ge(pe_kn, b + 1)
                wait(dve, k_mul, b)
                nc.vector.tensor_tensor(kraw[0:NKEY], bank[1][0:NKEY, :], bk[0:NKEY], ALU.add)\
                    .then_inc(kn_copied, 1)

            def v_copy(n, g):
                dve.wait_ge(pe_v, n + 1)
                c = slice(g * P, g * P + P)
                if A:
                    nc.vector.tensor_tensor(v[0:NKEY, 0, c], bank[1][0:NKEY, 0:P], bv[0:NKEY, c], ALU.add)\
                        .then_inc(v_copied, 1)
                else:
                    nc.vector.tensor_copy(v[:, :, c], bank[1][:, 0:TB * P].rearrange("p (t f) -> p t f", t=TB))\
                        .then_inc(v_copied, 1)

            def add_out(b, t):
                if A and t == 0:
                    dve.wait_ge(x_biased, b + 1)
                dve.wait_ge(pe_o, TB * b + t + 1)
                nc.vector.tensor_tensor(xt(b, t), xt(b, t), ps_t[:, t], ALU.add).then_inc(x_added, 1)

            if A:
                dve.wait_ge(ld_x0, 16)
            ln_in(0)
            ln_in_apply(0)
            nc.vector.memset(kD[:], 0.0).then_inc(zeroed, 1)
            if A:
                nc.vector.memset(prob[:], 0.0).then_inc(zeroed, 1)
                nc.vector.memset(v[:], 0.0).then_inc(zeroed, 1)
            dve.wait_ge(zeroed, 3 if A else 1)
            if A:
                dve.wait_ge(ld_b, 16 * 3)
                dve.wait_ge(ld_c, 16 * 4)
                kn_copy(0)
                k_copy_a(0)
            for g in range(2):
                if A:
                    q_rotate(g, g)
                else:
                    k_copy(g, g)
                v_copy(g, g)
            if A:
                dve.wait_ge(ld_x, 16 * (B - 1))

            def slot(b, g, first, last):
                n = 4 * b + g
                _, pg, pn = proj_of(b, g)
                project = g < 2 or not last
                max_scores(n, g)
                if g == 0 and not last:
                    ln_in(b + 1)
                if project and not A:
                    k_copy(pn, pg)
                if g == 0 and not last:
                    ln_in_apply(b + 1)
                if project:
                    v_copy(pn, pg)
                if g == 3 and not first:
                    ln_out_apply(b - 1)
                if g == 1 and not first:
                    add_out(b - 1, 0)
                if g == 2 and not first:
                    add_out(b - 1, 1)
                    dve.wait_ge(x_added, TB * b)
                    ln_out(b - 1)
                if g in (1, 2):
                    reciprocals(n, g)
                    if project and A:
                        q_rotate(pn, pg)
                if A and not last and g == 2:
                    kn_copy(b + 1)
                if A and not last and g == 3:
                    k_copy_a(b + 1)
                if not (first and g == 0):
                    turn_copy(n - 1)
                if g not in (1, 2):
                    reciprocals(n, g)
                    if project and A:
                        q_rotate(pn, pg)

            def batch(b, first=False, last=False):
                for g in range(G):
                    slot(b, g, first, last)

            batch(0, first=True)
            with dve.Fori(1, B - 1) as b:
                batch(b)
            batch(B - 1, last=True)
            turn_copy(4 * B - 1)
            for t in range(TB):
                add_out(B - 1, t)
            dve.wait_ge(x_added, TB * B)
            ln_out(B - 1)
            ln_out_apply(B - 1)

        @block.scalar
        def _(act):
            nc.scalar.preload_act_table(ACT.Exp)
            if A:
                act.dma_start(bq[:], consts["bq"]).then_inc(ld_q, 16)
                act.dma_start(bk[:], consts["bk"]).then_inc(ld_b, 16)
                act.dma_start(kcos[0:NKEY], consts["kcos"]).then_inc(ld_c, 16)
                act.dma_start(ksin[0:NKEY], consts["ksin"]).then_inc(ld_c, 16)
                act.dma_start(qcos[:], consts["qcos"]).then_inc(ld_c, 16)
                act.dma_start(qsin[:], consts["qsin"]).then_inc(ld_c, 16)
                act.dma_start(bv[:], consts["bv"]).then_inc(ld_b, 16)
                act.dma_start(bo[:], consts["bo"]).then_inc(ld_b, 16)

            def xT_copy(b):
                for t in range(TB):
                    act.wait_ge(pe_xT, TB * b + t + 1)
                    nc.scalar.activation(xnT[:, :, t * P:(t + 1) * P],
                                         bank[t][:].rearrange("p (k q) -> p k q", k=KC),
                                         ACT.Copy).then_inc(xT_copied, 1)

            def q_copy(n, g):
                act.wait_ge(pe_q, n + 1)
                if A:
                    wait(act, q_swap, n)
                    wait(act, q_cos, n)
                    nc.scalar.activation(qraw[:], bank[0][:, 0:S], ACT.Identity, bias=bq[:, g:g + 1])\
                        .then_inc(q_copied, 1)
                else:
                    nc.scalar.activation(qT[:, g], bank[0][:, 0:S], ACT.Copy, scale=float(HD) ** -0.5)\
                        .then_inc(q_copied, 1)

            def k_copy(n, g):
                act.wait_ge(pe_k, n + 1)
                for j in (2, 3):
                    last = nc.scalar.activation(kD[32 * j:32 * j + 32, g, j], bank[1][32 * j:32 * j + 32, 0:S],
                                                ACT.Copy)
                last.then_inc(k_act, 1)

            def k_copy_a(b):
                act.wait_ge(pe_k, b + 1)
                for j in (2, 3):
                    last = nc.scalar.activation(kD[32 * j:32 * j + 32, :, j],
                                                bank[1][32 * j:32 * j + 32, 0:4 * NKEY]
                                                .rearrange("p (g k) -> p g k", g=G), ACT.Copy)
                last.then_inc(k_act, 1)

            def exponentials(n, g):
                act.wait_ge(negated, n + 1)
                wait(act, summed, n - 1)
                for j in range(4):
                    for t in range(TB):
                        c = t * 4 + j
                        if A:
                            out = prob[:, g % 2, j, t * P:t * P + NKEY]
                            src = ps_s[:, 2 * (g % 2) + t, j * NKEY:(j + 1) * NKEY]
                        else:
                            src = out = prob[:, g % 2, j, 0:P] if t == 0 else prob[:, g % 2, j, P:3 * P]
                        last = nc.scalar.activation(out, src, ACT.Exp, bias=nmax[:, g % 2, c:c + 1],
                                                    accum_out=rsum[:, g % 2, c:c + 1])
                last.then_inc(exped, 1)

            def turn_copy(n):
                act.wait_ge(pe_t, n + 1)
                last = nc.scalar.activation(probT[:, 2:4], ps_t[:, 1].rearrange("p (j q) -> p j q", j=2), ACT.Copy)
                if not A:
                    last = nc.scalar.activation(probT1[:], bank[2][:].rearrange("p (j q) -> p j q", j=4), ACT.Copy)
                last.then_inc(pT_act, 1)

            def pv_copy(n, g):
                act.wait_ge(pe_pv, n + 1)
                nc.scalar.activation(oT[:, g], bank[0][:, 0:S], ACT.Copy).then_inc(pv_copied, 1)

            def oT_copy(b):
                for t in range(TB):
                    act.wait_ge(pe_oT, TB * b + t + 1)
                    src = bank[t][:].rearrange("p (k q) -> p k q", k=KC)
                    if A:
                        dst = big[:, :, bass.ds(b + t * P * B, P, step=B)] if isinstance(b, int) else \
                            big[:].rearrange("p k (q b) -> p k q b", b=B)[:, :, t * P:(t + 1) * P, bass.ds(b, 1)]
                        if not isinstance(b, int):
                            src = src.rearrange("p k (q one) -> p k q one", one=1)
                    else:
                        dst = big[:, :, bass.ds(b * S + t * P, P)]
                    nc.scalar.activation(dst, src, ACT.Copy).then_inc(oT_copied, 1)

            xT_copy(0)
            act.wait_ge(zeroed, 3 if A else 1)
            if A:
                k_copy_a(0)
                act.wait_ge(ld_q, 16 * 2)
            for g in range(2):
                q_copy(g, g)
                if not A:
                    k_copy(g, g)

            def slot(b, g, first, last):
                n = 4 * b + g
                _, pg, pn = proj_of(b, g)
                if not (first and g < 2):
                    pv_copy(n - 2, (g - 2) % 4)
                if A:
                    exponentials(n, g)
                if g < 2 or not last:
                    if not A:
                        k_copy(pn, pg)
                    q_copy(pn, pg)
                if not A:
                    exponentials(n, g)
                if g == 1 and not last:
                    xT_copy(b + 1)
                if A and g == 3 and not last:
                    k_copy_a(b + 1)
                if not (first and g == 0):
                    turn_copy(n - 1)
                if g == 3 and not first:
                    oT_copy(b - 1)

            def batch(b, first=False, last=False):
                for g in range(G):
                    slot(b, g, first, last)

            batch(0, first=True)
            with act.Fori(1, B - 1) as b:
                batch(b)
            batch(B - 1, last=True)
            pv_copy(4 * B - 2, 2)
            turn_copy(4 * B - 1)
            pv_copy(4 * B - 1, 3)
            oT_copy(B - 1)

        @block.tensor
        def _(pe):
            mm, tr = nc.tensor.matmul, nc.tensor.transpose

            def turn_x(b, src, ready, done, copied):
                pe.wait_ge(ready, b + 1)
                for t in range(TB):
                    for k in range(KC):
                        last = tr(bank[t][:, k * P:(k + 1) * P], src[:, t, k * P:(k + 1) * P], ident[:])
                    last.then_inc(done, 1)

            def project_q(n, g):
                for k in range(KC):
                    last = mm(bank[0][:, 0:S], wq[:, k, g * P:(g + 1) * P], xnT[:, k], start=(k == 0),
                              stop=(k == KC - 1))
                last.then_inc(pe_q, 1)

            def project_k(n, g):
                for k in range(KC):
                    last = mm(bank[1][:, 0:S], wk[:, k, g * P:(g + 1) * P], xnT[:, k], start=(k == 0),
                              stop=(k == KC - 1))
                last.then_inc(pe_k, 1)

            def project_kn(b):
                for k in range(KC):
                    last = mm(bank[1][0:NKEY, :], xkT[:, k], wk[:, k], start=(k == 0), stop=(k == KC - 1))
                last.then_inc(pe_kn, 1)

            def turn_k(b):
                pe.wait_ge(k_rope, b + 1)
                for g in range(G):
                    last = tr(bank[1][:, g * NKEY:(g + 1) * NKEY], krope[0:NKEY, g * P:(g + 1) * P],
                              ident[0:NKEY, 0:NKEY])
                last.then_inc(pe_k, 1)

            def project_v(n, g):
                c = slice(g * P, (g + 1) * P)
                for t in range(1 if A else TB):
                    out = bank[1][0:NKEY, 0:P] if A else bank[1][:, t * P:(t + 1) * P]
                    for k in range(KC):
                        lhs = xkT[:, k] if A else xnT[:, k, t * P:(t + 1) * P]
                        last = mm(out, lhs, wv[:, k, c], start=(k == 0), stop=(k == KC - 1))
                last.then_inc(pe_v, 1)

            def scores(n, g):
                if A:
                    for t in range(TB):
                        last = mm(ps_s[:, 2 * (g % 2) + t, 0:4 * NKEY], qT[:, g, t * P:(t + 1) * P],
                                  kD[:, g].rearrange("p j k -> p (j k)"), start=True, stop=True)
                else:
                    mm(ps_s[:, 0, :], qT[:, g, 0:P], kD[:, g, :, 0:P], start=True, stop=True).then_inc(pe_s, 1)
                    for jj in range(2):
                        last = mm(ps_s[:, 1 + jj, :], qT[:, g, P:2 * P],
                                  kD[:, g, 2 * jj:2 * jj + 2].rearrange("p j k -> p (j k)"), start=True, stop=True)
                        if jj == 0:
                            last.then_inc(pe_s, 1)
                last.then_inc(pe_s, 1)

            def turn_probs(n, g):
                pe.wait_ge(scaled, n + 1)
                pr = prob[:, g % 2]
                for j in range(4):
                    pt = ps_t[:, j // 2, (j % 2) * S:(j % 2) * S + S]
                    last = tr(pt[:, 0:P], pr[:, j, 0:P], ident[:])
                    last = tr(pt[:, P:2 * P], pr[:, j, P:2 * P], ident[:])
                    if not A:
                        last = tr(bank[2][:, j * P:(j + 1) * P], pr[:, j, 2 * P:3 * P], ident[:])
                last.then_inc(pe_t, 1)

            def apply_probs(n, g):
                pe.wait_ge(pT_dve, n + 1)
                pe.wait_ge(pT_act, n + 1)
                for j in range(4):
                    c = slice(g * P + j * HD, g * P + (j + 1) * HD)
                    out = bank[0][32 * j:32 * j + 32]
                    last = mm(out[:, 0:S], v[:, 0, c], probT[:, j], start=True, stop=A, skip_group_check=True)
                    if not A:
                        last = mm(out[:, P:S], v[:, 1, c], probT1[:, j], start=False, stop=True,
                                  skip_group_check=True)
                last.then_inc(pe_pv, 1)

            def project_out(b, t):
                for k in range(KC):
                    last = mm(ps_t[:, t], oT[:, k, t * P:(t + 1) * P], wo[:, k], start=(k == 0), stop=(k == KC - 1))
                last.then_inc(pe_o, 1)

            turn_x(0, xn, normed, pe_xT, xT_copied)
            pe.wait_ge(ld_k, 16)
            pe.wait_ge(xT_copied, TB)
            if A:
                pe.wait_ge(xk_ready, 1)
                project_kn(0)
                turn_k(0)
            pe.wait_ge(ld_q, 16 * 2 if A else 16)
            for g in range(2):
                wait(pe, q_copied, g)
                project_q(g, g)
                wait(pe, v_copied, g)
                if A:
                    if g == 0:
                        pe.wait_ge(k_dve, 1)
                        pe.wait_ge(k_act, 1)
                else:
                    project_k(g, g)
                    pe.wait_ge(k_dve, g + 1)
                    pe.wait_ge(k_act, g + 1)
                if g == 0:
                    pe.wait_ge(ld_v, 16)
                project_v(g, g)
            pe.wait_ge(ld_o, 16)

            def slot(b, g, first, last):
                n = 4 * b + g
                _, pg, pn = proj_of(b, g)
                project = g < 2 or not last
                if A:
                    pe.wait_ge(q_ready, n + 1)
                    pe.wait_ge(k_dve, b + 1)
                    pe.wait_ge(k_act, b + 1)
                    wait(pe, exped, n - 1)
                else:
                    pe.wait_ge(q_copied, n + 1)
                    wait(pe, maxed, n)
                scores(n, g)
                if not (first and g < 2):
                    pe.wait_ge(pT_dve, n - 1)
                    pe.wait_ge(pT_act, n - 1)
                    if g == 2 and not first:
                        project_out(b - 1, 1)
                pe.wait_ge(q_copied, pn if project else 4 * B)
                wait(pe, pv_copied, n - 2)
                if g == 2 and not last:
                    pe.wait_ge(xT_copied, TB * (b + 2))
                if g == 0 and not (isinstance(b, int) and b < 2):
                    pe.wait_ge(oT_copied, TB * (b - 1))
                if not (first and g < 2):
                    apply_probs(n - 2, (g - 2) % 4)
                if project:
                    pe.wait_ge(v_copied, pn)
                    if A:
                        if g == 2:
                            pe.wait_ge(xk_ready, b + 2)
                        if g == 3:
                            pe.wait_ge(kn_copied, b + 2)
                        project_v(pn, pg)
                    else:
                        project_k(pn, pg)
                    wait(pe, pv_copied, n - 1)
                    project_q(pn, pg)
                    if not A:
                        pe.wait_ge(k_dve, pn + 1)
                        pe.wait_ge(k_act, pn + 1)
                        project_v(pn, pg)
                if g == 1:
                    if not first:
                        pe.wait_ge(pv_copied, n - 1)
                        project_out(b - 1, 0)
                    if not last:
                        pe.wait_ge(q_copied, pn + 1)
                        pe.wait_ge(v_copied, pn + 1)
                        turn_x(b + 1, xn, normed, pe_xT, xT_copied)
                if A and g == 3 and not last:
                    pe.wait_ge(v_copied, pn + 1)
                    turn_k(b + 1)
                if A and g == 2 and not last:
                    pe.wait_ge(v_copied, pn + 1)
                    project_kn(b + 1)
                if not first and g in (1, 2):
                    pe.wait_ge(x_added, TB * (b - 1) + g)
                if not (first and g == 0):
                    turn_probs(n - 1, (g - 1) % 4)
                if g == 3 and not first:
                    if project:
                        pe.wait_ge(q_copied, pn + 1)
                        pe.wait_ge(v_copied, pn + 1)
                        if A:
                            pe.wait_ge(k_dve, b + 2)
                            pe.wait_ge(k_act, b + 2)
                    else:
                        pe.wait_ge(pv_copied, n - 1)
                    turn_x(b - 1, xo, onormed, pe_oT, oT_copied)

            def batch(b, first=False, last=False):
                for g in range(G):
                    slot(b, g, first, last)

            batch(0, first=True)
            with pe.Fori(1, B - 1) as b:
                batch(b)
            batch(B - 1, last=True)
            for n in (4 * B - 2, 4 * B - 1):
                pe.wait_ge(pT_dve, n + 1)
                pe.wait_ge(pT_act, n + 1)
                if n == 4 * B - 2:
                    pe.wait_ge(oT_copied, TB * (B - 1))
                else:
                    pe.wait_ge(pv_copied, n)
                apply_probs(n, n % 4)
                if n == 4 * B - 2:
                    turn_probs(n + 1, 3)
            pe.wait_ge(pv_copied, 4 * B)
            for t in range(TB):
                project_out(B - 1, t)
            turn_x(B - 1, xo, onormed, pe_oT, oT_copied)


def load_toep(eng, t, h, dst, done):
    row = t["kpad"][bass.ds(h, 1), 1:1 + D]
    src = bass.AP(row.tensor, row.offset, [[1, P], [1, D]])
    eng.dma_start(dst, src).then_inc(done, 16)


def load_cext(eng, t, h, dst, done):
    eng.dma_start(dst, t["ctx_rev"][bass.ds(h, 1)].rearrange("one p k c -> (one p) k c")).then_inc(done, 16)


def convolution(nc, big, t, toep, cext, toep_in, cext_in, ahead):
    with ExitStack() as ctx:
        def sb(name, shape, dt=F32):
            return ctx.enter_context(nc.sbuf_tensor("b_" + name, shape, dt))

        def sem(name):
            return ctx.enter_context(nc.semaphore("b_" + name))

        pair = sb("pair", [P, 2, KC, NDEL, CW])
        qx = sb("qx", [P, 2, KC, 11 * B])
        prod = sb("prod", [P, 2, KC, 8, CEXT * B])
        ps = ctx.enter_context(nc.psum_tensor("b_ps", [P, 2, KC, 512], F32))
        zeroed = sem("zeroed")
        paired, conv, extended = sem("paired"), sem("conv"), sem("extended")
        multiplied, wrapped, reduced, passed = sem("multiplied"), sem("wrapped"), sem("reduced"), sem("passed")
        block = ctx.enter_context(nc.Block())

        def loop(eng, body):
            for u in range(2):
                body(u, u, 0)
            with eng.Fori(1, CH // 2) as m:
                for u in range(2):
                    body(2 * m + u, u, m)

        @block.sync
        def _(sp):
            ahead(sp)

            def head(h, u, m):
                wait(sp, paired, h - 1)
                load_cext(sp, t, h, cext[:, u], cext_in[u])
                wait(sp, conv, h - 1)
                load_toep(sp, t, h, toep[:, u], toep_in[u])
            with sp.Fori(1, CH // 2) as m:
                for u in range(2):
                    head(2 * m + u, u, m)

        @block.gpsimd
        def _(pool):
            def pairs(h, u, m):
                pool.wait_ge(cext_in[u], 16 * (m + 1))
                wait(pool, conv, h - 1)
                c = cext[:, u]
                whole = bass.AP(c.tensor, c.offset, [list(c.ap[0]), list(c.ap[1]), [B, NDEL], [1, CW]])
                one = bass.AP(c.tensor, c.offset, [list(c.ap[0]), list(c.ap[1]), [0, NDEL], [1, CW]])
                nc.gpsimd.tensor_tensor(pair[:, u], whole, one, ALU.mult).then_inc(paired, 1)

            def wrap(h, u):
                pool.wait_ge(multiplied, h + 1)
                low = prod[:, u, :, 0:4, 0:4 * B]
                nc.gpsimd.tensor_tensor(low, low, prod[:, u, :, 4:8, CW:CEXT * B], ALU.add).then_inc(wrapped, 1)

            for h in range(2):
                pairs(h, h, 0)
            with pool.Fori(0, CH // 2 - 1) as m:
                for u in range(2):
                    pairs(2 * m + u + 2, u, m + 1)
                    wrap(2 * m + u, u)
            for h in range(CH - 2, CH):
                wrap(h, h % 2)

        @block.scalar
        def _(act):
            def head(h, u, m):
                wait(act, multiplied, h - 1)
                nc.scalar.activation(qx[:, u, :, 0:CW], big[:, :, bass.ds(h * CW, CW)], ACT.Copy)
                nc.scalar.activation(qx[:, u, :, CW:], big[:, :, bass.ds(h * CW, 3 * B)], ACT.Copy)\
                    .then_inc(extended, 1)
            loop(act, head)

        @block.tensor
        def _(pe):
            def head(h, u, m):
                pe.wait_ge(toep_in[u], 16 * (m + 1))
                pe.wait_ge(paired, h + 1)
                wait(pe, multiplied, h - 1)
                for lb in range(KC):
                    for mb in range(lb + 1):
                        last = nc.tensor.matmul(ps[:, u, lb, 0:NDEL * CW], toep[:, u, (lb - mb) * P:(lb - mb + 1) * P],
                                                pair[:, u, mb].rearrange("p d c -> p (d c)"),
                                                start=(mb == 0), stop=(mb == lb))
                last.then_inc(conv, 1)
            loop(pe, head)

        @block.vector
        def _(dve):
            for u in range(2):
                nc.vector.memset(prod[:, u, :, 4:8, 0:4 * B], 0.0).then_inc(zeroed, 1)
                nc.vector.memset(prod[:, u, :, 4:8, CW:], 0.0).then_inc(zeroed, 1)
            dve.wait_ge(zeroed, 4)

            def multiply(h, u):
                dve.wait_ge(conv, h + 1)
                dve.wait_ge(extended, h + 1)
                wait(dve, reduced, h - 1)
                y = ps[:, u, :, 0:NDEL * CW].rearrange("p k (d c) -> p k d c", d=NDEL)
                q, f = qx[:, u], prod[:, u]
                qs, fs = list(q.ap[1]), list(f.ap[1])
                one = bass.AP(q.tensor, q.offset, [list(q.ap[0]), qs, [0, NDEL], [1, CW]])
                to = bass.AP(f.tensor, f.offset + 3 * CEXT * B, [list(f.ap[0]), fs, [CEXT * B + B, NDEL], [1, CW]])
                nc.vector.tensor_tensor(to, y, one, ALU.mult)
                other = bass.AP(q.tensor, q.offset + B, [list(q.ap[0]), qs, [B, 3], [1, CW]])
                nc.vector.tensor_tensor(f[:, :, 0:3, 0:CW], y[:, :, 1:4], other, ALU.mult)\
                    .then_inc(multiplied, 1)

            def reduce(h, u):
                wait_apart(dve, wrapped, h + 1, passed)
                nc.vector.tensor_reduce(big[:, :, bass.ds(h * CW, CW)],
                                        prod[:, u, :, :, 0:CW].rearrange("p k r c -> p k c r"),
                                        AX.X, ALU.add).then_inc(reduced, 1)

            def head(h, u, m):
                multiply(h, u)
                if not (isinstance(h, int) and h == 0):
                    reduce(h - 1, 1 - u)
            loop(dve, head)
            reduce(CH - 1, 1)


def router(nc, x_sb, big, ident, t, wg, ld, alibi, ahead):
    R = 4
    NG = 3 * VCH
    with ExitStack() as ctx:
        def sb(name, shape, dt=F32):
            return ctx.enter_context(nc.sbuf_tensor("c_" + name, shape, dt))

        def sem(name):
            return ctx.enter_context(nc.semaphore("c_" + name))

        gb = sb("gb", [P, NG])
        rel = sb("rel", [P, 3 * P])
        slope = sb("slope", [P, H])
        yT = sb("yT", [P, 2, KC, P])
        xn = sb("xn", [P, R, D])
        xnT = sb("xnT", [P, 2, KC, P])
        sc = sb("sc", [P, 2, NG])
        top = sb("top", [P, 2, 8])
        ix = sb("ix", [P, R, 8], U32)
        st, mv = sb("st", [P, 2, 6]), sb("mv", [P, 2, 2])
        ve, rstd, mhalf = sb("ve", [P, 2]), sb("rstd", [P, 2]), sb("mhalf", [P, 1])
        ps = ctx.enter_context(nc.psum_tensor("c_ps", [P, 2, 3, 512], F32))
        ps_y = ctx.enter_context(nc.psum_tensor("c_ps_y", [P, 512], F32))
        ps_x = ctx.enter_context(nc.psum_tensor("c_ps_x", [P, 512], F32))
        gb_in, rel_in = sem("gb_in"), sem("rel_in")
        y_cut, pe_y, added = sem("y_cut"), sem("pe_y"), sem("added")
        stats, aggr, lnvar, lnrstd, normed = sem("stats"), sem("aggr"), sem("lnvar"), sem("lnrstd"), sem("normed")
        pe_x, xT_copied, scored = sem("pe_x"), sem("xT_copied"), sem("scored")
        biased, maxed, found, chosen = sem("biased"), sem("maxed"), sem("found"), sem("chosen")
        gathered = [sem(f"gathered{i}") for i in range(R)]
        setup, passed, passed_pool = sem("setup"), sem("passed"), sem("passed_pool")
        block = ctx.enter_context(nc.Block())

        def loop(eng, body):
            M = TILES // R
            for u in range(R):
                body(u, u, 0, True, False)
            with eng.Fori(1, M - 1) as m:
                for u in range(R):
                    body(R * m + u, u, m, False, False)
            for u in range(R):
                body(R * (M - 1) + u, u, M - 1, False, True)

        def x_tile(n):
            return x_sb[:, bass.ds(n * D, D)]

        @block.sync
        def _(sp):
            sp.dma_start(gb[:], t["gate_b"].rearrange("(one g) -> one g", one=1).broadcast_to([P, NG]))\
                .then_inc(gb_in, 16)
            sp.dma_start(rel[:], t["rel"]).then_inc(rel_in, 16)
            sp.dma_start(slope[:], t["slope"]).then_inc(rel_in, 16)
            ahead(sp)

        @block.scalar
        def _(act):
            def cut(n, u, m):
                wait(act, pe_y, n - 1)
                b = m * (R // TB) + u // TB
                src = big[:].rearrange("p k (q b) -> p k q b", b=B)[:, :, (u % TB) * P:(u % TB + 1) * P, bass.ds(b, 1)]
                nc.scalar.activation(yT[:, u % 2].rearrange("p k (q one) -> p k q one", one=1), src, ACT.Copy)\
                    .then_inc(y_cut, 1)

            def turned(n, u):
                act.wait_ge(pe_x, n + 1)
                wait(act, scored, n - 1)
                nc.scalar.activation(xnT[:, u % 2], ps_x[:].rearrange("p (k q) -> p k q", k=KC), ACT.Copy)\
                    .then_inc(xT_copied, 1)

            cut(0, 0, 0)
            cut(1, 1, 0)
            turned(0, 0)
            cut(2, 2, 0)

            def tile(n, u, m, first, last):
                if not (last and u >= R - 1):
                    turned(n + 1, (u + 1) % R)
                if not (last and u >= R - 3):
                    cut(n + 3, (u + 3) % R, m + (u + 3) // R)
            loop(act, tile)

        @block.tensor
        def _(pe):
            def turn_y(n, u):
                pe.wait_ge(y_cut, n + 1)
                wait(pe, added, n)
                for k in range(KC):
                    last = nc.tensor.transpose(ps_y[:, k * P:(k + 1) * P], yT[:, u % 2, k], ident[:])
                last.then_inc(pe_y, 1)

            def turn_x(n, u):
                pe.wait_ge(normed, n + 1)
                wait(pe, xT_copied, n)
                for k in range(KC):
                    last = nc.tensor.transpose(ps_x[:, k * P:(k + 1) * P], xn[:, u, k * P:(k + 1) * P], ident[:])
                last.then_inc(pe_x, 1)

            def scores(n, u, chunks):
                for c in chunks:
                    for k in range(KC):
                        last = nc.tensor.matmul(ps[:, u % 2, c, 0:VCH], xnT[:, u % 2, k],
                                                wg[:, k, c * VCH:(c + 1) * VCH], start=(k == 0), stop=(k == KC - 1))
                if 2 in chunks:
                    last.then_inc(scored, 1)

            turn_y(0, 0)
            turn_y(1, 1)
            turn_x(0, 0)
            pe.wait_ge(ld, 16)

            def tile(n, u, m, first, last):
                pe.wait_ge(xT_copied, n + 1)
                wait(pe, biased, n - 1)
                scores(n, u, (0, 1))
                if not (last and u >= R - 1):
                    turn_x(n + 1, (u + 1) % R)
                scores(n, u, (2,))
                if not (last and u >= R - 2):
                    turn_y(n + 2, (u + 2) % R)
            loop(pe, tile)

        @block.gpsimd
        def _(pool):
            def rstd_of(n, u):
                wait_apart(pool, aggr, n + 1, passed_pool)
                nc.gpsimd.tensor_scalar(ve[:, u % 2:u % 2 + 1], mv[:, u % 2, 1:2], LN_EPS, None, ALU.add)\
                    .then_inc(lnvar, 1)
                pool.wait_ge(lnvar, n + 1)
                nc.gpsimd.tensor_tensor(rstd[:, u % 2:u % 2 + 1], ve[:, u % 2:u % 2 + 1], mhalf[:], ALU.pow)\
                    .then_inc(lnrstd, 1)

            def gather(n, u):
                wait_apart(pool, found, n + 1, passed_pool)
                wait_apart(pool, pe_x, n + 1, passed_pool)
                nc.gpsimd.indirect_dma_start(
                    xn[:, u], None, t["pool"], bass.IndirectOffsetOnAxis(ap=ix[:, u, 0:1], axis=0),
                    bounds_check=NV - 1, oob_is_err=False).then_inc(gathered[u], 16)

            def add(n, u, m):
                pool.wait_ge(gathered[u], 16 * (m + 1))
                nc.gpsimd.tensor_tensor(x_tile(n), x_tile(n), xn[:, u], ALU.add).then_inc(chosen, 1)

            nc.gpsimd.memset(mhalf[:], -0.5).then_inc(setup, 1)
            pool.wait_ge(setup, 1)
            rstd_of(0, 0)
            rstd_of(1, 1)

            def tile(n, u, m, first, last):
                if not (first and u == 0):
                    add(n - 1, (u - 1) % R, m if u else m - 1)
                if not (last and u >= R - 2):
                    rstd_of(n + 2, (u + 2) % R)
                gather(n, u)
                if first:
                    pool.wait_ge(rel_in, 32)
                    h = slice(4 * u, 4 * u + 4)
                    nc.gpsimd.tensor_tensor(
                        alibi[:, h], rel[:].rearrange("p (one k) -> p one k", one=1).broadcast_to([P, 4, 3 * P]),
                        slope[:, h].rearrange("p (h one) -> p h one", one=1).broadcast_to([P, 4, 3 * P]),
                        ALU.mult).then_inc(setup, 1)
            loop(pool, tile)
            add(TILES - 1, R - 1, TILES // R - 1)

        @block.vector
        def _(dve):
            def norm_stats(n, u):
                dve.wait_ge(pe_y, n + 1)
                nc.vector.tensor_tensor(x_tile(n), x_tile(n), ps_y[:], ALU.add).then_inc(added, 1)
                wait_apart(dve, added, n + 1, passed)
                nc.vector.bn_stats(st[:, u % 2], x_tile(n)).then_inc(stats, 1)
                wait_apart(dve, stats, n + 1, passed)
                nc.vector.bn_aggr(mv[:, u % 2], st[:, u % 2]).then_inc(aggr, 1)

            def norm(n, u):
                dve.wait_ge(lnrstd, n + 1)
                wait(dve, chosen, n - R + 1)
                nc.vector.tensor_scalar(xn[:, u], x_tile(n), mv[:, u % 2, 0:1], rstd[:, u % 2:u % 2 + 1],
                                        ALU.subtract, ALU.mult).then_inc(normed, 1)

            def bias(n, u):
                dve.wait_ge(scored, n + 1)
                s = sc[:, u % 2]
                nc.vector.tensor_tensor(s.rearrange("p (c g) -> p c g", c=3), ps[:, u % 2, :, 0:VCH],
                                        gb[:].rearrange("p (c g) -> p c g", c=3), ALU.add).then_inc(biased, 1)

            def largest(n, u):
                wait_apart(dve, biased, n + 1, passed)
                nc.vector.max(top[:, u % 2], sc[:, u % 2]).then_inc(maxed, 1)

            def place(n, u):
                wait_apart(dve, maxed, n + 1, passed)
                nc.vector.max_index(ix[:, u], top[:, u % 2], sc[:, u % 2]).then_inc(found, 1)

            for n in range(2):
                norm_stats(n, n)
                norm(n, n)
            dve.wait_ge(gb_in, 16)

            def tile(n, u, m, first, last):
                bias(n, u)
                if not (last and u >= R - 2):
                    norm_stats(n + 2, (u + 2) % R)
                largest(n, u)
                if not (last and u >= R - 2):
                    norm(n + 2, (u + 2) % R)
                place(n, u)
            loop(dve, tile)


def load_head(eng, t, h, wh, cT, decay, done):
    eng.dma_start(wh, t["wh"][h]).then_inc(done, 16)
    eng.dma_start(cT, t["ctxT"][h]).then_inc(done, 16)
    eng.dma_start(decay, t["decay"][h]).then_inc(done, 16)


def retention(nc, big, t, o_sb, wh, cT, decay, in_, ahead):
    CHUNK = 512
    NCH = TOK // CHUNK
    with ExitStack() as ctx:
        def sb(name, shape, dt=F32):
            return ctx.enter_context(nc.sbuf_tensor("e_" + name, shape, dt))

        def sem(name):
            return ctx.enter_context(nc.semaphore("e_" + name))

        qT, kT = sb("qT", [P, TOK]), sb("kT", [P, TOK])
        v = sb("v", [P, TILES, RD])
        raw, a = sb("raw", [P, TB, S]), sb("a", [P, TB, S])
        ps_p = [ctx.enter_context(nc.psum_tensor(f"e_ps_p{i}", [P, CHUNK], F32)) for i in range(2)]
        ps_v = [ctx.enter_context(nc.psum_tensor(f"e_ps_v{i}", [P, CHUNK], F32)) for i in range(2)]
        ps_s = ctx.enter_context(nc.psum_tensor("e_ps_s", [P, TB, S], F32))
        ps_o = [ctx.enter_context(nc.psum_tensor(f"e_ps_o{i}", [P, CHUNK], F32)) for i in range(2)]
        pe_q, pe_k, pe_v, pe_s, pe_o = sem("pe_q"), sem("pe_k"), sem("pe_v"), sem("pe_s"), sem("pe_o")
        q_copied, k_copied, v_copied = sem("q_copied"), sem("k_copied"), sem("v_copied")
        decayed, negated, clamped, o_copied = sem("decayed"), sem("negated"), sem("clamped"), sem("o_copied")
        block = ctx.enter_context(nc.Block())

        def loop(eng, body):
            for h in range(RH):
                body(h, h % 2, h // 2, h == 0, h == RH - 1)

        @block.sync
        def _(sp):
            ahead(sp)
            for h in range(2, RH):
                sp.wait_ge(pe_v, NCH * (h - 1))
                sp.wait_ge(decayed, h - 1)
                load_head(sp, t, h, wh[:, h % 2], cT[:, h % 2], decay[:, h % 2], in_[h % 2])

        @block.tensor
        def _(pe):
            mm = nc.tensor.matmul

            def queries(h, u, m, first, last):
                pe.wait_ge(in_[u], 48 * (m + 1))
                for c in range(NCH):
                    i = NCH * h + c
                    wait(pe, k_copied, NCH * h - 1 + c) if c < 2 else pe.wait_ge(q_copied, i - 1)
                    mm(ps_p[c % 2][:], wh[:, u], big[:, h, c * CHUNK:(c + 1) * CHUNK], start=True, stop=True)\
                        .then_inc(pe_q, 1)

            def keys(h, u):
                for c in range(NCH):
                    i = NCH * h + c
                    pe.wait_ge(q_copied, NCH * h + NCH - 1 + c) if c < 2 else pe.wait_ge(k_copied, i - 1)
                    mm(ps_p[c % 2][:], wh[:, u], cT[:, u, c * CHUNK:(c + 1) * CHUNK], start=True, stop=True)\
                        .then_inc(pe_k, 1)

            def values(h, u):
                for c in range(NCH):
                    wait(pe, v_copied, NCH * h + c - 1)
                    for i in range(4):
                        last = mm(ps_v[c % 2][:, i * P:(i + 1) * P], cT[:, u, (4 * c + i) * P:(4 * c + i + 1) * P],
                                  wh[:, u], start=True, stop=True)
                    last.then_inc(pe_v, 1)

            def scores(h):
                pe.wait_ge(q_copied, NCH * (h + 1))
                pe.wait_ge(k_copied, NCH * (h + 1))
                wait(pe, decayed, h)
                for tt in range(TB):
                    for b in range(B):
                        last = mm(ps_s[:, tt], kT[:, b * S + tt * P:b * S + (tt + 1) * P], qT[:, b * S:(b + 1) * S],
                                  start=(b == 0), stop=(b == B - 1))
                last.then_inc(pe_s, 1)

            def outputs(h):
                pe.wait_ge(clamped, h + 1)
                pe.wait_ge(v_copied, NCH * (h + 1))
                for ss in range(TB):
                    for half in range(2):
                        wait(pe, o_copied, NCH * h + 2 * ss + half - 1)
                        vs = v[:].rearrange("p (b t) e -> p b t e", t=TB)
                        for tt in range(TB):
                            last = mm(ps_o[half][:], a[:, tt, ss * P:(ss + 1) * P],
                                      vs[:, 4 * half:4 * half + 4, tt, :], start=(tt == 0), stop=(tt == TB - 1))
                        last.then_inc(pe_o, 1)

            def head(h, u, m, first, last):
                if first:
                    queries(h, u, m, first, last)
                keys(h, u)
                if not first:
                    outputs(h - 1)
                values(h, u)
                scores(h)
                if not last:
                    queries(h + 1, 1 - u, m + u, first, last)
                else:
                    outputs(h)
            loop(pe, head)

        @block.scalar
        def _(act):
            def head(h, u, m, first, last):
                for c in range(NCH):
                    i = NCH * h + c
                    act.wait_ge(pe_q, i + 1)
                    wait(act, pe_s, h)
                    nc.scalar.activation(qT[:, c * CHUNK:(c + 1) * CHUNK], ps_p[c % 2][:], ACT.Copy)\
                        .then_inc(q_copied, 1)
                for c in range(NCH):
                    i = NCH * h + c
                    act.wait_ge(pe_v, i + 1)
                    wait(act, pe_o, NCH * h)
                    nc.scalar.activation(v[:, 4 * c:4 * c + 4], ps_v[c % 2][:].rearrange("p (t e) -> p t e", t=4),
                                         ACT.Copy).then_inc(v_copied, 1)
            loop(act, head)

        @block.vector
        def _(dve):
            def outputs(h):
                for ss in range(TB):
                    for half in range(2):
                        dve.wait_ge(pe_o, NCH * h + 2 * ss + half + 1)
                        o4 = o_sb[:].rearrange("p (b t) f -> p b t f", t=TB)
                        nc.vector.tensor_copy(o4[:, 4 * half:4 * half + 4, ss, h * RD:(h + 1) * RD],
                                              ps_o[half][:].rearrange("p (b e) -> p b e", b=4)).then_inc(o_copied, 1)

            def head(h, u, m, first, last):
                for c in range(NCH):
                    dve.wait_ge(pe_k, NCH * h + c + 1)
                    wait(dve, pe_s, h)
                    nc.vector.tensor_copy(kT[:, c * CHUNK:(c + 1) * CHUNK], ps_p[c % 2][:]).then_inc(k_copied, 1)
                if not first:
                    outputs(h - 1)
                dve.wait_ge(pe_s, h + 1)
                wait(dve, clamped, h)
                nc.vector.tensor_tensor(raw[:], ps_s[:], decay[:, u], ALU.mult).then_inc(decayed, 1)
                dve.wait_ge(decayed, h + 1)
                wait(dve, pe_o, NCH * h)
                nc.vector.tensor_scalar(a[:], raw[:], -1.0, 1.0, ALU.mult, ALU.max).then_inc(negated, 1)
                dve.wait_ge(negated, h + 1)
                nc.vector.tensor_tensor(a[:], a[:], raw[:], ALU.max).then_inc(clamped, 1)
            loop(dve, head)
            outputs(RH - 1)


def mixing(nc, x_sb, big, ident, o_sb, weights, ld, logitT, xn_rows, ahead):
    with ExitStack() as ctx:
        def sb(name, shape, dt=F32):
            return ctx.enter_context(nc.sbuf_tensor("f_" + name, shape, dt))

        def sem(name):
            return ctx.enter_context(nc.semaphore("f_" + name))

        wgate, wout, gamma, beta, wr, br = weights
        on = sb("on", [P, 2, D])
        w = sb("w", [P, 2, KC, P])
        y = sb("y", [P, 2, KC, P])
        wy = sb("wy", [P, 2, KC, P])
        xf = sb("xf", [P, 2, D])
        xfT = sb("xfT", [P, 2, KC, P])
        st, mv = sb("st", [P, 2, 2, 6]), sb("mv", [P, 2, 2, 2])
        ve, rstd, mhalf = sb("ve", [P, 2, 2]), sb("rstd", [P, 2, 2]), sb("mhalf", [P, 1])
        ps = [ctx.enter_context(nc.psum_tensor(f"f_ps{i}", [P, 512], F32)) for i in range(5)]
        ps_y, ps_w, ps_o, ps_x, ps_l = ps
        setup = sem("setup")
        ostats, oaggr, ovar, orstd, onormed = (sem(n) for n in ("ostats", "oaggr", "ovar", "orstd", "onormed"))
        xstats, xaggr, xvar, xrstd, xnormed = (sem(n) for n in ("xstats", "xaggr", "xvar", "xrstd", "xnormed"))
        pe_y, pe_w, pe_o, pe_x, pe_l = (sem(n) for n in ("pe_y", "pe_w", "pe_o", "pe_x", "pe_l"))
        relued, scaled, gated, added = sem("relued"), sem("scaled"), sem("gated"), sem("added")
        xT_copied, l_copied, passed, passed_pool = (sem(n) for n in ("xT_copied", "l_copied", "passed",
                                                                    "passed_pool"))
        stored = [sem("stored0"), sem("stored1")]
        block = ctx.enter_context(nc.Block())

        def loop(eng, body):
            M = TILES // 2
            for u in range(2):
                body(u, u, 0, True, False)
            with eng.Fori(1, M - 1) as m:
                for u in range(2):
                    body(2 * m + u, u, m, False, False)
            for u in range(2):
                body(2 * (M - 1) + u, u, M - 1, False, True)

        def tile_of(s, n):
            return s[:, bass.ds(n * D, D)]

        o2 = o_sb[:].rearrange("p n d -> p (n d)")

        @block.sync
        def _(sp):
            ahead(sp)

            def tile(n, u, m, first, last):
                sp.wait_ge(xnormed, n + 1)
                sp.dma_start(xn_rows[bass.ds(n * P, P), :], xf[:, u]).then_inc(stored[u], 16)
            loop(sp, tile)
            for i in range(2):
                sp.wait_ge(stored[i], 16 * (TILES // 2))

        @block.gpsimd
        def _(pool):
            def rstd_of(n, u, i, eps, got, var, done):
                wait_apart(pool, got, n + 1, passed_pool)
                nc.gpsimd.tensor_scalar(ve[:, i, u:u + 1], mv[:, i, u, 1:2], eps, None, ALU.add).then_inc(var, 1)
                pool.wait_ge(var, n + 1)
                nc.gpsimd.tensor_tensor(rstd[:, i, u:u + 1], ve[:, i, u:u + 1], mhalf[:], ALU.pow).then_inc(done, 1)

            nc.gpsimd.memset(mhalf[:], -0.5).then_inc(setup, 1)
            pool.wait_ge(setup, 1)
            for n in range(2):
                rstd_of(n, n, 0, GN_EPS, oaggr, ovar, orstd)

            def tile(n, u, m, first, last):
                if not last:
                    rstd_of(n + 2, u, 0, GN_EPS, oaggr, ovar, orstd)
                rstd_of(n, u, 1, LN_EPS, xaggr, xvar, xrstd)
            loop(pool, tile)

        @block.vector
        def _(dve):
            def stats(src, n, u, i, got, agg):
                nc.vector.bn_stats(st[:, i, u], tile_of(src, n)).then_inc(got, 1)
                wait_apart(dve, got, n + 1, passed)
                nc.vector.bn_aggr(mv[:, i, u], st[:, i, u]).then_inc(agg, 1)

            def apply(src, n, u, i, out, ready, done):
                dve.wait_ge(ready, n + 1)
                nc.vector.tensor_scalar(out[:, u], tile_of(src, n), mv[:, i, u, 0:1], rstd[:, i, u:u + 1],
                                        ALU.subtract, ALU.mult).then_inc(done, 1)

            def norm_o(n, u):
                stats(o2, n, u, 0, ostats, oaggr)
                wait(dve, pe_y, n - 1)
                apply(o2, n, u, 0, on, orstd, onormed)

            def gate(n, u):
                dve.wait_ge(scaled, n + 1)
                dve.wait_ge(relued, n + 1)
                wait(dve, pe_o, n - 1)
                nc.vector.tensor_tensor(wy[:, u], y[:, u], w[:, u], ALU.mult).then_inc(gated, 1)

            def norm_x(n, u, m):
                dve.wait_ge(pe_o, n + 1)
                nc.vector.tensor_tensor(tile_of(x_sb, n), tile_of(x_sb, n), ps_o[:], ALU.add).then_inc(added, 1)
                wait_apart(dve, added, n + 1, passed)
                stats(x_sb, n, u, 1, xstats, xaggr)
                wait(dve, pe_x, n - 1)
                wait(dve, stored[u], 16 * m)
                apply(x_sb, n, u, 1, xf, xrstd, xnormed)

            for n in range(2):
                norm_o(n, n)

            def tile(n, u, m, first, last):
                gate(n, u)
                if not last:
                    norm_o(n + 2, u)
                norm_x(n, u, m)
            loop(dve, tile)

        @block.scalar
        def _(act):
            act.wait_ge(ld, 96)

            def gates(n, u):
                act.wait_ge(pe_y, n + 1)
                wait(act, gated, n - 1)
                for k in range(KC):
                    last = nc.scalar.activation(y[:, u, k], ps_y[:, k * P:(k + 1) * P], ACT.Identity,
                                                bias=beta[:, k:k + 1], scale=gamma[:, k:k + 1])
                last.then_inc(scaled, 1)
                act.wait_ge(pe_w, n + 1)
                nc.scalar.activation(w[:, u], ps_w[:].rearrange("p (k q) -> p k q", k=KC), ACT.Relu)\
                    .then_inc(relued, 1)

            def turned(n, u):
                act.wait_ge(pe_x, n + 1)
                wait(act, pe_l, n - 1)
                nc.scalar.activation(xfT[:, u], ps_x[:].rearrange("p (k q) -> p k q", k=KC), ACT.Copy)\
                    .then_inc(xT_copied, 1)

            def logits(n, u):
                act.wait_ge(pe_l, n + 1)
                nc.scalar.activation(logitT[0:NE, bass.ds(n * P, P)], ps_l[0:NE, 0:P], ACT.Identity,
                                     bias=br[0:NE, 0:1]).then_inc(l_copied, 1)

            gates(0, 0)

            def tile(n, u, m, first, last):
                if not (last and u == 1):
                    gates(n + 1, 1 - u)
                if not (first and u == 0):
                    turned(n - 1, 1 - u)
                    logits(n - 1, 1 - u)
            loop(act, tile)
            turned(TILES - 1, 1)
            logits(TILES - 1, 1)

        @block.tensor
        def _(pe):
            mm, tr = nc.tensor.matmul, nc.tensor.transpose

            def gates(n, u):
                pe.wait_ge(onormed, n + 1)
                wait(pe, scaled, n)
                for k in range(KC):
                    last = tr(ps_y[:, k * P:(k + 1) * P], on[:, u, k * P:(k + 1) * P], ident[:])
                last.then_inc(pe_y, 1)
                wait(pe, relued, n)
                for e in range(KC):
                    for k in range(KC):
                        last = mm(ps_w[:, e * P:(e + 1) * P], wgate[:, k, e * P:(e + 1) * P],
                                  big[:, k, bass.ds(n * P, P)], start=(k == 0), stop=(k == KC - 1))
                last.then_inc(pe_w, 1)

            def project(n, u):
                pe.wait_ge(gated, n + 1)
                wait(pe, added, n)
                for k in range(KC):
                    last = mm(ps_o[:], wy[:, u, k], wout[:, k], start=(k == 0), stop=(k == KC - 1))
                last.then_inc(pe_o, 1)

            def turn_x(n, u):
                pe.wait_ge(xnormed, n + 1)
                wait(pe, xT_copied, n)
                for k in range(KC):
                    last = tr(ps_x[:, k * P:(k + 1) * P], xf[:, u, k * P:(k + 1) * P], ident[:])
                last.then_inc(pe_x, 1)

            def logits(n, u):
                pe.wait_ge(xT_copied, n + 1)
                wait(pe, l_copied, n)
                for k in range(KC):
                    last = mm(ps_l[0:NE, 0:P], wr[:, k], xfT[:, u, k], start=(k == 0), stop=(k == KC - 1))
                last.then_inc(pe_l, 1)

            pe.wait_ge(ld, 96)
            gates(0, 0)

            def tile(n, u, m, first, last):
                if not (last and u == 1):
                    gates(n + 1, 1 - u)
                if not (first and u == 0):
                    turn_x(n - 1, 1 - u)
                project(n, u)
                if not (first and u == 0):
                    logits(n - 1, 1 - u)
            loop(pe, tile)
            turn_x(TILES - 1, 1)
            logits(TILES - 1, 1)


def experts(nc, x_sb, ident, weights, ld, logitT, xn_rows, order_rows, out):
    R = 4
    with ExitStack() as ctx:
        def sb(name, shape, dt=F32):
            return ctx.enter_context(nc.sbuf_tensor("g_" + name, shape, dt))

        def sem(name):
            return ctx.enter_context(nc.semaphore("g_" + name))

        before, later, iota, ids, we, be = weights
        ones = sb("ones", [P, P])
        lg, ex, pr = (sb(n, [P, TILES, NE]) for n in ("lg", "ex", "pr"))
        far, place, hot, ranks = (sb(n, [P, TILES, NE]) for n in ("far", "place", "hot", "ranks"))
        m1, sm, ri, best, first_, rank = (sb(n, [P, TILES]) for n in ("m1", "sm", "ri", "best", "first", "rank"))
        rank_i = sb("rank_i", [P, TILES], U32)
        total = sb("total", [P, 1])
        totals = sb("totals", [P, P])
        ord_t = sb("ord_t", [TILES, P])
        order = sb("order", [P, TILES], U32)
        xs = sb("xs", [P, R, D])
        xsT = sb("xsT", [P, 2, KC, P])
        eo = sb("eo", [P, 2, D])
        ps = [ctx.enter_context(nc.psum_tensor(f"g_ps{i}", [P, 512], F32)) for i in range(8)]
        ps_l, ps_r, ps_t, ps_d = ps[0], ps[1], ps[2], ps[3]
        ps_x, ps_e = ps[4:6], ps[6:8]
        dv, pe_s, ac = sem("dv"), sem("pe_s"), sem("ac")
        sent, order_in, pl = sem("sent"), sem("order_in"), sem("pl")
        fetched = [sem(f"fetched{i}") for i in range(R)]
        pe_x, xT_copied, pe_e = sem("pe_x"), sem("xT_copied"), sem("pe_e")
        biased, mixed, passed_pool, passed = sem("biased"), sem("mixed"), sem("passed_pool"), sem("passed")
        outs = sem("outs")
        block = ctx.enter_context(nc.Block())

        def loop(eng, body):
            for u in range(R):
                body(u, u, 0)
            with eng.Fori(1, TILES // R) as m:
                for u in range(R):
                    body(R * m + u, u, m)

        def x_tile(n):
            return x_sb[:, bass.ds(n * D, D)]

        @block.sync
        def _(sp):
            sp.wait_ge(sent, 16 * TILES)
            sp.dma_start(ord_t[:], order_rows.rearrange("(n p) one -> n (p one)", p=P)).then_inc(order_in, 16)

            def tile(n, u, m):
                sp.wait_ge(mixed, n + 1)
                sp.dma_start(out[bass.ds(n * P, P), :], x_tile(n)).then_inc(outs, 16)
            loop(sp, tile)
            sp.wait_ge(outs, 16 * TILES)

        @block.tensor
        def _(pe):
            mm, tr = nc.tensor.matmul, nc.tensor.transpose
            for n in range(TILES):
                last = tr(ps_l[:, n * NE:(n + 1) * NE], logitT[0:NE, n * P:(n + 1) * P], ident[0:NE, 0:NE])
            last.then_inc(pe_s, 1)
            pe.wait_ge(dv, 12)
            pe.wait_ge(ld, 96)
            h2 = hot[:].rearrange("p n e -> p (n e)")
            mm(ps_t[:, 0:1], h2, ones[:, 0:1], start=True, stop=True).then_inc(pe_s, 1)
            mm(ps_r[:, 0:P], before[:], h2, start=True, stop=False)
            pe.wait_ge(dv, 14)
            mm(ps_r[:, 0:P], totals[:], later[:], start=False, stop=True).then_inc(pe_s, 1)
            pe.wait_ge(order_in, 16)
            tr(ps_d[:, 0:TILES], ord_t[:], ident[0:TILES, 0:TILES]).then_inc(pe_s, 1)

            def turn(n, u, m):
                pe.wait_ge(fetched[u], 16 * (m + 1))
                wait(pe, xT_copied, n - 1)
                for k in range(KC):
                    last = tr(ps_x[u % 2][:, k * P:(k + 1) * P], xs[:, u, k * P:(k + 1) * P], ident[:])
                last.then_inc(pe_x, 1)

            def expert(n, u):
                pe.wait_ge(xT_copied, n + 1)
                wait(pe, biased, n - 1)
                for k in range(KC):
                    last = mm(ps_e[u % 2][:], xsT[:, u % 2, k], we[:, k], start=(k == 0), stop=(k == KC - 1))
                last.then_inc(pe_e, 1)

            def tile(n, u, m):
                turn(n, u, m)
                if not (isinstance(n, int) and n == 0):
                    expert(n - 1, (u - 1) % R)
            loop(pe, tile)
            expert(TILES - 1, R - 1)

        @block.scalar
        def _(act):
            act.wait_ge(dv, 3)
            nc.scalar.activation(ex[:], lg[:], ACT.Exp).then_inc(ac, 1)

            def tile(n, u, m):
                act.wait_ge(pe_x, n + 1)
                wait(act, pe_e, n - 1)
                nc.scalar.activation(xsT[:, u % 2], ps_x[u % 2][:].rearrange("p (k q) -> p k q", k=KC), ACT.Copy)\
                    .then_inc(xT_copied, 1)
            loop(act, tile)

        @block.gpsimd
        def _(pool):
            pool.wait_ge(dv, 16)
            for n in range(TILES):
                nc.gpsimd.indirect_dma_start(order_rows, bass.IndirectOffsetOnAxis(ap=rank_i[:, n:n + 1], axis=0),
                                             ids[:, n:n + 1], None).then_inc(sent, 16)
            pool.wait_ge(dv, 17)

            for n in range(TILES):
                wait(pool, fetched[n % R], 16 * (n // R))
                wait(pool, pe_x, n - R + 1)
                nc.gpsimd.indirect_dma_start(xs[:, n % R], None, xn_rows,
                                             bass.IndirectOffsetOnAxis(ap=order[:, n:n + 1], axis=0))\
                    .then_inc(fetched[n % R], 16)

        @block.vector
        def _(dve):
            V = nc.vector
            done = [0]

            def step(ins):
                done[0] += 1
                ins.then_inc(dv, 1)
                dve.wait_ge(dv, done[0])

            wide = lambda a: a[:].rearrange("p (n one) -> p n one", one=1).broadcast_to([P, TILES, NE])
            step(V.memset(ones[:], 1.0))
            dve.wait_ge(pe_s, 1)
            dve.wait_ge(ld, 96)
            lp = ps_l[:, 0:TILES * NE].rearrange("p (n e) -> p n e", e=NE)
            step(V.tensor_reduce(m1[:], lp, AX.X, ALU.max))
            step(V.tensor_tensor(lg[:], lp, wide(m1), ALU.subtract))
            dve.wait_ge(ac, 1)
            step(V.tensor_reduce(sm[:], ex[:], AX.X, ALU.add))
            step(V.reciprocal(ri[:], sm[:]))
            step(V.tensor_tensor(pr[:], ex[:], wide(ri), ALU.mult))
            step(V.tensor_reduce(best[:], pr[:], AX.X, ALU.max))
            step(V.tensor_tensor(far[:], pr[:], wide(best), ALU.is_lt))
            step(V.tensor_scalar(far[:], far[:], float(NE), None, ALU.mult))
            step(V.tensor_tensor(place[:], far[:], iota[:], ALU.add))
            step(V.tensor_reduce(first_[:], place[:], AX.X, ALU.min))
            step(V.tensor_tensor(hot[:], iota[:], wide(first_), ALU.is_equal))
            dve.wait_ge(pe_s, 2)
            step(V.tensor_copy(total[:], ps_t[:, 0:1]))
            step(V.tensor_scalar(totals[:], ones[:], total[:, 0:1], None, ALU.mult))
            dve.wait_ge(pe_s, 3)
            step(V.tensor_tensor(ranks[:], hot[:], ps_r[:, 0:P].rearrange("p (n e) -> p n e", e=NE), ALU.mult))
            V.tensor_reduce(rank[:], ranks[:], AX.X, ALU.add).then_inc(passed, 1)
            dve.wait_ge(passed, 1)
            step(V.tensor_copy(rank_i[:], rank[:]))
            dve.wait_ge(pe_s, 4)
            step(V.tensor_copy(order[:], ps_d[:, 0:TILES]))

            def tile(n, u, m):
                dve.wait_ge(pe_e, n + 1)
                wait(dve, mixed, n - 1)
                V.tensor_tensor(eo[:, u % 2], ps_e[u % 2][:], be[:], ALU.add).then_inc(biased, 1)
                dve.wait_ge(biased, n + 1)
                V.scalar_tensor_tensor(out=x_tile(n), in0=eo[:, u % 2], scalar=best[:, bass.ds(n, 1)], in1=x_tile(n),
                                       op0=ALU.mult, op1=ALU.add).then_inc(mixed, 1)
            loop(dve, tile)


def layers(nc, t, out):
    with ExitStack() as ctx:
        def sb(name, shape, dt=F32):
            return ctx.enter_context(nc.sbuf_tensor(name, shape, dt))

        x_sb = sb("x_sb", [P, TILES * D])
        big = sb("big", [P, KC, TOK])
        ident = sb("ident", [P, P])
        wh, cT, decay = sb("wh", [P, 2, RD]), sb("cT", [P, 2, TOK]), sb("decay", [P, 2, TB, S])
        started = ctx.enter_context(nc.semaphore("started"))
        with nc.Block() as block:
            @block.sync
            def _(sp):
                sp.dma_start(ident[:], t["identity"]).then_inc(started, 16)
                sp.wait_ge(started, 16)

        def semaphore(name):
            return ctx.enter_context(nc.semaphore(name))

        def buffers(scope, prefix):
            return {n: (scope.enter_context(nc.sbuf_tensor(prefix + n, [P, KC, D], F32)), semaphore(prefix + n + "_in"),
                        t[prefix + n]) for n in ("wq", "wk", "wv", "wo")}

        row = lambda a: a.rearrange("(one d) -> one d", one=1).broadcast_to([P, D])
        t["kpad"] = nc.dram_tensor("kpad", (CH, P + D), F32).ap()
        padded = semaphore("padded")
        toep_in = [semaphore("toep_in0"), semaphore("toep_in1")]
        cext_in = [semaphore("cext_in0"), semaphore("cext_in1")]
        gate_in = semaphore("gate_in")
        head_in = [semaphore("head_in0"), semaphore("head_in1")]
        with ExitStack() as conv_ctx:
            toep = conv_ctx.enter_context(nc.sbuf_tensor("toep", [P, 2, D], F32))
            cext = conv_ctx.enter_context(nc.sbuf_tensor("cext", [P, 2, KC, CEXT * B], F32))
            with ExitStack() as a_ctx:
                a_c = {"bq": t["bq"], "bk": row(t["bk"]), "bv": row(t["bv"]), "bo": row(t["bo"]),
                       "qcos": t["qcos"], "qsin": t["qsin"], "kcos": t["kcos"], "ksin": t["ksin"]}

                def first_heads(sp):
                    for h in range(2):
                        load_toep(sp, t, h, toep[:, h], toep_in[h])
                        load_cext(sp, t, h, cext[:, h], cext_in[h])
                attention(nc, True, x_sb, big, ident, a_c, t, buffers(a_ctx, "a_"), None, padded, first_heads)
            used = nc.released_uncleared_semaphores
            with nc.Block() as block:
                @block.gpsimd
                def _(pool):
                    pool.sem_clear(range(min(used), max(used) + 1))
            with ExitStack() as d_ctx:
                d_w = buffers(d_ctx, "d_")
                alibi = d_ctx.enter_context(nc.sbuf_tensor("alibi", [P, H, 3 * P], F32))
                with nc.sbuf_tensor("wg", [P, KC, 3 * VCH], F32) as wg:
                    def gates(sp):
                        sp.dma_start(wg[:], t["gate_w"]).then_inc(gate_in, 16)
                    convolution(nc, big, t, toep, cext, toep_in, cext_in, gates)

                    def projections(sp):
                        for buf, loaded, dram in d_w.values():
                            sp.dma_start(buf[:], dram).then_inc(loaded, 16)
                    router(nc, x_sb, big, ident, t, wg, gate_in, alibi, projections)
                def first_retention_heads(sp):
                    for h in range(2):
                        load_head(sp, t, h, wh[:, h], cT[:, h], decay[:, h], head_in[h])
                attention(nc, False, x_sb, big, ident, None, t, d_w, alibi, None, first_retention_heads)
        xn_rows = nc.dram_tensor("xn_rows", (TOK, D), F32).ap()
        order_rows = nc.dram_tensor("order_rows", (TOK, 1), F32).ap()
        mix_in, expert_in = semaphore("mix_in"), semaphore("expert_in")
        logitT = ctx.enter_context(nc.sbuf_tensor("logitT", [P, TOK], F32))
        o_sb = ctx.enter_context(nc.sbuf_tensor("o_sb", [P, TILES, D], F32))
        mix = [ctx.enter_context(nc.sbuf_tensor(n, shape, F32)) for n, shape in (
            ("wgate", [P, KC, D]), ("wout", [P, KC, D]), ("gamma", [P, KC]), ("beta", [P, KC]),
            ("wr", [P, KC, NE]), ("br", [P, 1]))]

        def mixing_weights(sp):
            wgate, wout, gamma, beta, wr, br = mix
            for dst, src in ((wgate[:], t["wgate"]), (wout[:], t["wout"]), (gamma[:], t["gn_gamma"]),
                             (beta[:], t["gn_beta"]), (wr[:], t["wr"]), (br[0:NE], t["br"])):
                sp.dma_start(dst, src).then_inc(mix_in, 16)
        retention(nc, big, t, o_sb, wh, cT, decay, head_in, mixing_weights)
        route = [ctx.enter_context(nc.sbuf_tensor(n, shape, F32)) for n, shape in (
            ("before", [P, P]), ("later", [P, P]), ("iota", [P, TILES, NE]), ("ids", [P, TILES]),
            ("we", [P, KC, D]), ("be", [P, D]))]

        def expert_weights(sp):
            before, later, iota, ids, we, be = route
            for dst, src in ((before[:], t["before"]), (later[:], t["later"]), (iota[:], t["iota"]),
                             (ids[:], t["ids"]), (we[:], t["we"]), (be[:], row(t["be"]))):
                sp.dma_start(dst, src).then_inc(expert_in, 16)
        mixing(nc, x_sb, big, ident, o_sb, mix, mix_in, logitT, xn_rows, expert_weights)
        experts(nc, x_sb, ident, route, expert_in, logitT, xn_rows, order_rows, out)


def laid_out(inputs):
    f = lambda n: np.asarray(inputs[n])
    chunks = lambda w: np.ascontiguousarray(w.reshape(KC, P, -1).transpose(1, 0, 2))
    halves = np.concatenate([np.arange(0, HD, 2), np.arange(1, HD, 2)])
    paired = (np.arange(H)[:, None] * HD + halves[None]).reshape(-1)
    a = {"x": f("x").reshape(TOK, D),
         "a_wq": chunks(f("L0_attn_Wq")[paired].T), "a_wk": chunks(f("L0_attn_Wk")[paired].T),
         "a_wv": chunks(f("L0_attn_Wv").T), "a_wo": chunks(f("L0_attn_Wo").T),
         "bq": np.ascontiguousarray(f("L0_attn_bq")[paired].reshape(G, P).T),
         "bk": np.ascontiguousarray(f("L0_attn_bk")[paired]), "bv": f("L0_attn_bv"), "bo": f("L0_attn_bo")}
    for n in "qkvo":
        a["d_w" + n] = chunks(f("L1_attn_W" + n).T)
    ctx = f("ctx_2048")
    rev = ctx.reshape(B, CH, CD, KC, P)[:, :, :, :, ::-1][:, :, np.arange(CEXT) % CD]
    a["ctx_rev"] = np.ascontiguousarray(rev.transpose(1, 4, 3, 2, 0).reshape(CH, P, KC, CEXT * B))
    a["conv_k"], a["conv_d"] = f("L0_xattn_ssm_kernel"), f("L0_xattn_D").reshape(CH, 1)
    a["gate_w"], a["gate_b"] = chunks(f("L0_ffn_gate_w").T), f("L0_ffn_gate_b")
    a["pool"] = np.ascontiguousarray(f("L0_ffn_vector_pool")[:, 16])
    a["wh"] = f("L1_xattn_Wh")
    a["ctxT"] = np.ascontiguousarray(ctx.reshape(TOK, RH, RD).transpose(1, 2, 0))
    a["wgate"], a["wout"] = chunks(f("L1_xattn_wg_w")), chunks(f("L1_xattn_wo_w"))
    a["gn_gamma"] = np.ascontiguousarray(f("L1_xattn_gn_gamma").reshape(KC, P).T)
    a["gn_beta"] = np.ascontiguousarray(f("L1_xattn_gn_beta").reshape(KC, P).T)
    a["wr"], a["br"] = chunks(f("L1_ffn_Wg")), f("L1_ffn_bg").reshape(NE, 1)
    a["we"], a["be"] = chunks(f("L1_ffn_We")), f("L1_ffn_be")
    a.update(shape_constants())
    return a


def shape_constants():
    f32 = np.float32
    theta = f32(1.0) / f32(10000.0) ** (np.arange(0, HD, 2, dtype=f32) / f32(HD))
    angle = np.arange(S, dtype=f32)[:, None] * theta[None]
    cos, sin = np.cos(angle).astype(f32), np.sin(angle).astype(f32)
    cos2, sin2 = np.concatenate([cos, cos], 1), np.concatenate([-sin, sin], 1)
    scale = f32(HD ** -0.5)
    kept = np.concatenate([np.arange(START), np.arange(S - RECENT, S)])
    c = {"qcos": np.tile(cos2.T * scale, (4, 1)), "qsin": np.tile(sin2.T * scale, (4, 1)),
         "kcos": cos2[kept], "ksin": sin2[kept], "identity": np.eye(P, dtype=f32)}
    k, q = np.arange(S)[None, :], np.arange(S)[:, None]
    rel = np.where(k <= q, k - q, -1e30)
    c["rel"] = np.concatenate([rel[0:P, 0:P], rel[P:S]], 1)
    slope = f32(0.5) ** (np.arange(1, H + 1, dtype=f32) * f32(8.0) / f32(H))
    c["slope"] = np.tile(slope[None], (P, 1))
    gam = f32(1.0) - f32(2.0) ** (f32(-5.0) - np.arange(RH, dtype=f32))
    expo = (k - q).astype(f32)
    dm = np.where(expo[None] <= 0, gam[:, None, None] ** expo[None], f32(0))
    dm = dm / np.sqrt(dm.sum(-1, dtype=f32))[:, None, :] / np.sqrt(f32(RD))
    c["decay"] = dm.transpose(0, 2, 1).reshape(RH, TB, P, S).transpose(0, 2, 1, 3)
    i = np.arange(P)
    c["before"] = (i[:, None] < i[None]).astype(f32)
    ne = (i % NE) * TILES + i // NE
    c["later"] = (ne[:, None] < ne[None]).astype(f32)
    c["iota"] = np.broadcast_to(np.arange(NE, dtype=f32), (P, TILES, NE))
    c["ids"] = (np.arange(TILES)[None] * P + i[:, None]).astype(f32)
    return {k: np.ascontiguousarray(a.astype(f32)) for k, a in c.items()}


def kernel(**inputs):
    import concourse.bacc as _bacc
    from concourse.bass_utils import run_bass_kernel_spmd as _run

    nc = _bacc.Bacc("TRN2", target_bir_lowering=False, num_devices=1)
    arrays, t = {}, {}
    for name, a in laid_out(inputs).items():
        arrays[name + "_dram"] = a
        t[name] = nc.dram_tensor(name + "_dram", a.shape, mybir.dt.from_np(a.dtype), kind="ExternalInput").ap()
    out = nc.dram_tensor("out_dram", (TOK, D), F32, kind="ExternalOutput").ap()
    layers(nc, t, out)
    r = _run(nc, [arrays], core_ids=[0])
    return r.results[0]["out_dram"].reshape(B, S, D)
```

```python
from contextlib import ExitStack

import concourse.bass as bass
from concourse import mybir
import numpy as np

P = 128
B, S, D = 8, 256, 512
TOK = B * S
TILES = TOK // P
TB = S // P
KC = D // P
H, HD = 16, 32
G = H // 4
LN_EPS = 1e-5
START = -(-S // 10)
RECENT = -(-S // 4)
NKEY = START + RECENT

CH = 32
CD = S // CH
NDEL = 5
CEXT = 12
CW = CD * B
NV = 1250
NG = NV + 1
VCH = 418
NC = 3 * VCH
RH, RD = 4, 128
GN_EPS = 1e-3
NE = 8

F32 = mybir.dt.float32
F32R = mybir.dt.float32r
BF16 = mybir.dt.bfloat16
U32 = mybir.dt.uint32
I32 = mybir.dt.int32
ALU = mybir.AluOpType
ACT = mybir.ActivationFunctionType
AX = mybir.AxisListType
SWAP16 = [(i + 16) % 32 for i in range(32)]


def wait(eng, sem, value):
    if isinstance(value, int) and value <= 0:
        return
    eng.wait_ge(sem, value)


def wait_apart(eng, sem, value, passed):
    eng.wait_ge(sem, value)
    eng.sem_inc(passed, 1)


def split_product(nc, out, lhs, rhs, start, stop):
    nc.tensor.matmul(out, lhs[0], rhs[0], start=start, stop=False)
    nc.tensor.matmul(out, lhs[0], rhs[1], start=False, stop=False)
    return nc.tensor.matmul(out, lhs[1], rhs[0], start=False, stop=stop)


def attention(nc, first_layer, x_sb, big, ident, consts, t, wv, ld_v, alibi, padded, ahead):
    A = first_layer
    pre = "a_" if A else "d_"
    NQ = NKEY if A else S
    with ExitStack() as ctx:
        def sb(name, shape, dt=F32):
            return ctx.enter_context(nc.sbuf_tensor(pre + name, shape, dt))

        def sem(name):
            return ctx.enter_context(nc.semaphore(pre + name))

        parts = ("wq", "wo") if A else ("wk", "wq", "wo")
        high = {n: sb(n + "_high", [P, KC, D], F32R) for n in parts}
        low = {n: sb(n + "_low", [P, KC, D], F32R) for n in parts}
        raw = {n: big[:, i].rearrange("p (k d) -> p k d", k=KC) for i, n in enumerate(parts)}
        ld_q, ld_k, ld_o = sem("ld_q"), sem("ld_k"), sem("ld_o")
        if A:
            wk = sb("wk", [P, KC, D])
        xn = sb("xn", [P, TB, D])
        xnT = sb("xnT", [P, KC, S])
        xnT_high, xnT_low = sb("xnT_high", [P, KC, S], F32R), sb("xnT_low", [P, KC, S], F32R)
        qT = sb("qT", [P, G, S])
        kD = sb("kD", [P, G, 4, NQ])
        v = sb("v", [P, 1 if A else TB, D])
        PW = TB * P if A else 3 * P
        prob = sb("prob", [P, 2, 4, PW])
        probT = sb("probT", [P, 4, S])
        probT1 = None if A else sb("probT1", [P, 4, P])
        oT_high, oT_low = sb("oT_high", [P, G, S], F32R), sb("oT_low", [P, G, S], F32R)
        xo = xn
        nmax = sb("nmax", [P, 2, 8])
        mx = sb("mx", [P, 2, 8])
        rsum = sb("rsum", [P, 2, 8])
        rinv = sb("rinv", [P, 2, 8])
        st = sb("st", [P, 2, TB, 6])
        mv = sb("mv", [P, 2, TB, 2])
        ve = sb("ve", [P, 2, TB])
        rstd = sb("rstd", [P, 2, TB])
        mhalf = sb("mhalf", [P, TB])
        if A:
            xkT = sb("xkT", [P, KC, NKEY])
            bq = sb("bq", [P, G])
            bk, bv, bo = (sb(n, [P, D]) for n in ("bk", "bv", "bo"))
            qcos, qsin = sb("qcos", [P, S]), sb("qsin", [P, S])
            kcos, ksin = sb("kcos", [P, HD]), sb("ksin", [P, HD])
            qraw, qsw, qm1, qm2 = (sb(n, [P, S]) for n in ("qraw", "qsw", "qm1", "qm2"))
            kraw, km1, km2, krope = (sb(n, [P, D]) for n in ("kraw", "km1", "km2", "krope"))
            kz = sb("kz", [CH, P + D])
            dk = sb("dk", [CH, 1])

        bank = [ctx.enter_context(nc.psum_tensor(f"{pre}bank{i}", [P, 512], F32)) for i in range(2 if A else 3)]
        ps_s = ctx.enter_context(nc.psum_tensor(pre + "ps_s", [P, 4 if A else 3, 512], F32))
        ps_t = ctx.enter_context(nc.psum_tensor(pre + "ps_t", [P, 2, 512], F32))

        ld_x0, ld_x, ld_i = sem("ld_x0"), sem("ld_x"), sem("ld_i")
        ld_kc, ld_qc, ld_b = sem("ld_kc"), sem("ld_qc"), sem("ld_b")
        stats, lnvar, lnrstd, normed = sem("stats"), sem("lnvar"), sem("lnrstd"), sem("normed")
        ostats, olnvar, olnrstd, onormed = sem("ostats"), sem("olnvar"), sem("olnrstd"), sem("onormed")
        aggr, oaggr = sem("aggr"), sem("oaggr")
        pe_xT, pe_q, pe_k, pe_v, pe_s = sem("pe_xT"), sem("pe_q"), sem("pe_k"), sem("pe_v"), sem("pe_s")
        pe_t, pe_pv, pe_o, pe_oT = sem("pe_t"), sem("pe_pv"), sem("pe_o"), sem("pe_oT")
        xT_copied, q_copied, q_ready = sem("xT_copied"), sem("q_copied"), sem("q_ready")
        k_act, k_dve, v_copied = sem("k_act"), sem("k_dve"), sem("v_copied")
        maxed, negated, exped, summed, scaled = (sem("maxed"), sem("negated"), sem("exped"),
                                                 sem("summed"), sem("scaled"))
        pT_act, pT_dve, pv_copied = sem("pT_act"), sem("pT_dve"), sem("pv_copied")
        pv_low, xT_low = sem("pv_low"), sem("xT_low")
        w_high = {n: sem(n + "_high") for n in parts}
        w_low = {n: sem(n + "_low") for n in parts}
        x_added, x_biased, oT_copied = sem("x_added"), sem("x_biased"), sem("oT_copied")
        zeroed, setup = sem("zeroed"), sem("setup")
        passed_dve, passed_pool = sem("passed_dve"), sem("passed_pool")
        if A:
            pe_kn, kn_copied, k_mul, k_rope = sem("pe_kn"), sem("kn_copied"), sem("k_mul"), sem("k_rope")
            q_swap, q_cos, q_sin, xk_ready = sem("q_swap"), sem("q_cos"), sem("q_sin"), sem("xk_ready")
            ld_taps, tapped = sem("ld_taps"), sem("tapped")

        block = ctx.enter_context(nc.Block())

        def xt(b, t):
            return x_sb[:, bass.ds((b * TB + t) * D, D)]

        def low_part(eng, n):
            for k in range(KC):
                eng.wait_ge(w_high[n], k + 1)
                eng.tensor_tensor(low[n][:, k], raw[n][:, k], high[n][:, k].bitcast(F32), ALU.subtract)\
                    .then_inc(w_low[n], 1)

        def proj_of(b, g):
            return (b, g + 2, 4 * b + g + 2) if g < 2 else (b + 1, g - 2, 4 * b + g + 2)

        @block.sync
        def _(sp):
            if A:
                xr = t["x"].rearrange("(t p) d -> p t d", p=P)
                xs = x_sb[:].rearrange("p (t d) -> p t d", d=D)
                sp.dma_start(xs[:, 0:TB], xr[:, 0:TB]).then_inc(ld_x0, 16)
                sp.dma_start(ident[:], t["identity"]).then_inc(ld_i, 16)
                sp.dma_start(wk[:], t["a_wk"]).then_inc(ld_k, 16)
                sp.dma_start(bk[:], consts["bk"]).then_inc(ld_kc, 16)
                sp.dma_start(kcos[0:NKEY], consts["kcos"]).then_inc(ld_kc, 16)
                sp.dma_start(ksin[0:NKEY], consts["ksin"]).then_inc(ld_kc, 16)
                sp.dma_start(raw["wq"], t["a_wq"]).then_inc(ld_q, 16)
                sp.dma_start(bq[:], consts["bq"]).then_inc(ld_q, 16)
                sp.dma_start(qcos[:], consts["qcos"]).then_inc(ld_qc, 16)
                sp.dma_start(qsin[:], consts["qsin"]).then_inc(ld_qc, 16)
                sp.dma_start(wv[:], t["a_wv"]).then_inc(ld_v, 16)
                sp.dma_start(bv[:], consts["bv"]).then_inc(ld_b, 16)
                sp.dma_start(bo[:], consts["bo"]).then_inc(ld_b, 16)
                for b in range(1, B):
                    sp.dma_start(xs[:, b * TB:(b + 1) * TB], xr[:, b * TB:(b + 1) * TB]).then_inc(ld_x, 16)
                    if b == 1:
                        sp.dma_start(raw["wo"], t["a_wo"]).then_inc(ld_o, 16)
                sp.dma_start(dk[:], t["conv_d"]).then_inc(ld_taps, 16)
                sp.wait_ge(tapped, 1)
                sp.dma_start(kz[:, P:], t["conv_k"]).then_inc(ld_taps, 16)
                sp.wait_ge(tapped, 2)
                sp.dma_start(t["kpad"], kz[:]).then_inc(padded, 16)
                sp.wait_ge(padded, 16)
                ahead(sp)
            else:
                for n, loaded in (("wk", ld_k), ("wq", ld_q), ("wo", ld_o)):
                    sp.dma_start(raw[n], t["d_" + n]).then_inc(loaded, 16)

        @block.gpsimd
        def _(pool):
            def rstd_of(b, mv_, ve_, rstd_, got, done1, done2):
                wait_apart(pool, got, b + 1, passed_pool)
                nc.gpsimd.tensor_scalar(ve_, mv_[:, :, 1], LN_EPS, None, ALU.add).then_inc(done1, 1)
                pool.wait_ge(done1, b + 1)
                nc.gpsimd.tensor_tensor(rstd_, ve_, mhalf[:], ALU.pow).then_inc(done2, 1)

            def ln_in(b):
                rstd_of(b, mv[:, 0], ve[:, 0], rstd[:, 0], aggr, lnvar, lnrstd)

            def ln_out(b):
                rstd_of(b, mv[:, 1], ve[:, 1], rstd[:, 1], oaggr, olnvar, olnrstd)

            def scale_probs(n, g):
                pool.wait_ge(summed, n + 1)
                pr = prob[:, g % 2]
                iv = rinv[:, g % 2]
                if A:
                    pr = pr.rearrange("p j (t k) -> p j t k", t=TB)[:, :, :, 0:NKEY]
                    iv = iv.rearrange("p (t j one) -> p j t one", t=TB, one=1).broadcast_to([P, 4, TB, NKEY])
                    nc.gpsimd.tensor_tensor(pr, pr, iv, ALU.mult).then_inc(scaled, 1)
                else:
                    i0 = iv[:, 0:4].rearrange("p (j one) -> p j one", one=1).broadcast_to([P, 4, P])
                    i1 = iv[:, 4:8].rearrange("p (j one) -> p j one", one=1).broadcast_to([P, 4, 2 * P])
                    nc.gpsimd.tensor_tensor(pr[:, :, 0:P], pr[:, :, 0:P], i0, ALU.mult)
                    nc.gpsimd.tensor_tensor(pr[:, :, P:], pr[:, :, P:], i1, ALU.mult).then_inc(scaled, 1)

            def q_times_cos(n):
                pool.wait_ge(q_copied, n + 1)
                wait(pool, q_ready, n)
                nc.gpsimd.tensor_tensor(qm1[:], qraw[:], qcos[:], ALU.mult).then_inc(q_cos, 1)

            def kept_keys(b):
                wait_apart(pool, xT_copied, TB * (b + 1), passed_pool)
                nc.gpsimd.tensor_copy(xkT[:, :, 0:START], xnT[:, :, 0:START])
                nc.gpsimd.tensor_copy(xkT[:, :, START:], xnT[:, :, S - RECENT:]).then_inc(xk_ready, 1)

            def k_rotate(b):
                pool.wait_ge(kn_copied, b + 1)
                kv3 = lambda t: t[0:NKEY].rearrange("p (h f) -> p h f", f=HD)
                tb = lambda t, a, z: t[0:NKEY, a:z].rearrange("p (one f) -> p one f", one=1).broadcast_to(
                    [NKEY, H, z - a])
                nc.gpsimd.tensor_tensor(kv3(km1), kv3(kraw), tb(kcos, 0, HD), ALU.mult)
                nc.gpsimd.tensor_tensor(kv3(km2)[:, :, 0:16], kv3(kraw)[:, :, 16:32], tb(ksin, 0, 16), ALU.mult)
                nc.gpsimd.tensor_tensor(kv3(km2)[:, :, 16:32], kv3(kraw)[:, :, 0:16], tb(ksin, 16, 32),
                                        ALU.mult).then_inc(k_mul, 1)
                pool.wait_ge(k_mul, b + 1)
                nc.gpsimd.tensor_tensor(krope[0:NKEY], km1[0:NKEY], km2[0:NKEY], ALU.add).then_inc(k_rope, 1)

            def add_bo(b):
                pool.wait_ge(normed, b + 1)
                nc.gpsimd.tensor_tensor(xt(b, 0), xt(b, 0), bo[:], ALU.add)
                nc.gpsimd.tensor_tensor(xt(b, 1), xt(b, 1), bo[:], ALU.add).then_inc(x_biased, 1)

            nc.gpsimd.memset(mhalf[:], -0.5).then_inc(setup, 1)
            pool.wait_ge(setup, 1)
            if A:
                nc.gpsimd.memset(kz[:], 0.0).then_inc(tapped, 1)
            ln_in(0)
            if not A:
                nc.gpsimd.memset(kD[:], 0.0).then_inc(zeroed, 1)
                low_part(pool, "wo")
            if A:
                kept_keys(0)
                pool.wait_ge(ld_kc, 16 * 3)
                k_rotate(0)
                pool.wait_ge(ld_qc, 16 * 2)
                for n in range(2):
                    q_times_cos(n)
                pool.wait_ge(ld_b, 16 * 2)
                add_bo(0)

            def slot(b, g, first, last):
                n = 4 * b + g
                if g == 0 and not last:
                    ln_in(b + 1)
                if A and not last:
                    if g == 2:
                        kept_keys(b + 1)
                    if g == 3:
                        k_rotate(b + 1)
                if g == 2 and not first:
                    ln_out(b - 1)
                scale_probs(n, g)
                if A and (g < 2 or not last):
                    q_times_cos(proj_of(b, g)[2])
                if A and not last and g == 3:
                    add_bo(b + 1)

            def batch(b, first=False, last=False):
                for g in range(G):
                    slot(b, g, first, last)

            batch(0, first=True)
            if A:
                pool.wait_ge(ld_taps, 32)
                pool.wait_ge(tapped, 1)
                nc.gpsimd.tensor_tensor(kz[:, P:P + 1], kz[:, P:P + 1], dk[:], ALU.add).then_inc(tapped, 1)
            with pool.Fori(1, B - 1) as b:
                batch(b)
            batch(B - 1, last=True)
            ln_out(B - 1)

        @block.vector
        def _(dve):
            def ln_stats(b, i, got, agg):
                if not isinstance(b, int):
                    dve.sem_inc(passed_dve, 1)
                for t in range(TB):
                    last = nc.vector.bn_stats(st[:, i, t], xt(b, t))
                last.then_inc(got, 1)
                wait_apart(dve, got, b + 1, passed_dve)
                for t in range(TB):
                    last = nc.vector.bn_aggr(mv[:, i, t], st[:, i, t])
                last.then_inc(agg, 1)

            def ln_apply(b, i, got, out, done):
                dve.wait_ge(got, b + 1)
                for t in range(TB):
                    last = nc.vector.tensor_scalar(out[:, t], xt(b, t), mv[:, i, t, 0:1], rstd[:, i, t:t + 1],
                                                   ALU.subtract, ALU.mult)
                last.then_inc(done, 1)

            def ln_in(b):
                ln_stats(b, 0, stats, aggr)

            def ln_in_apply(b):
                wait(dve, pe_xT, TB * b)
                if not (isinstance(b, int) and b < 3):
                    dve.wait_ge(pe_oT, TB * (b - 2))
                ln_apply(b, 0, lnrstd, xn, normed)

            def ln_out(b):
                ln_stats(b, 1, ostats, oaggr)

            def ln_out_apply(b):
                wait(dve, pe_oT, TB * b)
                dve.wait_ge(pe_xT, TB * (b + 2 if not isinstance(b, int) else min(b + 3, B)))
                ln_apply(b, 1, olnrstd, xo, onormed)

            def max_scores(n, g):
                dve.wait_ge(pe_s, n + 1 if A else 3 * n + 1)
                wait(dve, exped, n - 1)
                wait(dve, pe_t, n - 1)
                if not A:
                    dve.sem_inc(passed_dve, 1)
                if A:
                    nc.vector.tensor_reduce(mx[:, g % 2].rearrange("p (t j) -> p t j", t=TB),
                                            ps_s[:, 2 * (g % 2):2 * (g % 2) + TB, 0:4 * NKEY]
                                            .rearrange("p t (j k) -> p t j k", j=4),
                                            AX.X, ALU.max).then_inc(maxed, 1)
                else:
                    for j in range(4):
                        nc.vector.tensor_tensor_reduce(
                            out=prob[:, g % 2, j, 0:P], in0=ps_s[:, 0, j * P:(j + 1) * P],
                            in1=alibi[:, 4 * g + j, P:], scale=1.0, scalar=-3e38, op0=ALU.add, op1=ALU.max,
                            accum_out=mx[:, g % 2, j:j + 1])
                    for j in range(4):
                        if j % 2 == 0:
                            dve.wait_ge(pe_s, 3 * n + 2 + j // 2)
                            dve.sem_inc(passed_dve, 1)
                        last = nc.vector.tensor_tensor_reduce(
                            out=prob[:, g % 2, j, P:3 * P],
                            in0=ps_s[:, 1 + j // 2, (j % 2) * S:(j % 2) * S + S],
                            in1=alibi[:, 4 * g + j], scale=1.0, scalar=-3e38, op0=ALU.add, op1=ALU.max,
                            accum_out=mx[:, g % 2, 4 + j:5 + j])
                    last.then_inc(maxed, 1)
                dve.wait_ge(maxed, n + 1)
                nc.vector.tensor_scalar(nmax[:, g % 2], mx[:, g % 2], -1.0, None, ALU.mult).then_inc(negated, 1)

            def turn_copy(n):
                dve.wait_ge(pe_t, n + 1)
                nc.vector.tensor_copy(probT[:, 0:2], ps_t[:, 0].rearrange("p (j q) -> p j q", j=2)).then_inc(pT_dve, 1)

            def reciprocals(n, g):
                dve.wait_ge(exped, n + 1)
                wait(dve, scaled, n - 1)
                nc.vector.reciprocal(rinv[:, g % 2], rsum[:, g % 2]).then_inc(summed, 1)

            def q_rotate(n, g):
                wait_apart(dve, q_copied, n + 1, passed_dve)
                nc.vector.stream_shuffle(qsw[:], qraw[:], SWAP16).then_inc(q_swap, 1)
                dve.wait_ge(q_swap, n + 1)
                nc.vector.tensor_tensor(qm2[:], qsw[:], qsin[:], ALU.mult).then_inc(q_sin, 1)
                dve.wait_ge(q_sin, n + 1)
                dve.wait_ge(q_cos, n + 1)
                nc.vector.tensor_tensor(qT[:, g], qm1[:], qm2[:], ALU.add).then_inc(q_ready, 1)

            def k_copy(n, g):
                dve.wait_ge(pe_k, n + 1)
                for j in (0, 1):
                    last = nc.vector.tensor_copy(kD[32 * j:32 * j + 32, g, j], bank[1][32 * j:32 * j + 32, 0:S])
                last.then_inc(k_dve, 1)

            def k_copy_a(b):
                dve.wait_ge(pe_k, b + 1)
                for j in (0, 1):
                    last = nc.vector.tensor_copy(kD[32 * j:32 * j + 32, :, j],
                                                 bank[1][32 * j:32 * j + 32, 0:4 * NKEY]
                                                 .rearrange("p (g k) -> p g k", g=G))
                last.then_inc(k_dve, 1)

            def kn_copy(b):
                dve.wait_ge(pe_kn, b + 1)
                wait(dve, k_mul, b)
                nc.vector.tensor_tensor(kraw[0:NKEY], bank[1][0:NKEY, :], bk[0:NKEY], ALU.add)\
                    .then_inc(kn_copied, 1)

            def v_copy(n, g):
                dve.wait_ge(pe_v, n + 1)
                c = slice(g * P, g * P + P)
                if A:
                    nc.vector.tensor_tensor(v[0:NKEY, 0, c], bank[1][0:NKEY, 0:P], bv[0:NKEY, c], ALU.add)\
                        .then_inc(v_copied, 1)
                else:
                    nc.vector.tensor_copy(v[:, :, c], bank[1][:, 0:TB * P].rearrange("p (t f) -> p t f", t=TB))\
                        .then_inc(v_copied, 1)

            def pv_low_part(n, g):
                dve.wait_ge(pv_copied, n + 1)
                nc.vector.tensor_tensor(oT_low[:, g], bank[0][:, 0:S], oT_high[:, g].bitcast(F32), ALU.subtract)\
                    .then_inc(pv_low, 1)

            def xT_low_part(b):
                for t in range(TB):
                    dve.wait_ge(xT_copied, TB * b + t + 1)
                    c = slice(t * P, (t + 1) * P)
                    nc.vector.tensor_tensor(xnT_low[:, :, c], bank[t][:].rearrange("p (k q) -> p k q", k=KC),
                                            xnT_high[:, :, c].bitcast(F32), ALU.subtract).then_inc(xT_low, 1)

            def add_out(b, t):
                if A and t == 0:
                    dve.wait_ge(x_biased, b + 1)
                dve.wait_ge(pe_o, TB * b + t + 1)
                nc.vector.tensor_tensor(xt(b, t), xt(b, t), ps_t[:, t], ALU.add).then_inc(x_added, 1)

            if A:
                nc.vector.memset(kD[:], 0.0).then_inc(zeroed, 1)
                nc.vector.memset(prob[:], 0.0).then_inc(zeroed, 1)
                nc.vector.memset(v[:], 0.0).then_inc(zeroed, 1)
                dve.wait_ge(zeroed, 3)
                dve.wait_ge(ld_x0, 16)
            ln_in(0)
            ln_in_apply(0)
            if not A:
                low_part(dve, "wk")
            xT_low_part(0)
            if not A:
                low_part(dve, "wq")
                dve.wait_ge(zeroed, 1)
            if A:
                low_part(dve, "wq")
                dve.wait_ge(ld_kc, 16 * 3)
                kn_copy(0)
                dve.wait_ge(ld_b, 16 * 2)
            for g in range(2):
                if not A:
                    k_copy(g, g)
                v_copy(g, g)
            if A:
                k_copy_a(0)
                dve.wait_ge(ld_qc, 16 * 2)
                q_rotate(0, 0)
                low_part(dve, "wo")
                dve.wait_ge(ld_x, 16 * (B - 1))

            def slot(b, g, first, last):
                n = 4 * b + g
                _, pg, pn = proj_of(b, g)
                project = g < 2 or not last
                max_scores(n, g)
                if not (first and g < 2):
                    pv_low_part(n - 2, (g - 2) % 4)
                if A and not (g == 3 and last):
                    q_rotate(n + 1, (g + 1) % 4)
                if project and not A:
                    k_copy(pn, pg)
                if g == 0 and not last:
                    ln_in(b + 1)
                if g == 2 and not first:
                    add_out(b - 1, 1)
                if project:
                    v_copy(pn, pg)
                if g == 3 and not first:
                    ln_out_apply(b - 1)
                if g == 1 and not first:
                    add_out(b - 1, 0)
                if g == 2 and not first:
                    dve.wait_ge(x_added, TB * b)
                    ln_out(b - 1)
                if g in (1, 2):
                    reciprocals(n, g)
                if g == 1 and not last:
                    xT_low_part(b + 1)
                if A and not last and g == 2:
                    kn_copy(b + 1)
                if A and not last and g == 3:
                    k_copy_a(b + 1)
                if not (first and g == 0):
                    turn_copy(n - 1)
                if g not in (1, 2):
                    reciprocals(n, g)
                if g == 0 and not last:
                    ln_in_apply(b + 1)

            def batch(b, first=False, last=False):
                for g in range(G):
                    slot(b, g, first, last)

            batch(0, first=True)
            with dve.Fori(1, B - 1) as b:
                batch(b)
            batch(B - 1, last=True)
            pv_low_part(4 * B - 2, 2)
            turn_copy(4 * B - 1)
            pv_low_part(4 * B - 1, 3)
            for t in range(TB):
                add_out(B - 1, t)
            dve.wait_ge(x_added, TB * B)
            ln_out(B - 1)
            ln_out_apply(B - 1)

        @block.scalar
        def _(act):
            nc.scalar.preload_act_table(ACT.Exp)
            def xT_copy(b):
                for t in range(TB):
                    act.wait_ge(pe_xT, TB * b + t + 1)
                    c, src = slice(t * P, (t + 1) * P), bank[t][:].rearrange("p (k q) -> p k q", k=KC)
                    nc.scalar.activation(xnT_high[:, :, c], src, ACT.Copy)
                    nc.scalar.activation(xnT[:, :, c], src, ACT.Copy).then_inc(xT_copied, 1)

            def q_copy(n, g):
                act.wait_ge(pe_q, n + 1)
                if A:
                    wait(act, q_swap, n)
                    wait(act, q_cos, n)
                    nc.scalar.activation(qraw[:], bank[0][:, 0:S], ACT.Identity, bias=bq[:, g:g + 1])\
                        .then_inc(q_copied, 1)
                else:
                    nc.scalar.activation(qT[:, g], bank[0][:, 0:S], ACT.Copy, scale=float(HD) ** -0.5)\
                        .then_inc(q_copied, 1)

            def k_copy(n, g):
                act.wait_ge(pe_k, n + 1)
                for j in (2, 3):
                    last = nc.scalar.activation(kD[32 * j:32 * j + 32, g, j], bank[1][32 * j:32 * j + 32, 0:S],
                                                ACT.Copy)
                last.then_inc(k_act, 1)

            def k_copy_a(b):
                act.wait_ge(pe_k, b + 1)
                for j in (2, 3):
                    last = nc.scalar.activation(kD[32 * j:32 * j + 32, :, j],
                                                bank[1][32 * j:32 * j + 32, 0:4 * NKEY]
                                                .rearrange("p (g k) -> p g k", g=G), ACT.Copy)
                last.then_inc(k_act, 1)

            def exponentials(n, g):
                act.wait_ge(negated, n + 1)
                wait(act, summed, n - 1)
                for j in range(4):
                    for t in range(TB):
                        c = t * 4 + j
                        if A:
                            out = prob[:, g % 2, j, t * P:t * P + NKEY]
                            src = ps_s[:, 2 * (g % 2) + t, j * NKEY:(j + 1) * NKEY]
                        else:
                            src = out = prob[:, g % 2, j, 0:P] if t == 0 else prob[:, g % 2, j, P:3 * P]
                        last = nc.scalar.activation(out, src, ACT.Exp, bias=nmax[:, g % 2, c:c + 1],
                                                    accum_out=rsum[:, g % 2, c:c + 1])
                last.then_inc(exped, 1)

            def turn_copy(n):
                act.wait_ge(pe_t, n + 1)
                last = nc.scalar.activation(probT[:, 2:4], ps_t[:, 1].rearrange("p (j q) -> p j q", j=2), ACT.Copy)
                if not A:
                    last = nc.scalar.activation(probT1[:], bank[2][:].rearrange("p (j q) -> p j q", j=4), ACT.Copy)
                last.then_inc(pT_act, 1)

            def pv_copy(n, g):
                act.wait_ge(pe_pv, n + 1)
                nc.scalar.activation(oT_high[:, g], bank[0][:, 0:S], ACT.Copy).then_inc(pv_copied, 1)

            def oT_copy(b):
                for t in range(TB):
                    act.wait_ge(pe_oT, TB * b + t + 1)
                    src = bank[t][:].rearrange("p (k q) -> p k q", k=KC)
                    if A:
                        dst = big[:, :, bass.ds(b + t * P * B, P, step=B)] if isinstance(b, int) else \
                            big[:].rearrange("p k (q b) -> p k q b", b=B)[:, :, t * P:(t + 1) * P, bass.ds(b, 1)]
                        if not isinstance(b, int):
                            src = src.rearrange("p k (q one) -> p k q one", one=1)
                    else:
                        dst = big[:, :, bass.ds(b * S + t * P, P)]
                    nc.scalar.activation(dst, src, ACT.Copy).then_inc(oT_copied, 1)

            def high_part(n, loaded, count):
                act.wait_ge(loaded, count)
                for k in range(KC):
                    nc.scalar.activation(high[n][:, k], raw[n][:, k], ACT.Copy).then_inc(w_high[n], 1)

            if not A:
                high_part("wk", ld_k, 16)
            xT_copy(0)
            high_part("wq", ld_q, 32 if A else 16)
            act.wait_ge(zeroed, 3 if A else 1)
            for g in range(2):
                q_copy(g, g)
                if not A:
                    k_copy(g, g)
            if A:
                k_copy_a(0)
            high_part("wo", ld_o, 16)

            def slot(b, g, first, last):
                n = 4 * b + g
                _, pg, pn = proj_of(b, g)
                if not (first and g < 2):
                    pv_copy(n - 2, (g - 2) % 4)
                if A:
                    exponentials(n, g)
                if g < 2 or not last:
                    if not A:
                        k_copy(pn, pg)
                    q_copy(pn, pg)
                if not A:
                    exponentials(n, g)
                if g == 1 and not last:
                    xT_copy(b + 1)
                if A and g == 3 and not last:
                    k_copy_a(b + 1)
                if not (first and g == 0):
                    turn_copy(n - 1)
                if g == 3 and not first:
                    oT_copy(b - 1)

            def batch(b, first=False, last=False):
                for g in range(G):
                    slot(b, g, first, last)

            batch(0, first=True)
            with act.Fori(1, B - 1) as b:
                batch(b)
            batch(B - 1, last=True)
            pv_copy(4 * B - 2, 2)
            turn_copy(4 * B - 1)
            pv_copy(4 * B - 1, 3)
            oT_copy(B - 1)

        @block.tensor
        def _(pe):
            mm, tr = nc.tensor.matmul, nc.tensor.transpose

            def turn_x(b, src, ready, done, copied):
                pe.wait_ge(ready, b + 1)
                for t in range(TB):
                    for k in range(KC):
                        last = tr(bank[t][:, k * P:(k + 1) * P], src[:, t, k * P:(k + 1) * P], ident[:])
                    last.then_inc(done, 1)

            def parts_of(n, k, c):
                return high[n][:, k, c], low[n][:, k, c]

            def project_q(n, g):
                c = slice(g * P, (g + 1) * P)
                for k in range(KC):
                    last = split_product(nc, bank[0][:, 0:S], parts_of("wq", k, c), (xnT_high[:, k], xnT_low[:, k]),
                                         k == 0, k == KC - 1)
                last.then_inc(pe_q, 1)

            def project_k(n, g):
                c = slice(g * P, (g + 1) * P)
                for k in range(KC):
                    last = split_product(nc, bank[1][:, 0:S], parts_of("wk", k, c), (xnT_high[:, k], xnT_low[:, k]),
                                         k == 0, k == KC - 1)
                last.then_inc(pe_k, 1)

            def project_kn(b):
                for k in range(KC):
                    last = mm(bank[1][0:NKEY, :], xkT[:, k], wk[:, k], start=(k == 0), stop=(k == KC - 1))
                last.then_inc(pe_kn, 1)

            def turn_k(b):
                pe.wait_ge(k_rope, b + 1)
                for g in range(G):
                    last = tr(bank[1][:, g * NKEY:(g + 1) * NKEY], krope[0:NKEY, g * P:(g + 1) * P],
                              ident[0:NKEY, 0:NKEY])
                last.then_inc(pe_k, 1)

            def project_v(n, g):
                c = slice(g * P, (g + 1) * P)
                for t in range(1 if A else TB):
                    out = bank[1][0:NKEY, 0:P] if A else bank[1][:, t * P:(t + 1) * P]
                    for k in range(KC):
                        lhs = xkT[:, k] if A else xnT[:, k, t * P:(t + 1) * P]
                        last = mm(out, lhs, wv[:, k, c], start=(k == 0), stop=(k == KC - 1))
                last.then_inc(pe_v, 1)

            def scores(n, g):
                if A:
                    for t in range(TB):
                        last = mm(ps_s[:, 2 * (g % 2) + t, 0:4 * NKEY], qT[:, g, t * P:(t + 1) * P],
                                  kD[:, g].rearrange("p j k -> p (j k)"), start=True, stop=True)
                else:
                    mm(ps_s[:, 0, :], qT[:, g, 0:P], kD[:, g, :, 0:P], start=True, stop=True).then_inc(pe_s, 1)
                    for jj in range(2):
                        last = mm(ps_s[:, 1 + jj, :], qT[:, g, P:2 * P],
                                  kD[:, g, 2 * jj:2 * jj + 2].rearrange("p j k -> p (j k)"), start=True, stop=True)
                        if jj == 0:
                            last.then_inc(pe_s, 1)
                last.then_inc(pe_s, 1)

            def turn_probs(n, g):
                pe.wait_ge(scaled, n + 1)
                pr = prob[:, g % 2]
                for j in range(4):
                    pt = ps_t[:, j // 2, (j % 2) * S:(j % 2) * S + S]
                    last = tr(pt[:, 0:P], pr[:, j, 0:P], ident[:])
                    last = tr(pt[:, P:2 * P], pr[:, j, P:2 * P], ident[:])
                    if not A:
                        last = tr(bank[2][:, j * P:(j + 1) * P], pr[:, j, 2 * P:3 * P], ident[:])
                last.then_inc(pe_t, 1)

            def apply_probs(n, g):
                pe.wait_ge(pT_dve, n + 1)
                pe.wait_ge(pT_act, n + 1)
                for j in range(4):
                    c = slice(g * P + j * HD, g * P + (j + 1) * HD)
                    out = bank[0][32 * j:32 * j + 32]
                    last = mm(out[:, 0:S], v[:, 0, c], probT[:, j], start=True, stop=A, skip_group_check=True)
                    if not A:
                        last = mm(out[:, P:S], v[:, 1, c], probT1[:, j], start=False, stop=True,
                                  skip_group_check=True)
                last.then_inc(pe_pv, 1)

            def project_out(b, t):
                for k in range(KC):
                    c = slice(t * P, (t + 1) * P)
                    last = split_product(nc, ps_t[:, t], (oT_high[:, k, c], oT_low[:, k, c]),
                                         parts_of("wo", k, slice(0, D)), k == 0, k == KC - 1)
                last.then_inc(pe_o, 1)

            if A:
                pe.wait_ge(ld_i, 16)
            turn_x(0, xn, normed, pe_xT, xT_copied)
            pe.wait_ge(ld_k, 16)
            pe.wait_ge(xT_copied, TB)
            pe.wait_ge(xT_low, TB)
            if A:
                pe.wait_ge(xk_ready, 1)
                project_kn(0)
            for n in parts[:-1]:
                pe.wait_ge(w_low[n], KC)
            for g in range(2):
                wait(pe, q_copied, g)
                project_q(g, g)
                wait(pe, v_copied, g)
                if A:
                    pe.wait_ge(kn_copied, 1)
                else:
                    project_k(g, g)
                    pe.wait_ge(k_dve, g + 1)
                    pe.wait_ge(k_act, g + 1)
                if g == 0:
                    pe.wait_ge(ld_v, 16)
                project_v(g, g)
            if A:
                pe.wait_ge(v_copied, 2)
                turn_k(0)

            def slot(b, g, first, last):
                n = 4 * b + g
                _, pg, pn = proj_of(b, g)
                project = g < 2 or not last
                if A:
                    pe.wait_ge(q_ready, n + 1)
                    pe.wait_ge(k_dve, b + 1)
                    pe.wait_ge(k_act, b + 1)
                    wait(pe, exped, n - 1)
                else:
                    pe.wait_ge(q_copied, n + 1)
                    wait(pe, maxed, n)
                scores(n, g)
                if first and g == 3:
                    pe.wait_ge(w_low["wo"], KC)
                if not (first and g < 2):
                    pe.wait_ge(pT_act, n - 1)
                    if g == 2 and not first:
                        project_out(b - 1, 1)
                    pe.wait_ge(pT_dve, n - 1)
                pe.wait_ge(q_copied, pn if project else 4 * B)
                wait(pe, pv_low, n - 2)
                if g == 2 and not last:
                    pe.wait_ge(xT_copied, TB * (b + 2))
                    pe.wait_ge(xT_low, TB * (b + 2))
                if g == 0 and not (isinstance(b, int) and b < 2):
                    pe.wait_ge(oT_copied, TB * (b - 1))
                if not (first and g < 2):
                    apply_probs(n - 2, (g - 2) % 4)
                if project:
                    pe.wait_ge(v_copied, pn)
                    if A:
                        if g == 2:
                            pe.wait_ge(xk_ready, b + 2)
                        if g == 3:
                            pe.wait_ge(kn_copied, b + 2)
                        project_v(pn, pg)
                        if g in (0, 3) and not (first and g == 0):
                            turn_probs(n - 1, (g - 1) % 4)
                    else:
                        project_k(pn, pg)
                    wait(pe, pv_low, n - 1)
                    project_q(pn, pg)
                    if not A:
                        pe.wait_ge(k_dve, pn + 1)
                        pe.wait_ge(k_act, pn + 1)
                        project_v(pn, pg)
                if g == 1:
                    if not first:
                        pe.wait_ge(pv_low, n - 1)
                        project_out(b - 1, 0)
                    if not last:
                        pe.wait_ge(q_copied, pn + 1)
                        pe.wait_ge(v_copied, pn + 1)
                        turn_x(b + 1, xn, normed, pe_xT, xT_copied)
                if A and g == 3 and not last:
                    pe.wait_ge(v_copied, pn + 1)
                    turn_k(b + 1)
                if A and g == 2 and not last:
                    pe.wait_ge(v_copied, pn + 1)
                    project_kn(b + 1)
                if not first and g in (1, 2):
                    pe.wait_ge(x_added, TB * (b - 1) + g)
                if not (first and g == 0) and not (A and project and g in (0, 3)):
                    turn_probs(n - 1, (g - 1) % 4)
                if g == 3 and not first:
                    if project:
                        pe.wait_ge(q_copied, pn + 1)
                        pe.wait_ge(v_copied, pn + 1)
                        if A:
                            pe.wait_ge(k_dve, b + 2)
                            pe.wait_ge(k_act, b + 2)
                    else:
                        pe.wait_ge(pv_low, n - 1)
                    turn_x(b - 1, xo, onormed, pe_oT, oT_copied)

            def batch(b, first=False, last=False):
                for g in range(G):
                    slot(b, g, first, last)

            batch(0, first=True)
            with pe.Fori(1, B - 1) as b:
                batch(b)
            batch(B - 1, last=True)
            for n in (4 * B - 2, 4 * B - 1):
                pe.wait_ge(pT_dve, n + 1)
                pe.wait_ge(pT_act, n + 1)
                if n == 4 * B - 2:
                    pe.wait_ge(oT_copied, TB * (B - 1))
                else:
                    pe.wait_ge(pv_low, n)
                apply_probs(n, n % 4)
                if n == 4 * B - 2:
                    turn_probs(n + 1, 3)
            pe.wait_ge(pv_low, 4 * B)
            for t in range(TB):
                project_out(B - 1, t)
            turn_x(B - 1, xo, onormed, pe_oT, oT_copied)


def load_toep(eng, t, h, dst, done):
    row = t["kpad"][bass.ds(h, 1), 1:1 + D]
    src = bass.AP(row.tensor, row.offset, [[1, P], [1, D]])
    eng.dma_start(dst, src).then_inc(done, 16)


def load_cext(eng, t, h, dst, done):
    eng.dma_start(dst, t["ctx_rev"][bass.ds(h, 1)].rearrange("one p k c -> (one p) k c")).then_inc(done, 16)


def convolution(nc, big, t, toep, cext, toep_in, cext_in, gates, gates_low):
    with ExitStack() as ctx:
        def sb(name, shape, dt=F32):
            return ctx.enter_context(nc.sbuf_tensor("b_" + name, shape, dt))

        def sem(name):
            return ctx.enter_context(nc.semaphore("b_" + name))

        pair = sb("pair", [P, 2, KC, NDEL, CW])
        qx = sb("qx", [P, 2, KC, 11 * B])
        prod = sb("prod", [P, 2, KC, 8, CEXT * B])
        ps = ctx.enter_context(nc.psum_tensor("b_ps", [P, 2, KC, 512], F32))
        wg, wg_high, wg_low = gates
        zeroed, gates_in, gates_padded, gates_high = sem("zeroed"), sem("gates_in"), sem("gates_padded"), sem("gates_high")
        paired, conv, extended = sem("paired"), sem("conv"), sem("extended")
        multiplied, wrapped, reduced, passed = sem("multiplied"), sem("wrapped"), sem("reduced"), sem("passed")
        block = ctx.enter_context(nc.Block())

        def loop(eng, body, gate_step=None):
            for u in range(2):
                body(u, u, 0)
            first_pairs = CH // 2 - (KC if gate_step else 0)
            with eng.Fori(1, first_pairs) as m:
                for u in range(2):
                    body(2 * m + u, u, m)
            if gate_step:
                with eng.Fori(0, KC) as k:
                    gate_step(k)
                    for u in range(2):
                        body(2 * k + (2 * first_pairs + u), u, k + first_pairs)

        @block.sync
        def _(sp):
            def head(h, u, m):
                wait(sp, paired, h - 1)
                load_cext(sp, t, h, cext[:, u], cext_in[u])
                wait(sp, conv, h - 1)
                load_toep(sp, t, h, toep[:, u], toep_in[u])
            with sp.Fori(0, KC) as k:
                for u in range(2):
                    head(2 * k + (2 + u), u, k + 1)
                sp.dma_start(wg[:, bass.ds(k, 1), 0:NG], t["gate_w"][:, bass.ds(k, 1)]).then_inc(gates_in, 16)
            with sp.Fori(1 + KC, CH // 2) as m:
                for u in range(2):
                    head(2 * m + u, u, m)

        @block.gpsimd
        def _(pool):
            def pairs(h, u, m):
                pool.wait_ge(cext_in[u], 16 * (m + 1))
                wait(pool, conv, h - 1)
                c = cext[:, u]
                whole = bass.AP(c.tensor, c.offset, [list(c.ap[0]), list(c.ap[1]), [B, NDEL], [1, CW]])
                one = bass.AP(c.tensor, c.offset, [list(c.ap[0]), list(c.ap[1]), [0, NDEL], [1, CW]])
                nc.gpsimd.tensor_tensor(pair[:, u], whole, one, ALU.mult).then_inc(paired, 1)

            def wrap(h, u):
                pool.wait_ge(multiplied, h + 1)
                low = prod[:, u, :, 0:4, 0:4 * B]
                nc.gpsimd.tensor_tensor(low, low, prod[:, u, :, 4:8, CW:CEXT * B], ALU.add).then_inc(wrapped, 1)

            nc.gpsimd.memset(wg[:, :, NG:], 0.0).then_inc(gates_padded, 1)
            for h in range(2):
                pairs(h, h, 0)
            with pool.Fori(0, CH // 2 - 1) as m:
                for u in range(2):
                    pairs(2 * m + u + 2, u, m + 1)
                    wrap(2 * m + u, u)
            for h in range(CH - 2, CH):
                wrap(h, h % 2)

        @block.scalar
        def _(act):
            def head(h, u, m):
                wait(act, multiplied, h - 1)
                nc.scalar.activation(qx[:, u, :, 0:CW], big[:, :, bass.ds(h * CW, CW)], ACT.Copy)
                nc.scalar.activation(qx[:, u, :, CW:], big[:, :, bass.ds(h * CW, 3 * B)], ACT.Copy)\
                    .then_inc(extended, 1)

            def gate_step(k):
                act.wait_ge(gates_in, 16 * KC)
                act.wait_ge(gates_padded, 1)
                nc.scalar.activation(wg_high[:, bass.ds(k, 1)], wg[:, bass.ds(k, 1)], ACT.Copy).then_inc(gates_high, 1)
            loop(act, head, gate_step)

        @block.tensor
        def _(pe):
            def head(h, u, m):
                pe.wait_ge(toep_in[u], 16 * (m + 1))
                pe.wait_ge(paired, h + 1)
                wait(pe, multiplied, h - 1)
                for lb in range(KC):
                    for mb in range(lb + 1):
                        last = nc.tensor.matmul(ps[:, u, lb, 0:NDEL * CW], toep[:, u, (lb - mb) * P:(lb - mb + 1) * P],
                                                pair[:, u, mb].rearrange("p d c -> p (d c)"),
                                                start=(mb == 0), stop=(mb == lb))
                last.then_inc(conv, 1)
            loop(pe, head)

        @block.vector
        def _(dve):
            for u in range(2):
                nc.vector.memset(prod[:, u, :, 4:8, 0:4 * B], 0.0).then_inc(zeroed, 1)
                nc.vector.memset(prod[:, u, :, 4:8, CW:], 0.0).then_inc(zeroed, 1)
            dve.wait_ge(zeroed, 4)

            def multiply(h, u):
                dve.wait_ge(conv, h + 1)
                dve.wait_ge(extended, h + 1)
                wait(dve, reduced, h - 1)
                y = ps[:, u, :, 0:NDEL * CW].rearrange("p k (d c) -> p k d c", d=NDEL)
                q, f = qx[:, u], prod[:, u]
                qs, fs = list(q.ap[1]), list(f.ap[1])
                one = bass.AP(q.tensor, q.offset, [list(q.ap[0]), qs, [0, NDEL], [1, CW]])
                to = bass.AP(f.tensor, f.offset + 3 * CEXT * B, [list(f.ap[0]), fs, [CEXT * B + B, NDEL], [1, CW]])
                nc.vector.tensor_tensor(to, y, one, ALU.mult)
                other = bass.AP(q.tensor, q.offset + B, [list(q.ap[0]), qs, [B, 3], [1, CW]])
                nc.vector.tensor_tensor(f[:, :, 0:3, 0:CW], y[:, :, 1:4], other, ALU.mult)\
                    .then_inc(multiplied, 1)

            def reduce(h, u):
                wait_apart(dve, wrapped, h + 1, passed)
                nc.vector.tensor_reduce(big[:, :, bass.ds(h * CW, CW)],
                                        prod[:, u, :, :, 0:CW].rearrange("p k r c -> p k c r"),
                                        AX.X, ALU.add).then_inc(reduced, 1)

            def head(h, u, m):
                multiply(h, u)
                if not (isinstance(h, int) and h == 0):
                    reduce(h - 1, 1 - u)

            def gate_step(k):
                dve.wait_ge(gates_high, k + 1)
                nc.vector.tensor_tensor(wg_low[:, bass.ds(k, 1)], wg[:, bass.ds(k, 1)],
                                        wg_high[:, bass.ds(k, 1)].bitcast(F32), ALU.subtract).then_inc(gates_low, 1)
            loop(dve, head, gate_step)
            reduce(CH - 1, 1)


def router(nc, x_sb, big, ident, t, alibi, gathered, gates, gates_low, ahead):
    R = 4
    with ExitStack() as ctx:
        def sb(name, shape, dt=F32):
            return ctx.enter_context(nc.sbuf_tensor("c_" + name, shape, dt))

        def sem(name):
            return ctx.enter_context(nc.semaphore("c_" + name))

        _, wg_high, wg_low = gates
        gb = sb("gb", [P, NC])
        rel = sb("rel", [P, 2 * P])
        slope = sb("slope", [P, H])
        yT = sb("yT", [P, 2, KC, P])
        xn = sb("xn", [P, R, D])
        xT_high, xT_low = sb("xT_high", [P, 2, KC, P], F32R), sb("xT_low", [P, 2, KC, P], F32R)
        sc = sb("sc", [P, 2, NC])
        top = sb("top", [P, 2, 8])
        ix = sb("ix", [P, R, 8], U32)
        st, mv = sb("st", [P, 2, 6]), sb("mv", [P, 2, 2])
        ve, rstd, mhalf = sb("ve", [P, 2]), sb("rstd", [P, 2]), sb("mhalf", [P, 1])
        ps = ctx.enter_context(nc.psum_tensor("c_ps", [P, 2, 3, 512], F32))
        ps_y = ctx.enter_context(nc.psum_tensor("c_ps_y", [P, 512], F32))
        ps_x = ctx.enter_context(nc.psum_tensor("c_ps_x", [P, 512], F32))
        gb_in, rel_in = sem("gb_in"), sem("rel_in")
        y_cut, pe_y, added = sem("y_cut"), sem("pe_y"), sem("added")
        stats, aggr, lnvar, lnrstd, normed = sem("stats"), sem("aggr"), sem("lnvar"), sem("lnrstd"), sem("normed")
        pe_x, high_copied, xT_copied, scored = sem("pe_x"), sem("high_copied"), sem("xT_copied"), sem("scored")
        b_padded = sem("b_padded")
        biased, maxed, found, chosen = sem("biased"), sem("maxed"), sem("found"), sem("chosen")
        setup, passed, passed_pool = sem("setup"), sem("passed"), sem("passed_pool")
        block = ctx.enter_context(nc.Block())

        def loop(eng, body):
            M = TILES // R
            for u in range(R):
                body(u, u, 0, True, False)
            with eng.Fori(1, M - 1) as m:
                for u in range(R):
                    body(R * m + u, u, m, False, False)
            for u in range(R):
                body(R * (M - 1) + u, u, M - 1, False, True)

        def x_tile(n):
            return x_sb[:, bass.ds(n * D, D)]

        @block.sync
        def _(sp):
            sp.dma_start(gb[:, 0:NG], t["gate_b"].rearrange("(one g) -> one g", one=1).broadcast_to([P, NG]))\
                .then_inc(gb_in, 16)
            sp.dma_start(rel[:], t["rel"]).then_inc(rel_in, 16)
            sp.dma_start(slope[:], t["slope"]).then_inc(rel_in, 16)
            ahead(sp)

        @block.scalar
        def _(act):
            def cut(n, u, m):
                wait(act, pe_y, n - 1)
                b = m * (R // TB) + u // TB
                src = big[:].rearrange("p k (q b) -> p k q b", b=B)[:, :, (u % TB) * P:(u % TB + 1) * P, bass.ds(b, 1)]
                nc.scalar.activation(yT[:, u % 2].rearrange("p k (q one) -> p k q one", one=1), src, ACT.Copy)\
                    .then_inc(y_cut, 1)

            def turned(n, u):
                act.wait_ge(pe_x, n + 1)
                wait(act, scored, n - 1)
                nc.scalar.activation(xT_high[:, u % 2], ps_x[:].rearrange("p (k q) -> p k q", k=KC), ACT.Copy)\
                    .then_inc(high_copied, 1)

            cut(0, 0, 0)
            cut(1, 1, 0)
            turned(0, 0)
            cut(2, 2, 0)
            cut(3, 3, 0)

            def tile(n, u, m, first, last):
                if not (last and u >= R - 1):
                    turned(n + 1, (u + 1) % R)
                if not last:
                    cut(n + R, u, m + 1)
            loop(act, tile)

        @block.tensor
        def _(pe):
            def turn_y(n, u):
                pe.wait_ge(y_cut, n + 1)
                wait(pe, added, n)
                for k in range(KC):
                    last = nc.tensor.transpose(ps_y[:, k * P:(k + 1) * P], yT[:, u % 2, k], ident[:])
                last.then_inc(pe_y, 1)

            def turn_x(n, u):
                pe.wait_ge(normed, n + 1)
                wait(pe, xT_copied, n)
                for k in range(KC):
                    last = nc.tensor.transpose(ps_x[:, k * P:(k + 1) * P], xn[:, u, k * P:(k + 1) * P], ident[:])
                last.then_inc(pe_x, 1)

            def scores(n, u, chunks):
                for c in chunks:
                    for k in range(KC):
                        cols = slice(c * VCH, (c + 1) * VCH)
                        last = split_product(nc, ps[:, u % 2, c, 0:VCH], (xT_high[:, u % 2, k], xT_low[:, u % 2, k]),
                                             (wg_high[:, k, cols], wg_low[:, k, cols]), k == 0, k == KC - 1)
                if 2 in chunks:
                    last.then_inc(scored, 1)

            turn_y(0, 0)
            turn_y(1, 1)
            turn_x(0, 0)
            turn_y(2, 2)
            pe.wait_ge(gates_low, KC)

            def tile(n, u, m, first, last):
                pe.wait_ge(xT_copied, n + 1)
                wait(pe, biased, n - 1)
                scores(n, u, (0,))
                if not (last and u >= R - 1):
                    turn_x(n + 1, (u + 1) % R)
                scores(n, u, (1, 2))
                if not (last and u >= R - 3):
                    turn_y(n + 3, (u + 3) % R)
            loop(pe, tile)

        @block.gpsimd
        def _(pool):
            def rstd_of(n, u):
                wait_apart(pool, aggr, n + 1, passed_pool)
                nc.gpsimd.tensor_scalar(ve[:, u % 2:u % 2 + 1], mv[:, u % 2, 1:2], LN_EPS, None, ALU.add)\
                    .then_inc(lnvar, 1)
                pool.wait_ge(lnvar, n + 1)
                nc.gpsimd.tensor_tensor(rstd[:, u % 2:u % 2 + 1], ve[:, u % 2:u % 2 + 1], mhalf[:], ALU.pow)\
                    .then_inc(lnrstd, 1)

            def gather(n, u):
                wait_apart(pool, found, n + 1, passed_pool)
                wait_apart(pool, pe_x, n + 1, passed_pool)
                nc.gpsimd.indirect_dma_start(
                    xn[:, u], None, t["pool"], bass.IndirectOffsetOnAxis(ap=ix[:, u, 0:1], axis=0),
                    bounds_check=NV - 1, oob_is_err=False).then_inc(gathered[u], 16)

            def add(n, u, m):
                pool.wait_ge(gathered[u], 16 * (m + 1))
                nc.gpsimd.tensor_tensor(x_tile(n), x_tile(n), xn[:, u], ALU.add).then_inc(chosen, 1)

            nc.gpsimd.memset(gb[:, NG:NC], 0.0).then_inc(b_padded, 1)
            nc.gpsimd.memset(mhalf[:], -0.5).then_inc(setup, 1)
            pool.wait_ge(setup, 1)
            rstd_of(0, 0)
            rstd_of(1, 1)
            rstd_of(2, 2)

            def tile(n, u, m, first, last):
                if not (first and u == 0):
                    add(n - 1, (u - 1) % R, m if u else m - 1)
                if not (last and u >= R - 3):
                    rstd_of(n + 3, (u + 3) % R)
                gather(n, u)
                if first:
                    pool.wait_ge(rel_in, 32)
                    h = slice(4 * u, 4 * u + 4)
                    nc.gpsimd.tensor_tensor(
                        alibi[:, h], rel[:].rearrange("p (one k) -> p one k", one=1).broadcast_to([P, 4, 2 * P]),
                        slope[:, h].rearrange("p (h one) -> p h one", one=1).broadcast_to([P, 4, 2 * P]),
                        ALU.mult).then_inc(setup, 1)
            loop(pool, tile)
            add(TILES - 1, R - 1, TILES // R - 1)

        @block.vector
        def _(dve):
            def norm_stats(n, u):
                dve.wait_ge(pe_y, n + 1)
                nc.vector.tensor_tensor(x_tile(n), x_tile(n), ps_y[:], ALU.add).then_inc(added, 1)
                wait_apart(dve, added, n + 1, passed)
                nc.vector.bn_stats(st[:, u % 2], x_tile(n)).then_inc(stats, 1)
                wait_apart(dve, stats, n + 1, passed)
                nc.vector.bn_aggr(mv[:, u % 2], st[:, u % 2]).then_inc(aggr, 1)

            def norm(n, u):
                dve.wait_ge(lnrstd, n + 1)
                wait(dve, chosen, n - R + 1)
                nc.vector.tensor_scalar(xn[:, u], x_tile(n), mv[:, u % 2, 0:1], rstd[:, u % 2:u % 2 + 1],
                                        ALU.subtract, ALU.mult).then_inc(normed, 1)

            def bias(n, u):
                dve.wait_ge(scored, n + 1)
                s = sc[:, u % 2]
                nc.vector.tensor_tensor(s.rearrange("p (c g) -> p c g", c=3), ps[:, u % 2, :, 0:VCH],
                                        gb[:].rearrange("p (c g) -> p c g", c=3), ALU.add).then_inc(biased, 1)

            def largest(n, u):
                wait_apart(dve, biased, n + 1, passed)
                nc.vector.max(top[:, u % 2], sc[:, u % 2, 0:NG]).then_inc(maxed, 1)

            def place(n, u):
                wait_apart(dve, maxed, n + 1, passed)
                nc.vector.max_index(ix[:, u], top[:, u % 2], sc[:, u % 2, 0:NG]).then_inc(found, 1)

            def low(n, u):
                dve.wait_ge(high_copied, n + 1)
                nc.vector.tensor_tensor(xT_low[:, u % 2], ps_x[:].rearrange("p (k q) -> p k q", k=KC),
                                        xT_high[:, u % 2].bitcast(F32), ALU.subtract).then_inc(xT_copied, 1)

            for n in range(2):
                norm_stats(n, n)
                norm(n, n)
            low(0, 0)
            norm_stats(2, 2)
            dve.wait_ge(gb_in, 16)
            dve.wait_ge(b_padded, 1)

            def tile(n, u, m, first, last):
                if not (last and u >= R - 1):
                    low(n + 1, (u + 1) % R)
                bias(n, u)
                if not (last and u >= R - 2):
                    norm(n + 2, (u + 2) % R)
                largest(n, u)
                if not (last and u >= R - 3):
                    norm_stats(n + 3, (u + 3) % R)
                place(n, u)
            loop(dve, tile)


def load_head(eng, t, h, cT, decay, done):
    eng.dma_start(cT, t["ctxT"][h]).then_inc(done, 16)
    eng.dma_start(decay, t["decay"][h]).then_inc(done, 16)


def retention(nc, big, t, o_sb, ahead):
    CHUNK = 512
    NCH = TOK // CHUNK
    with ExitStack() as ctx:
        def sb(name, shape, dt=F32):
            return ctx.enter_context(nc.sbuf_tensor("e_" + name, shape, dt))

        def sem(name):
            return ctx.enter_context(nc.semaphore("e_" + name))

        wh = sb("wh", [P, RH, RD])
        wh_in = sem("wh_in")
        cT = sb("cT", [P, 2, TOK])
        decay = sb("decay", [P, 2, TB, S])
        in_ = [sem("in0"), sem("in1")]
        qT = sb("q_high", [P, TOK], F32R), sb("q_low", [P, TOK], F32R)
        kT = sb("k_high", [P, TOK], F32R), sb("k_low", [P, TOK], F32R)
        v = sb("v_high", [P, TILES, RD], F32R), sb("v_low", [P, TILES, RD], F32R)
        raw, a = sb("raw", [P, TB, S]), sb("a", [P, TB, S])
        aT = sb("a_high", [P, TB, S], F32R), sb("a_low", [P, TB, S], F32R)
        ps_p = [ctx.enter_context(nc.psum_tensor(f"e_ps_p{i}", [P, CHUNK], F32)) for i in range(3)]
        ps_v = [ctx.enter_context(nc.psum_tensor(f"e_ps_v{i}", [P, CHUNK], F32)) for i in range(2)]
        ps_s = ctx.enter_context(nc.psum_tensor("e_ps_s", [P, TB, S], F32))
        ps_o = [ctx.enter_context(nc.psum_tensor(f"e_ps_o{i}", [P, CHUNK], F32)) for i in range(2)]
        pe_p, pe_v, pe_s, pe_o = sem("pe_p"), sem("pe_v"), sem("pe_s"), sem("pe_o")
        p_copied, v_copied = sem("p_copied"), sem("v_copied")
        p_high, v_high, a_high, a_low = (sem(n + "_done") for n in ("p_high", "v_high", "a_high", "a_low"))
        decayed, negated, clamped, o_copied = sem("decayed"), sem("negated"), sem("clamped"), sem("o_copied")
        block = ctx.enter_context(nc.Block())

        def loop(eng, body):
            for h in range(RH):
                body(h, h % 2, h // 2, h == 0, h == RH - 1)

        @block.sync
        def _(sp):
            sp.dma_start(wh[:], t["wh"]).then_inc(wh_in, 16)
            for h in range(2):
                load_head(sp, t, h, cT[:, h], decay[:, h], in_[h])
            ahead(sp)
            for h in range(2, RH):
                sp.wait_ge(pe_v, NCH * (h - 1))
                sp.wait_ge(decayed, h - 1)
                load_head(sp, t, h, cT[:, h % 2], decay[:, h % 2], in_[h % 2])

        @block.tensor
        def _(pe):
            mm = nc.tensor.matmul

            def project(j, h, src):
                wait(pe, p_copied, j - 2)
                mm(ps_p[j % 3][:], wh[:, h], src, start=True, stop=True).then_inc(pe_p, 1)

            def queries(h):
                for c in range(NCH):
                    project(2 * NCH * h + c, h, big[:, h, c * CHUNK:(c + 1) * CHUNK])

            def keys(h, u):
                pe.wait_ge(in_[u], 32 * (h // 2 + 1))
                for c in range(NCH):
                    project(2 * NCH * h + NCH + c, h, cT[:, u, c * CHUNK:(c + 1) * CHUNK])

            def values(h, u):
                for c in range(NCH):
                    wait(pe, v_copied, NCH * h + c - 1)
                    for i in range(4):
                        last = mm(ps_v[c % 2][:, i * P:(i + 1) * P], cT[:, u, (4 * c + i) * P:(4 * c + i + 1) * P],
                                  wh[:, h], start=True, stop=True)
                    last.then_inc(pe_v, 1)

            def scores(h):
                pe.wait_ge(p_copied, 2 * NCH * (h + 1))
                wait(pe, decayed, h)
                for tt in range(TB):
                    for b in range(B):
                        c, q = slice(b * S + tt * P, b * S + (tt + 1) * P), slice(b * S, (b + 1) * S)
                        last = split_product(nc, ps_s[:, tt], [k[:, c] for k in kT], [x[:, q] for x in qT],
                                             b == 0, b == B - 1)
                last.then_inc(pe_s, 1)

            def outputs(h):
                pe.wait_ge(a_low, h + 1)
                pe.wait_ge(v_copied, NCH * (h + 1))
                for ss in range(TB):
                    for half in range(2):
                        wait(pe, o_copied, NCH * h + 2 * ss + half - 1)
                        vs = [x[:].rearrange("p (b t) e -> p b t e", t=TB) for x in v]
                        for tt in range(TB):
                            last = split_product(nc, ps_o[half][:], [x[:, tt, ss * P:(ss + 1) * P] for x in aT],
                                                 [x[:, 4 * half:4 * half + 4, tt, :] for x in vs],
                                                 tt == 0, tt == TB - 1)
                        last.then_inc(pe_o, 1)

            def head(h, u, m, first, last):
                if first:
                    pe.wait_ge(wh_in, 16)
                    queries(h)
                keys(h, u)
                if not first:
                    outputs(h - 1)
                values(h, u)
                scores(h)
                if not last:
                    queries(h + 1)
                else:
                    outputs(h)
            loop(pe, head)

        @block.scalar
        def _(act):
            def head(h, u, m, first, last):
                def chunk(i, high):
                    act.wait_ge(pe_p, i + 1)
                    wait(act, pe_s, h)
                    c = i % NCH
                    nc.scalar.activation(high[:, c * CHUNK:(c + 1) * CHUNK], ps_p[i % 3][:], ACT.Copy)\
                        .then_inc(p_high, 1)

                for c in range(NCH):
                    chunk(2 * NCH * h + c, qT[0])
                for c in range(NCH):
                    if c == 2 and not first:
                        scores(h - 1)
                    chunk(2 * NCH * h + NCH + c, kT[0])
                for c in range(NCH):
                    act.wait_ge(pe_v, NCH * h + c + 1)
                    wait(act, pe_o, NCH * h)
                    nc.scalar.activation(v[0][:, 4 * c:4 * c + 4], ps_v[c % 2][:].rearrange("p (t e) -> p t e", t=4),
                                         ACT.Copy).then_inc(v_high, 1)

            def scores(h):
                act.wait_ge(clamped, h + 1)
                wait(act, pe_o, NCH * h)
                nc.scalar.activation(aT[0][:], a[:], ACT.Copy).then_inc(a_high, 1)

            loop(act, head)
            scores(RH - 1)

        @block.vector
        def _(dve):
            def outputs(h):
                for ss in range(TB):
                    for half in range(2):
                        dve.wait_ge(pe_o, NCH * h + 2 * ss + half + 1)
                        o4 = o_sb[:].rearrange("p (b t) f -> p b t f", t=TB)
                        nc.vector.tensor_copy(o4[:, 4 * half:4 * half + 4, ss, h * RD:(h + 1) * RD],
                                              ps_o[half][:].rearrange("p (b e) -> p b e", b=4)).then_inc(o_copied, 1)

            def low(out, whole, high, ready, count, done):
                dve.wait_ge(ready, count)
                nc.vector.tensor_tensor(out, whole, high.bitcast(F32), ALU.subtract).then_inc(done, 1)

            def head(h, u, m, first, last):
                def chunk(i, parts):
                    s = slice(i % NCH * CHUNK, (i % NCH + 1) * CHUNK)
                    low(parts[1][:, s], ps_p[i % 3][:], parts[0][:, s], p_high, i + 1, p_copied)

                for c in range(NCH):
                    chunk(2 * NCH * h + c, qT)
                if not first:
                    clamp(h - 1)
                for c in range(NCH):
                    if c == 2 and not first:
                        low(aT[1][:], a[:], aT[0][:], a_high, h, a_low)
                    chunk(2 * NCH * h + NCH + c, kT)
                if not first:
                    outputs(h - 1)
                for c in range(NCH):
                    s = slice(4 * c, 4 * c + 4)
                    low(v[1][:, s], ps_v[c % 2][:].rearrange("p (t e) -> p t e", t=4), v[0][:, s], v_high,
                        NCH * h + c + 1, v_copied)
                dve.wait_ge(pe_s, h + 1)
                nc.vector.tensor_tensor(raw[:], ps_s[:], decay[:, u], ALU.mult).then_inc(decayed, 1)

            def clamp(h):
                dve.wait_ge(decayed, h + 1)
                wait(dve, a_low, h)
                nc.vector.tensor_scalar(a[:], raw[:], -1.0, 1.0, ALU.mult, ALU.max).then_inc(negated, 1)
                dve.wait_ge(negated, h + 1)
                nc.vector.tensor_tensor(a[:], a[:], raw[:], ALU.max).then_inc(clamped, 1)

            loop(dve, head)
            clamp(RH - 1)
            low(aT[1][:], a[:], aT[0][:], a_high, RH, a_low)
            outputs(RH - 1)


def mixing(nc, x_sb, big, ident, o_sb, weights, ld, logitT, ahead):
    with ExitStack() as ctx:
        def sb(name, shape, dt=F32):
            return ctx.enter_context(nc.sbuf_tensor("f_" + name, shape, dt))

        def sem(name):
            return ctx.enter_context(nc.semaphore("f_" + name))

        wgate, wout, gamma, beta, wr, br = weights
        on = sb("on", [P, 2, D])
        w = sb("w", [P, 2, D])
        wy = sb("wy", [P, 2, D])
        wy_high, wy_low = sb("wy_high", [P, 2, KC, P], F32R), sb("wy_low", [P, 2, KC, P], F32R)
        in_high, in_low = sb("in_high", [P, 2, KC, P], F32R), sb("in_low", [P, 2, KC, P], F32R)
        wgate_high, wgate_low = sb("wgate_high", [P, KC, D], F32R), sb("wgate_low", [P, KC, D], F32R)
        wout_high, wout_low = sb("wout_high", [P, KC, D], F32R), sb("wout_low", [P, KC, D], F32R)
        xf = sb("xf", [P, 2, D])
        st, mv = sb("st", [P, 2, 2, 6]), sb("mv", [P, 2, 2, 2])
        ve, rstd, mhalf = sb("ve", [P, 2, 2]), sb("rstd", [P, 2, 2]), sb("mhalf", [P, 1])
        ps = [ctx.enter_context(nc.psum_tensor(f"f_ps{i}", [P, 512], F32)) for i in range(5)]
        ps_y, ps_w, ps_o, ps_x, ps_l = ps
        setup = sem("setup")
        ostats, oaggr, ovar, orstd, onormed = (sem(n) for n in ("ostats", "oaggr", "ovar", "orstd", "onormed"))
        xstats, xaggr, xvar, xrstd, xnormed = (sem(n) for n in ("xstats", "xaggr", "xvar", "xrstd", "xnormed"))
        pe_y, pe_w, pe_o, pe_x, pe_l = (sem(n) for n in ("pe_y", "pe_w", "pe_o", "pe_x", "pe_l"))
        split_high, split_low, gated_high, gated_low = (sem(n) for n in ("split_high", "split_low", "gated_high",
                                                                         "gated_low"))
        gate_high, gate_low, out_high, out_low = (sem(n) for n in ("gate_high", "gate_low", "out_high", "out_low"))
        relued, times_gamma, scaled, gated, added = (sem(n) for n in ("relued", "times_gamma", "scaled", "gated",
                                                                     "added"))
        xT_copied, l_copied, passed, passed_pool = (sem(n) for n in ("xT_copied", "l_copied", "passed",
                                                                    "passed_pool"))
        block = ctx.enter_context(nc.Block())

        def loop(eng, body):
            for n in range(2):
                body(n, n)
            with eng.Fori(1, TILES // 2 - 2) as m:
                for u in range(2):
                    body(2 * m + u, u)
            for n in range(TILES - 4, TILES):
                body(n, n % 2)

        def exists(n):
            return not isinstance(n, int) or 0 <= n < TILES

        def tile_of(s, n):
            return s[:, bass.ds(n * D, D)]

        o2 = o_sb[:].rearrange("p n d -> p (n d)")

        def whole_of(n):
            return big[:, :, bass.ds(n * P, P)]

        @block.sync
        def _(sp):
            ahead(sp)

        @block.gpsimd
        def _(pool):
            def rstd_of(n, u, i, eps, got, var, done):
                wait_apart(pool, got, n + 1, passed_pool)
                nc.gpsimd.tensor_scalar(ve[:, i, u:u + 1], mv[:, i, u, 1:2], eps, None, ALU.add).then_inc(var, 1)
                pool.wait_ge(var, n + 1)
                nc.gpsimd.tensor_tensor(rstd[:, i, u:u + 1], ve[:, i, u:u + 1], mhalf[:], ALU.pow).then_inc(done, 1)

            nc.gpsimd.memset(mhalf[:], -0.5).then_inc(setup, 1)
            pool.wait_ge(setup, 1)
            def affine(n, u):
                pool.wait_ge(onormed, n + 1)
                nc.gpsimd.tensor_tensor(on[:, u], on[:, u], gamma[:], ALU.mult).then_inc(times_gamma, 1)
                wait_apart(pool, times_gamma, n + 1, passed_pool)
                nc.gpsimd.tensor_tensor(on[:, u], on[:, u], beta[:], ALU.add).then_inc(scaled, 1)

            for n in range(2):
                rstd_of(n, n, 0, GN_EPS, oaggr, ovar, orstd)
            pool.wait_ge(ld, 96)
            affine(0, 0)
            affine(1, 1)
            rstd_of(2, 0, 0, GN_EPS, oaggr, ovar, orstd)
            affine(2, 0)

            def tile(n, u):
                if exists(n + 3):
                    rstd_of(n + 3, 1 - u, 0, GN_EPS, oaggr, ovar, orstd)
                    affine(n + 3, 1 - u)
                rstd_of(n, u, 1, LN_EPS, xaggr, xvar, xrstd)
            loop(pool, tile)

        @block.vector
        def _(dve):
            def stats(src, n, u, i, got, agg):
                nc.vector.bn_stats(st[:, i, u], tile_of(src, n)).then_inc(got, 1)
                wait_apart(dve, got, n + 1, passed)
                nc.vector.bn_aggr(mv[:, i, u], st[:, i, u]).then_inc(agg, 1)

            def apply(src, n, u, i, out, ready, done):
                dve.wait_ge(ready, n + 1)
                nc.vector.tensor_scalar(out[:, u], tile_of(src, n), mv[:, i, u, 0:1], rstd[:, i, u:u + 1],
                                        ALU.subtract, ALU.mult).then_inc(done, 1)

            def apply_o(n, u):
                wait(dve, gated, n - 1)
                apply(o2, n, u, 0, on, orstd, onormed)

            def norm_o(n, u):
                stats(o2, n, u, 0, ostats, oaggr)
                apply_o(n, u)

            def gate(n, u):
                dve.wait_ge(scaled, n + 1)
                dve.wait_ge(relued, n + 1)
                wait(dve, pe_y, n - 1)
                nc.vector.tensor_tensor(wy[:, u], on[:, u], w[:, u], ALU.mult).then_inc(gated, 1)

            def norm_x(n, u):
                dve.wait_ge(pe_o, n + 1)
                nc.vector.tensor_tensor(tile_of(x_sb, n), tile_of(x_sb, n), ps_o[:], ALU.add).then_inc(added, 1)
                wait_apart(dve, added, n + 1, passed)
                stats(x_sb, n, u, 1, xstats, xaggr)
                wait(dve, pe_x, n - 1)
                apply(x_sb, n, u, 1, xf, xrstd, xnormed)

            def gated_low_part(n, u):
                dve.wait_ge(gated_high, n + 1)
                nc.vector.tensor_tensor(wy_low[:, u], ps_y[:].rearrange("p (k q) -> p k q", k=KC),
                                        wy_high[:, u].bitcast(F32), ALU.subtract).then_inc(gated_low, 1)

            def split_low_part(n, u):
                dve.wait_ge(split_high, n + 1)
                nc.vector.tensor_tensor(in_low[:, u], whole_of(n), in_high[:, u].bitcast(F32), ALU.subtract)\
                    .then_inc(split_low, 1)

            def weights_low(whole, high, low, ready, done):
                for k in range(KC):
                    dve.wait_ge(ready, k + 1)
                    nc.vector.tensor_tensor(low[:, k], whole[:, k], high[:, k].bitcast(F32), ALU.subtract)\
                        .then_inc(done, 1)

            weights_low(wgate, wgate_high, wgate_low, gate_high, gate_low)
            for n in range(2):
                split_low_part(n, n)
            for n in range(2):
                norm_o(n, n)
            weights_low(wout, wout_high, wout_low, out_high, out_low)
            gate(0, 0)
            split_low_part(2, 0)
            gate(1, 1)
            gated_low_part(0, 0)
            norm_o(2, 0)

            def tile(n, u):
                if exists(n + 3):
                    stats(o2, n + 3, 1 - u, 0, ostats, oaggr)
                if exists(n + 2):
                    gate(n + 2, u)
                if exists(n + 3):
                    apply_o(n + 3, 1 - u)
                    split_low_part(n + 3, 1 - u)
                if exists(n + 1):
                    gated_low_part(n + 1, 1 - u)
                norm_x(n, u)
            loop(dve, tile)

        @block.scalar
        def _(act):
            act.wait_ge(ld, 96)

            def split_high_part(n, u):
                wait(act, pe_w, n - 1)
                nc.scalar.activation(in_high[:, u], whole_of(n), ACT.Copy).then_inc(split_high, 1)

            def relu(n, u):
                act.wait_ge(pe_w, n + 1)
                wait(act, gated, n - 1)
                nc.scalar.activation(w[:, u], ps_w[:], ACT.Relu).then_inc(relued, 1)

            def turned(n, u):
                act.wait_ge(pe_x, n + 1)
                nc.scalar.activation(tile_of(o2, n), ps_x[:], ACT.Copy)\
                    .then_inc(xT_copied, 1)

            def logits(n, u):
                act.wait_ge(pe_l, n + 1)
                nc.scalar.activation(logitT[0:NE, bass.ds(n * P, P)], ps_l[0:NE, 0:P], ACT.Identity,
                                     bias=br[0:NE, 0:1]).then_inc(l_copied, 1)

            def gated_high_part(n, u):
                act.wait_ge(pe_y, n + 1)
                wait(act, pe_o, n - 1)
                nc.scalar.activation(wy_high[:, u], ps_y[:].rearrange("p (k q) -> p k q", k=KC), ACT.Copy)\
                    .then_inc(gated_high, 1)

            for k in range(KC):
                nc.scalar.activation(wgate_high[:, k], wgate[:, k], ACT.Copy).then_inc(gate_high, 1)
            for n in range(2):
                split_high_part(n, n)
            for k in range(KC):
                nc.scalar.activation(wout_high[:, k], wout[:, k], ACT.Copy).then_inc(out_high, 1)
            relu(0, 0)
            split_high_part(2, 0)
            relu(1, 1)
            gated_high_part(0, 0)

            def tile(n, u):
                if exists(n + 3):
                    split_high_part(n + 3, 1 - u)
                if exists(n + 2):
                    relu(n + 2, u)
                if exists(n - 2):
                    logits(n - 2, u)
                if exists(n + 1):
                    gated_high_part(n + 1, 1 - u)
                if exists(n - 1):
                    turned(n - 1, 1 - u)
            loop(act, tile)
            logits(TILES - 2, 0)
            turned(TILES - 1, 1)
            logits(TILES - 1, 1)

        @block.tensor
        def _(pe):
            mm, tr = nc.tensor.matmul, nc.tensor.transpose

            def gates(n, u):
                pe.wait_ge(split_low, n + 1)
                wait(pe, relued, n)
                for k in range(KC):
                    last = split_product(nc, ps_w[:], (in_high[:, u, k], in_low[:, u, k]),
                                         (wgate_high[:, k], wgate_low[:, k]), k == 0, k == KC - 1)
                last.then_inc(pe_w, 1)

            def turn_gated(n, u):
                pe.wait_ge(gated, n + 1)
                wait(pe, gated_low, n)
                for k in range(KC):
                    last = tr(ps_y[:, k * P:(k + 1) * P], wy[:, u, k * P:(k + 1) * P], ident[:])
                last.then_inc(pe_y, 1)

            def project(n, u):
                pe.wait_ge(gated_low, n + 1)
                wait(pe, added, n)
                for k in range(KC):
                    last = split_product(nc, ps_o[:], (wy_high[:, u, k], wy_low[:, u, k]),
                                         (wout_high[:, k], wout_low[:, k]), k == 0, k == KC - 1)
                last.then_inc(pe_o, 1)

            def turn_x(n, u):
                pe.wait_ge(xnormed, n + 1)
                wait(pe, xT_copied, n)
                for k in range(KC):
                    last = tr(ps_x[:, k * P:(k + 1) * P], xf[:, u, k * P:(k + 1) * P], ident[:])
                last.then_inc(pe_x, 1)

            def logits(n, u):
                pe.wait_ge(xT_copied, n + 1)
                wait(pe, l_copied, n)
                for k in range(KC):
                    last = mm(ps_l[0:NE, 0:P], wr[:, k], o2[:, bass.ds(n * D + k * P, P)],
                              start=(k == 0), stop=(k == KC - 1))
                last.then_inc(pe_l, 1)

            pe.wait_ge(ld, 96)
            pe.wait_ge(gate_low, KC)
            gates(0, 0)
            gates(1, 1)
            turn_gated(0, 0)
            pe.wait_ge(out_low, KC)

            def tile(n, u):
                if exists(n + 2):
                    gates(n + 2, u)
                if exists(n - 2):
                    logits(n - 2, u)
                if exists(n + 1):
                    turn_gated(n + 1, 1 - u)
                project(n, u)
                if exists(n - 1):
                    turn_x(n - 1, 1 - u)
            loop(pe, tile)
            logits(TILES - 2, 0)
            turn_x(TILES - 1, 1)
            logits(TILES - 1, 1)


def experts(nc, x_sb, big, xnT_sb, ident, weights, ld, logitT, spare, xp_rows, out):
    R = 4
    EARLY = 8
    F = 3
    with ExitStack() as ctx:
        def sb(name, shape, dt=F32):
            return ctx.enter_context(nc.sbuf_tensor("g_" + name, shape, dt))

        def sem(name):
            return ctx.enter_context(nc.semaphore("g_" + name))

        before, later, iota, we, be = weights
        ones = sb("ones", [P, P])
        lg, ex, pr = (sb(n, [P, TILES, NE]) for n in ("lg", "ex", "pr"))
        far, place, hot, ranks = (sb(n, [P, TILES, NE]) for n in ("far", "place", "hot", "ranks"))
        m1, sm, ri, best, first_, rank = (sb(n, [P, TILES]) for n in ("m1", "sm", "ri", "best", "first", "rank"))
        rank_i = sb("rank_i", [P, TILES], U32)
        total = sb("total", [P, 1])
        totals = sb("totals", [P, P])
        xT_high, xT_low = sb("xT_high", [P, R, KC, P], F32R), sb("xT_low", [P, R, KC, P], F32R)
        we_high, we_low = sb("we_high", [P, KC, D], F32R), sb("we_low", [P, KC, D], F32R)
        xp = sb("xp", [P, TILES, D + 1])
        at_rank = spare[:].rearrange("p k d -> p (k d)")[:, 0:F * (D + 1)].rearrange("p (f d) -> p f d", f=F)
        ps = [ctx.enter_context(nc.psum_tensor(f"g_ps{i}", [P, 512], F32)) for i in range(7)]
        ps_l, ps_r, ps_t = ps[0:3]
        ps_e = ps[3:7]
        dv, pe_s, ac = sem("dv"), sem("pe_s"), sem("ac")
        x_high, x_low, pe_e, copied = sem("x_high"), sem("x_low"), sem("pe_e"), sem("copied")
        w_high, w_low = sem("w_high"), sem("w_low")
        based, mixed, passed, outs = sem("based"), sem("mixed"), sem("passed"), sem("outs")
        x_low_late, stored = sem("x_low_late"), sem("stored")
        fetched = [sem(f"fetched{i}") for i in range(F)]
        block = ctx.enter_context(nc.Block())
        y_sb = big[:].rearrange("p k t -> p (k t)")
        xT_all = xnT_sb[:].rearrange("p n d -> p (n d)")

        def tile_of(s, n):
            return s[:, bass.ds(n * D, D)]

        @block.sync
        def _(sp):
            for n in range(TILES):
                sp.wait_ge(based, n + 2)
                sp.dma_start(xp_rows[n * P:(n + 1) * P, :], xp[:, n]).then_inc(stored, 16)
            sp.wait_ge(outs, 16 * TILES)

        @block.tensor
        def _(pe):
            mm, tr = nc.tensor.matmul, nc.tensor.transpose
            for n in range(TILES):
                last = tr(ps_l[:, n * NE:(n + 1) * NE], logitT[0:NE, n * P:(n + 1) * P], ident[0:NE, 0:NE])
            last.then_inc(pe_s, 1)
            h2 = hot[:].rearrange("p n e -> p (n e)")

            def expert(n, u, split, count):
                pe.wait_ge(split, count)
                wait(pe, copied, n - R + 1)
                for k in range(KC):
                    last = split_product(nc, ps_e[u][:], (xT_high[:, u, k], xT_low[:, u, k]),
                                         (we_high[:, k], we_low[:, k]), k == 0, k == KC - 1)
                last.then_inc(pe_e, 1)

            pe.wait_ge(w_low, KC)
            for n in range(EARLY):
                expert(n, n % R, x_low, n + 1)
                if n == R - 2:
                    pe.wait_ge(dv, 12)
                    mm(ps_t[:, 0:1], h2, ones[:, 0:1], start=True, stop=True).then_inc(pe_s, 1)
                    mm(ps_r[:, 0:P], before[:], h2, start=True, stop=False)
                elif n == R - 1:
                    pe.wait_ge(dv, 14)
                    mm(ps_r[:, 0:P], totals[:], later[:], start=False, stop=True).then_inc(pe_s, 1)
            with pe.Fori(EARLY // R, TILES // R) as m:
                for u in range(R):
                    expert(R * m + u, u, x_low_late, R * m + (u + 1 - EARLY))

        @block.scalar
        def _(act):
            act.wait_ge(ld, 80)

            def high(n, u):
                wait(act, pe_e, n - R + 1)
                nc.scalar.activation(xT_high[:, u].rearrange("p k q -> p (k q)"), tile_of(xT_all, n), ACT.Copy)\
                    .then_inc(x_high, 1)

            def copy(n, u):
                act.wait_ge(pe_e, n + 1)
                nc.scalar.activation(tile_of(y_sb, n), ps_e[u][:], ACT.Copy).then_inc(copied, 1)

            high(0, 0)
            for k in range(KC):
                nc.scalar.activation(we_high[:, k], we[:, k], ACT.Copy).then_inc(w_high, 1)
            for u in range(1, R):
                high(u, u)
            act.wait_ge(dv, 3)
            nc.scalar.activation(ex[:], lg[:], ACT.Exp).then_inc(ac, 1)
            with act.Fori(0, TILES // R - 1) as m:
                for u in range(R):
                    copy(R * m + u, u)
                    high(R * m + (R + u), u)
            for u in range(R):
                copy(TILES - R + u, u)

        @block.gpsimd
        def _(pool):
            def low(n):
                pool.wait_ge(x_high, n + 1)
                wait(pool, pe_e, n - R + 1)
                u = n % R
                nc.gpsimd.tensor_tensor(xT_low[:, u].rearrange("p k q -> p (k q)"), tile_of(xT_all, n),
                                        xT_high[:, u].rearrange("p k q -> p (k q)").bitcast(F32), ALU.subtract)\
                    .then_inc(x_low, 1)

            def fetch(n):
                wait(pool, mixed, n - F + 1)
                nc.gpsimd.indirect_dma_start(at_rank[:, n % F], None, xp_rows,
                                             bass.IndirectOffsetOnAxis(ap=rank_i[:, n:n + 1], axis=0))\
                    .then_inc(fetched[n % F], 16)

            def send(n):
                pool.wait_ge(mixed, n + 1)
                nc.gpsimd.indirect_dma_start(out, bass.IndirectOffsetOnAxis(ap=rank_i[:, n:n + 1], axis=0),
                                             tile_of(y_sb, n), None).then_inc(outs, 16)

            for n in range(EARLY):
                low(n)
            pool.wait_ge(dv, 16)
            pool.wait_ge(stored, 16 * TILES)
            for n in range(F):
                fetch(n)
            for n in range(TILES):
                if n + F < TILES:
                    fetch(n + F)
                send(n)

        @block.vector
        def _(dve):
            V = nc.vector
            done = [0]

            def step(ins):
                done[0] += 1
                ins.then_inc(dv, 1)
                dve.wait_ge(dv, done[0])

            wide = lambda a: a[:].rearrange("p (n one) -> p n one", one=1).broadcast_to([P, TILES, NE])
            step(V.memset(ones[:], 1.0))
            dve.wait_ge(ld, 80)
            for k in range(KC):
                dve.wait_ge(w_high, k + 1)
                V.tensor_tensor(we_low[:, k], we[:, k], we_high[:, k].bitcast(F32), ALU.subtract)\
                    .then_inc(w_low, 1)
            dve.wait_ge(pe_s, 1)
            lp = ps_l[:, 0:TILES * NE].rearrange("p (n e) -> p n e", e=NE)
            step(V.tensor_reduce(m1[:], lp, AX.X, ALU.max))
            step(V.tensor_tensor(lg[:], lp, wide(m1), ALU.subtract))
            dve.wait_ge(ac, 1)
            step(V.tensor_reduce(sm[:], ex[:], AX.X, ALU.add))
            step(V.reciprocal(ri[:], sm[:]))
            step(V.tensor_tensor(pr[:], ex[:], wide(ri), ALU.mult))
            step(V.tensor_reduce(best[:], pr[:], AX.X, ALU.max))
            step(V.tensor_tensor(far[:], pr[:], wide(best), ALU.is_lt))
            step(V.tensor_scalar(far[:], far[:], float(NE), None, ALU.mult))
            step(V.tensor_tensor(place[:], far[:], iota[:], ALU.add))
            step(V.tensor_reduce(first_[:], place[:], AX.X, ALU.min))
            step(V.tensor_tensor(hot[:], iota[:], wide(first_), ALU.is_equal))

            V.tensor_copy(xp[:, :, D:D + 1], best[:].rearrange("p (n one) -> p n one", one=1)).then_inc(based, 1)

            def base(n):
                V.scalar_tensor_tensor(out=xp[:, n, 0:D], in0=be[:], scalar=best[:, n:n + 1],
                                       in1=tile_of(x_sb, n), op0=ALU.mult, op1=ALU.add).then_inc(based, 1)

            for n in range(TILES // 2):
                base(n)
            dve.wait_ge(pe_s, 2)
            step(V.tensor_copy(total[:], ps_t[:, 0:1]))
            step(V.tensor_scalar(totals[:], ones[:], total[:, 0:1], None, ALU.mult))
            for n in range(TILES // 2, TILES):
                base(n)
            dve.wait_ge(pe_s, 3)
            step(V.tensor_tensor(ranks[:], hot[:], ps_r[:, 0:P].rearrange("p (n e) -> p n e", e=NE), ALU.mult))
            V.tensor_reduce(rank[:], ranks[:], AX.X, ALU.add).then_inc(passed, 1)
            dve.wait_ge(passed, 1)
            step(V.tensor_copy(rank_i[:], rank[:]))

            def low(n):
                dve.wait_ge(x_high, n + 1)
                dve.wait_ge(pe_e, n - R + 1)
                u = n % R
                V.tensor_tensor(xT_low[:, u].rearrange("p k q -> p (k q)"), tile_of(xT_all, n),
                                xT_high[:, u].rearrange("p k q -> p (k q)").bitcast(F32), ALU.subtract)\
                    .then_inc(x_low_late, 1)

            def mix(n):
                dve.wait_ge(fetched[n % F], 16 * (n // F + 1))
                dve.wait_ge(copied, n + 1)
                p = at_rank[:, n % F, D:D + 1]
                V.scalar_tensor_tensor(out=tile_of(y_sb, n), in0=tile_of(y_sb, n), scalar=p,
                                       in1=at_rank[:, n % F, 0:D], op0=ALU.mult, op1=ALU.add).then_inc(mixed, 1)

            low(EARLY)
            low(EARLY + 1)
            for n in range(TILES):
                mix(n)
                if EARLY + 2 + n < TILES:
                    low(EARLY + 2 + n)


def clear_semaphores(nc):
    used = set(nc.released_uncleared_semaphores)
    starts = [i for i in sorted(used) if i - 1 not in used]
    ends = [i + 1 for i in sorted(used) if i + 1 not in used]
    with nc.Block() as block:
        @block.gpsimd
        def _(pool):
            for start, end in zip(starts, ends):
                pool.sem_clear(range(start, end))


def layers(nc, t, out):
    with ExitStack() as ctx:
        def sb(name, shape, dt=F32):
            return ctx.enter_context(nc.sbuf_tensor(name, shape, dt))

        x_sb = sb("x_sb", [P, TILES * D])
        big = sb("big", [P, KC, TOK])
        ident = sb("ident", [P, P])

        def semaphore(name):
            return ctx.enter_context(nc.semaphore(name))

        row = lambda a: a.rearrange("(one d) -> one d", one=1).broadcast_to([P, D])
        t["kpad"] = nc.dram_tensor("kpad", (CH, P + D), F32).ap()
        padded = semaphore("padded")
        gathered = [semaphore(f"gathered{i}") for i in range(4)]
        toep_in = [semaphore("toep_in0"), semaphore("toep_in1")]
        cext_in = [semaphore("cext_in0"), semaphore("cext_in1")]
        gates_low, wv_in = semaphore("gates_low"), semaphore("d_wv_in")
        with ExitStack() as d_ctx:
            wv_d = d_ctx.enter_context(nc.sbuf_tensor("wv_d", [P, KC, D], F32))
            toep = wv_d[:, 0:2]
            cext = wv_d[:, 2:4].rearrange("p u d -> p (u d)")[:, 0:2 * KC * CEXT * B]\
                .rearrange("p (u k c) -> p u k c", u=2, k=KC)
            with ExitStack() as a_ctx:
                a_c = {"bq": t["bq"], "bk": row(t["bk"]), "bv": row(t["bv"]), "bo": row(t["bo"]),
                       "qcos": t["qcos"], "qsin": t["qsin"], "kcos": t["kcos"], "ksin": t["ksin"]}

                def first_heads(sp):
                    for h in range(2):
                        load_toep(sp, t, h, toep[:, h], toep_in[h])
                        load_cext(sp, t, h, cext[:, h], cext_in[h])
                wv = a_ctx.enter_context(nc.sbuf_tensor("a_wv", [P, KC, D], F32))
                attention(nc, True, x_sb, big, ident, a_c, t, wv, semaphore("a_wv_in"), None, padded, first_heads)
            alibi = d_ctx.enter_context(nc.sbuf_tensor("alibi", [P, H, 2 * P], F32))

            def projections(sp):
                sp.dma_start(wv_d[:], t["d_wv"]).then_inc(wv_in, 16)

            with ExitStack() as gate_ctx:
                gates = [gate_ctx.enter_context(nc.sbuf_tensor(n, [P, KC, NC], dt))
                         for n, dt in (("wg", F32), ("wg_high", F32R), ("wg_low", F32R))]
                convolution(nc, big, t, toep, cext, toep_in, cext_in, gates, gates_low)
                router(nc, x_sb, big, ident, t, alibi, gathered, gates, gates_low, projections)
            clear_semaphores(nc)
            attention(nc, False, x_sb, big, ident, None, t, wv_d, wv_in, alibi, None, None)
        xp_rows = nc.dram_tensor("xp_rows", (TOK, D + 1), F32).ap()
        mix_in, expert_in = semaphore("mix_in"), semaphore("expert_in")
        logitT = ctx.enter_context(nc.sbuf_tensor("logitT", [P, TOK], F32))
        o_sb = ctx.enter_context(nc.sbuf_tensor("o_sb", [P, TILES, D], F32))
        mix = [ctx.enter_context(nc.sbuf_tensor(n, shape, F32)) for n, shape in (
            ("wgate", [P, KC, D]), ("wout", [P, KC, D]), ("gamma", [P, D]), ("beta", [P, D]),
            ("wr", [P, KC, NE]), ("br", [P, 1]))]

        def mixing_weights(sp):
            wgate, wout, gamma, beta, wr, br = mix
            for dst, src in ((wgate[:], t["wgate"]), (wout[:], t["wout"]), (gamma[:], row(t["gn_gamma"])),
                             (beta[:], row(t["gn_beta"])), (wr[:], t["wr"]), (br[0:NE], t["br"])):
                sp.dma_start(dst, src).then_inc(mix_in, 16)
        retention(nc, big, t, o_sb, mixing_weights)
        route = [ctx.enter_context(nc.sbuf_tensor(n, shape, F32)) for n, shape in (
            ("before", [P, P]), ("later", [P, P]), ("iota", [P, TILES, NE]),
            ("we", [P, KC, D]), ("be", [P, D]))]

        def expert_weights(sp):
            before, later, iota, we, be = route
            for dst, src in ((before[:], t["before"]), (later[:], t["later"]), (iota[:], t["iota"]),
                             (we[:], t["we"]), (be[:], row(t["be"]))):
                sp.dma_start(dst, src).then_inc(expert_in, 16)
        mixing(nc, x_sb, big, ident, o_sb, mix, mix_in, logitT, expert_weights)
        experts(nc, x_sb, big, o_sb, ident, route, expert_in, logitT, mix[0], xp_rows, out)


def laid_out(inputs):
    f = lambda n: np.asarray(inputs[n])
    chunks = lambda w: np.ascontiguousarray(w.reshape(KC, P, -1).transpose(1, 0, 2))
    halves = np.concatenate([np.arange(0, HD, 2), np.arange(1, HD, 2)])
    paired = (np.arange(H)[:, None] * HD + halves[None]).reshape(-1)
    a = {"x": f("x").reshape(TOK, D),
         "a_wq": chunks(f("L0_attn_Wq")[paired].T), "a_wk": chunks(f("L0_attn_Wk")[paired].T),
         "a_wv": chunks(f("L0_attn_Wv").T), "a_wo": chunks(f("L0_attn_Wo").T),
         "bq": np.ascontiguousarray(f("L0_attn_bq")[paired].reshape(G, P).T),
         "bk": np.ascontiguousarray(f("L0_attn_bk")[paired]), "bv": f("L0_attn_bv"), "bo": f("L0_attn_bo")}
    for n in "qkvo":
        a["d_w" + n] = chunks(f("L1_attn_W" + n).T)
    ctx = f("ctx_2048")
    rev = ctx.reshape(B, CH, CD, KC, P)[:, :, :, :, ::-1][:, :, np.arange(CEXT) % CD]
    a["ctx_rev"] = np.ascontiguousarray(rev.transpose(1, 4, 3, 2, 0).reshape(CH, P, KC, CEXT * B))
    a["conv_k"], a["conv_d"] = f("L0_xattn_ssm_kernel"), f("L0_xattn_D").reshape(CH, 1)
    a["gate_w"], a["gate_b"] = chunks(f("L0_ffn_gate_w").T), f("L0_ffn_gate_b")
    a["pool"] = np.ascontiguousarray(f("L0_ffn_vector_pool")[:, 16])
    a["wh"] = np.ascontiguousarray(f("L1_xattn_Wh").transpose(1, 0, 2))
    a["ctxT"] = np.ascontiguousarray(ctx.reshape(TOK, RH, RD).transpose(1, 2, 0))
    a["wgate"], a["wout"] = chunks(f("L1_xattn_wg_w")), chunks(f("L1_xattn_wo_w"))
    a["gn_gamma"] = f("L1_xattn_gn_gamma")
    a["gn_beta"] = f("L1_xattn_gn_beta")
    a["wr"], a["br"] = chunks(f("L1_ffn_Wg")), f("L1_ffn_bg").reshape(NE, 1)
    a["we"], a["be"] = chunks(f("L1_ffn_We")), f("L1_ffn_be")
    a.update(shape_constants())
    return a


def shape_constants():
    f32 = np.float32
    theta = f32(1.0) / f32(10000.0) ** (np.arange(0, HD, 2, dtype=f32) / f32(HD))
    angle = np.arange(S, dtype=f32)[:, None] * theta[None]
    cos, sin = np.cos(angle).astype(f32), np.sin(angle).astype(f32)
    cos2, sin2 = np.concatenate([cos, cos], 1), np.concatenate([-sin, sin], 1)
    scale = f32(HD ** -0.5)
    kept = np.concatenate([np.arange(START), np.arange(S - RECENT, S)])
    c = {"qcos": np.tile(cos2.T * scale, (4, 1)), "qsin": np.tile(sin2.T * scale, (4, 1)),
         "kcos": cos2[kept], "ksin": sin2[kept], "identity": np.eye(P, dtype=f32)}
    k, q = np.arange(S)[None, :], np.arange(S)[:, None]
    rel = np.where(k <= q, k - q, -1e30)
    c["rel"] = rel[P:S]
    slope = f32(0.5) ** (np.arange(1, H + 1, dtype=f32) * f32(8.0) / f32(H))
    c["slope"] = np.tile(slope[None], (P, 1))
    gam = f32(1.0) - f32(2.0) ** (f32(-5.0) - np.arange(RH, dtype=f32))
    expo = (k - q).astype(f32)
    dm = np.where(expo[None] <= 0, gam[:, None, None] ** expo[None], f32(0))
    dm = dm / np.sqrt(dm.sum(-1, dtype=f32))[:, None, :] / np.sqrt(f32(RD))
    c["decay"] = dm.transpose(0, 2, 1).reshape(RH, TB, P, S).transpose(0, 2, 1, 3)
    i = np.arange(P)
    c["before"] = (i[:, None] < i[None]).astype(f32)
    ne = (i % NE) * TILES + i // NE
    c["later"] = (ne[:, None] < ne[None]).astype(f32)
    c["iota"] = np.broadcast_to(np.arange(NE, dtype=f32), (P, TILES, NE))
    return {k: np.ascontiguousarray(a.astype(f32)) for k, a in c.items()}


def kernel(**inputs):
    import concourse.bacc as _bacc
    from concourse.bass_utils import run_bass_kernel_spmd as _run

    nc = _bacc.Bacc("TRN2", target_bir_lowering=False, num_devices=1)
    arrays, t = {}, {}
    for name, a in laid_out(inputs).items():
        arrays[name + "_dram"] = a
        t[name] = nc.dram_tensor(name + "_dram", a.shape, mybir.dt.from_np(a.dtype), kind="ExternalInput").ap()
    out = nc.dram_tensor("out_dram", (TOK, D), F32, kind="ExternalOutput").ap()
    layers(nc, t, out)
    r = _run(nc, [arrays], core_ids=[0])
    return r.results[0]["out_dram"].reshape(B, S, D)
```
